# Optimizing a Trainium2 kernel written in Bass

```python
import numpy as np
import jax
import jax.numpy as jnp

def _softmax(x, axis=-1):
    return jax.nn.softmax(x, axis=axis)

def _gelu(x):
    return jax.nn.gelu(x, approximate=True)

def _silu(x):
    return jax.nn.silu(x)

def _sigmoid(x):
    return jax.nn.sigmoid(x)

def _layernorm(x, axis=-1, eps=1e-05):
    m = jnp.mean(x, axis=axis, keepdims=True)
    v = jnp.var(x, axis=axis, keepdims=True)
    return (x - m) / jnp.sqrt(v + eps)

def _scatter_add(tgt, idx, src, axis=0):
    return tgt.at[idx].add(src)

def _segment_sum(src, seg, n):
    return jax.ops.segment_sum(src, seg, n)
kernel_name = 'mk_adaln_ffn_d1_seqx_r8_1971d6'

def setup_inputs(seed: int=0):
    np.random.seed(seed)
    _w = jnp.asarray

    def _rec_inputs():
        import jax
        import jax.numpy as jnp
        _rk = jax.random.key(seed)
        x = -0.0002928 + 1 * jax.random.normal(jax.random.fold_in(_rk, 1), (32, 128, 128), jnp.float32)
        _lenS = 128 - jax.random.randint(jax.random.fold_in(_rk, 7), (32,), 0, max(1, 128 // 4) + 1, jnp.int32)
        _lenS2 = 128 - jax.random.randint(jax.random.fold_in(_rk, 8), (32,), 0, max(1, 128 // 4) + 1, jnp.int32)
        fside_BxS_0 = 0.0061147 + 1.02565 * jax.random.normal(jax.random.fold_in(_rk, 12), (32, 128), jnp.float32)
        itok_BxSxS_0_4 = jax.random.randint(jax.random.fold_in(_rk, 13), (32, 128, 128), 0, 5, jnp.int32)
        fside_BxSxS_0 = -3.24666e-05 + 0.0312493 * jax.random.normal(jax.random.fold_in(_rk, 14), (32, 128, 128), jnp.float32)
        cond_2048 = -4.62462e-05 + 0.0441849 * jax.random.normal(jax.random.fold_in(_rk, 16), (32, 256), jnp.float32)
        _validS = jnp.arange(128)[None, :] < _lenS[:, None]
        _validS2 = jnp.arange(128)[None, :] < _lenS2[:, None]
        _causal = jnp.tril(jnp.ones((128, 128), dtype=bool))
        mask_BxS_ff1 = jnp.where(jnp.ones((32, 128), dtype=bool), 1.0, 0.0).astype(jnp.float32)
        mask_BxS_ff0 = jnp.where(jnp.ones((32, 128), dtype=bool), 0.0, -1000000000.0).astype(jnp.float32)
        return (x, fside_BxS_0, itok_BxSxS_0_4, fside_BxSxS_0, cond_2048, mask_BxS_ff1, mask_BxS_ff0)
    x, fside_BxS_0, itok_BxSxS_0_4, fside_BxSxS_0, cond_2048, mask_BxS_ff1, mask_BxS_ff0 = _rec_inputs()

    def _L0_cond_setup():
        import jax, jax.numpy as jnp
        import numpy as np
        B, N, D = (4, 128, 128)
        T_ITER = 4
        E_TYPES = 4
        ALPHA = 0.2

        def _lin_w(key, out_f, in_f):
            bound = float(np.sqrt(3.0 / ((in_f + out_f) / 2.0)))
            return jax.random.uniform(key, (out_f, in_f), minval=-bound, maxval=bound, dtype=jnp.float32)

        def _lin(x, w, b):
            return x @ w.T + b

        def _qdgat_forward(ents, ent_mask, q_encoding, adj, types, init_mem, w_qin, b_qin, w_qt, b_qt, w_pl, b_pl, w_pc, b_pc, w_q, b_q, w_k, b_k, w_v, b_v, w_pk, b_pk, w_pv, b_pv, wes, w_mu, b_mu, w_cb, b_cb):
            d = ents.shape[-1]
            x_loc = ents
            x_ctx = jnp.broadcast_to(init_mem, ents.shape)
            var_drop = ent_mask[:, :, None]
            adj_pos = adj > 0
            q_base = jax.nn.elu(_lin(q_encoding, w_qin, b_qin))
            n_types = wes.shape[0] + 1
            for t in range(T_ITER):
                cmd = _lin(q_base, w_qt[t], b_qt[t])
                xc = x_ctx * var_drop
                pl = _lin(x_loc, w_pl, b_pl)
                pc = _lin(xc, w_pc, b_pc)
                x_joint = jnp.concatenate([x_loc, xc, pl * pc], axis=-1)
                q = _lin(x_joint, w_q, b_q)
                k = _lin(x_joint, w_k, b_k) * _lin(cmd, w_pk, b_pk)[:, None, :]
                v = _lin(x_joint, w_v, b_v) * _lin(cmd, w_pv, b_pv)[:, None, :]
                edge_score = jnp.zeros(adj.shape, jnp.float32)
                for i in range(n_types):
                    if types >> i & 1 == 1:
                        w1, w2 = (wes[i - 1, :d], wes[i - 1, d:])
                        s = (q @ w1)[:, :, None] + (k @ w2)[:, None, :]
                        edge_score = edge_score + jnp.where(adj == i, s, 0.0)
                e = jnp.where(edge_score > 0, edge_score, ALPHA * edge_score)
                logits = jnp.where(adj_pos, e, jnp.float32(-9000000000000000.0))
                prob = jax.nn.softmax(logits, axis=-1)
                message = jnp.einsum('bij,bjd->bid', prob, v)
                x_ctx = _lin(jnp.concatenate([xc, message], axis=-1), w_mu, b_mu)
            return _lin(jnp.concatenate([x_loc, x_ctx], axis=-1), w_cb, b_cb)
        key = jax.random.key(seed)
        ks = jax.random.split(key, 32)
        inp = {}
        inp['ents'] = jax.random.normal(ks[0], (B, N, D), jnp.float32)
        inp['ent_mask'] = jnp.ones((B, N), jnp.float32)
        inp['q_encoding'] = jax.random.normal(ks[1], (B, D), jnp.float32)
        inp['adj'] = jax.random.randint(ks[2], (B, N, N), 0, E_TYPES + 1, dtype=jnp.int32)
        inp['types'] = 30
        inp['init_mem'] = jax.random.normal(ks[3], (1, D), jnp.float32)
        inp['w_qin'] = _lin_w(ks[4], D, D)
        inp['b_qin'] = jnp.zeros((D,), jnp.float32)
        inp['w_qt'] = jnp.stack([_lin_w(ks[5 + t], D, D) for t in range(T_ITER)])
        inp['b_qt'] = jnp.zeros((T_ITER, D), jnp.float32)
        inp['w_pl'] = _lin_w(ks[9], D, D)
        inp['b_pl'] = jnp.zeros((D,), jnp.float32)
        inp['w_pc'] = _lin_w(ks[10], D, D)
        inp['b_pc'] = jnp.zeros((D,), jnp.float32)
        inp['w_q'] = _lin_w(ks[11], D, 3 * D)
        inp['b_q'] = jnp.zeros((D,), jnp.float32)
        inp['w_k'] = _lin_w(ks[12], D, 3 * D)
        inp['b_k'] = jnp.zeros((D,), jnp.float32)
        inp['w_v'] = _lin_w(ks[13], D, 3 * D)
        inp['b_v'] = jnp.zeros((D,), jnp.float32)
        inp['w_pk'] = _lin_w(ks[14], D, D)
        inp['b_pk'] = jnp.zeros((D,), jnp.float32)
        inp['w_pv'] = _lin_w(ks[15], D, D)
        inp['b_pv'] = jnp.zeros((D,), jnp.float32)
        wb = 1.414 * float(np.sqrt(6.0 / (2 * D + 1)))
        inp['wes'] = jax.random.uniform(ks[16], (E_TYPES, 2 * D), minval=-wb, maxval=wb, dtype=jnp.float32)
        inp['w_mu'] = _lin_w(ks[17], D, 2 * D)
        inp['b_mu'] = jnp.zeros((D,), jnp.float32)
        inp['w_cb'] = _lin_w(ks[18], D, 2 * D)
        inp['b_cb'] = jnp.zeros((D,), jnp.float32)
        return inp
    _L0_cond_all = _L0_cond_setup()
    _L0_cond_in = {k: v for k, v in _L0_cond_all.items() if k in ('init_mem', 'w_qin', 'b_qin', 'w_pl', 'b_pl', 'w_pc', 'b_pc', 'w_q', 'b_q', 'w_k', 'b_k', 'w_v', 'b_v', 'w_pk', 'b_pk', 'w_pv', 'b_pv', 'w_mu', 'b_mu', 'w_cb', 'b_cb')}
    del _L0_cond_all

    def _L0_ffn_setup():
        import jax, jax.numpy as jnp
        import numpy as np
        NHEAD = 16
        NUM_GROUPS = 4
        EXPERTS_PER_GROUP = 2
        LN_EPS = 1e-05

        def _layernorm(x, g, b):
            mu = jnp.mean(x, axis=-1, keepdims=True)
            var = jnp.mean(jnp.square(x - mu), axis=-1, keepdims=True)
            return (x - mu) * jax.lax.rsqrt(var + LN_EPS) * g + b

        def _mha(x, wi, bi, wo, bo):
            B, S, D = x.shape
            hd = D // NHEAD
            qkv = x @ wi.T + bi
            q, k, v = jnp.split(qkv, 3, axis=-1)

            def heads(t):
                return t.reshape(B, S, NHEAD, hd).transpose(0, 2, 1, 3)
            q, k, v = (heads(q), heads(k), heads(v))
            scores = jnp.einsum('bhqd,bhkd->bhqk', q, k) / jnp.sqrt(jnp.asarray(hd, x.dtype))
            attn = jax.nn.softmax(scores, axis=-1)
            o = jnp.einsum('bhqk,bhkd->bhqd', attn, v)
            o = o.transpose(0, 2, 1, 3).reshape(B, S, D)
            return o @ wo.T + bo

        def _hier_moe(x, w_group, b_group, w_expert, b_expert, w1, b1, w2, b2):
            B, S, D = x.shape
            xt = x.reshape(B * S, D)
            T = xt.shape[0]
            E = NUM_GROUPS * EXPERTS_PER_GROUP
            gp = jax.nn.softmax(xt @ w_group + b_group, axis=-1)
            g_idx = jnp.argmax(gp, axis=-1)
            g_prob = jnp.max(gp, axis=-1)
            elog = jnp.einsum('td,gde->tge', xt, w_expert) + b_expert
            ep = jax.nn.softmax(elog, axis=-1)
            ep_sel = jnp.take_along_axis(ep, g_idx[:, None, None], axis=1)[:, 0, :]
            e_idx_local = jnp.argmax(ep_sel, axis=-1)
            e_prob = jnp.max(ep_sel, axis=-1)
            flat_e = g_idx * EXPERTS_PER_GROUP + e_idx_local
            combine = jax.nn.one_hot(flat_e, E, dtype=xt.dtype) * (g_prob * e_prob)[:, None]
            h = jax.nn.relu(jnp.einsum('td,edf->etf', xt, w1) + b1[:, None, :])
            y = jnp.einsum('etf,efd->etd', h, w2) + b2[:, None, :]
            out = jnp.einsum('te,etd->td', combine, y)
            return out.reshape(B, S, D)
        key = jax.random.key(seed)
        ks = jax.random.split(key, 8)
        B, S, D, F = (2, 128, 128, 256)
        G, Epg = (NUM_GROUPS, EXPERTS_PER_GROUP)
        E = G * Epg
        sc = lambda fan: 1.0 / np.sqrt(fan)
        return {'x': jax.random.normal(ks[0], (B, S, D), jnp.float32), 'in_proj_w': jax.random.normal(ks[1], (3 * D, D), jnp.float32) * sc(D), 'in_proj_b': jnp.zeros((3 * D,), jnp.float32), 'out_proj_w': jax.random.normal(ks[2], (D, D), jnp.float32) * sc(D), 'out_proj_b': jnp.zeros((D,), jnp.float32), 'ln1_g': jnp.ones((D,), jnp.float32), 'ln1_b': jnp.zeros((D,), jnp.float32), 'ln2_g': jnp.ones((D,), jnp.float32), 'ln2_b': jnp.zeros((D,), jnp.float32), 'w_group': jax.random.normal(ks[3], (D, G), jnp.float32) * sc(D), 'b_group': jnp.zeros((G,), jnp.float32), 'w_expert': jax.random.normal(ks[4], (G, D, Epg), jnp.float32) * sc(D), 'b_expert': jnp.zeros((G, Epg), jnp.float32), 'w1': jax.random.normal(ks[5], (E, D, F), jnp.float32) * sc(D), 'b1': jnp.zeros((E, F), jnp.float32), 'w2': jax.random.normal(ks[6], (E, F, D), jnp.float32) * sc(F), 'b2': jnp.zeros((E, D), jnp.float32)}
    _L0_ffn_all = _L0_ffn_setup()
    _L0_ffn_in = {k: v for k, v in _L0_ffn_all.items() if k in ('in_proj_w', 'in_proj_b', 'out_proj_w', 'out_proj_b', 'ln1_g', 'ln1_b', 'ln2_g', 'ln2_b', 'w_group', 'b_group', 'w_expert', 'b_expert', 'w1', 'b1', 'w2', 'b2')}
    del _L0_ffn_all
    return {'x': x, 'fside_BxS_0': fside_BxS_0, 'itok_BxSxS_0_4': itok_BxSxS_0_4, 'fside_BxSxS_0': fside_BxSxS_0, 'cond_2048': cond_2048, 'mask_BxS_ff1': mask_BxS_ff1, 'mask_BxS_ff0': mask_BxS_ff0, 'L0_cond_init_mem': _L0_cond_in['init_mem'], 'L0_cond_w_qin': _L0_cond_in['w_qin'], 'L0_cond_b_qin': _L0_cond_in['b_qin'], 'L0_cond_w_pl': _L0_cond_in['w_pl'], 'L0_cond_b_pl': _L0_cond_in['b_pl'], 'L0_cond_w_pc': _L0_cond_in['w_pc'], 'L0_cond_b_pc': _L0_cond_in['b_pc'], 'L0_cond_w_q': _L0_cond_in['w_q'], 'L0_cond_b_q': _L0_cond_in['b_q'], 'L0_cond_w_k': _L0_cond_in['w_k'], 'L0_cond_b_k': _L0_cond_in['b_k'], 'L0_cond_w_v': _L0_cond_in['w_v'], 'L0_cond_b_v': _L0_cond_in['b_v'], 'L0_cond_w_pk': _L0_cond_in['w_pk'], 'L0_cond_b_pk': _L0_cond_in['b_pk'], 'L0_cond_w_pv': _L0_cond_in['w_pv'], 'L0_cond_b_pv': _L0_cond_in['b_pv'], 'L0_cond_w_mu': _L0_cond_in['w_mu'], 'L0_cond_b_mu': _L0_cond_in['b_mu'], 'L0_cond_w_cb': _L0_cond_in['w_cb'], 'L0_cond_b_cb': _L0_cond_in['b_cb'], 'L0_ffn_in_proj_w': _L0_ffn_in['in_proj_w'], 'L0_ffn_in_proj_b': _L0_ffn_in['in_proj_b'], 'L0_ffn_out_proj_w': _L0_ffn_in['out_proj_w'], 'L0_ffn_out_proj_b': _L0_ffn_in['out_proj_b'], 'L0_ffn_ln1_g': _L0_ffn_in['ln1_g'], 'L0_ffn_ln1_b': _L0_ffn_in['ln1_b'], 'L0_ffn_ln2_g': _L0_ffn_in['ln2_g'], 'L0_ffn_ln2_b': _L0_ffn_in['ln2_b'], 'L0_ffn_w_group': _L0_ffn_in['w_group'], 'L0_ffn_b_group': _L0_ffn_in['b_group'], 'L0_ffn_w_expert': _L0_ffn_in['w_expert'], 'L0_ffn_b_expert': _L0_ffn_in['b_expert'], 'L0_ffn_w1': _L0_ffn_in['w1'], 'L0_ffn_b1': _L0_ffn_in['b1'], 'L0_ffn_w2': _L0_ffn_in['w2'], 'L0_ffn_b2': _L0_ffn_in['b2']}

def reference(x, fside_BxS_0, itok_BxSxS_0_4, fside_BxSxS_0, cond_2048, mask_BxS_ff1, mask_BxS_ff0, L0_cond_init_mem, L0_cond_w_qin, L0_cond_b_qin, L0_cond_w_pl, L0_cond_b_pl, L0_cond_w_pc, L0_cond_b_pc, L0_cond_w_q, L0_cond_b_q, L0_cond_w_k, L0_cond_b_k, L0_cond_w_v, L0_cond_b_v, L0_cond_w_pk, L0_cond_b_pk, L0_cond_w_pv, L0_cond_b_pv, L0_cond_w_mu, L0_cond_b_mu, L0_cond_w_cb, L0_cond_b_cb, L0_ffn_in_proj_w, L0_ffn_in_proj_b, L0_ffn_out_proj_w, L0_ffn_out_proj_b, L0_ffn_ln1_g, L0_ffn_ln1_b, L0_ffn_ln2_g, L0_ffn_ln2_b, L0_ffn_w_group, L0_ffn_b_group, L0_ffn_w_expert, L0_ffn_b_expert, L0_ffn_w1, L0_ffn_b1, L0_ffn_w2, L0_ffn_b2):
    import jax
    import jax.numpy as jnp

    def _L0_cond_ref(ents, ent_mask, q_encoding, adj, types, init_mem, w_qin, b_qin, w_qt, b_qt, w_pl, b_pl, w_pc, b_pc, w_q, b_q, w_k, b_k, w_v, b_v, w_pk, b_pk, w_pv, b_pv, wes, w_mu, b_mu, w_cb, b_cb):
        import jax, jax.numpy as jnp
        import numpy as np
        B, N, D = (4, 128, 128)
        T_ITER = 4
        E_TYPES = 4
        ALPHA = 0.2

        def _lin_w(key, out_f, in_f):
            bound = float(np.sqrt(3.0 / ((in_f + out_f) / 2.0)))
            return jax.random.uniform(key, (out_f, in_f), minval=-bound, maxval=bound, dtype=jnp.float32)

        def _lin(x, w, b):
            return x @ w.T + b

        def _qdgat_forward(ents, ent_mask, q_encoding, adj, types, init_mem, w_qin, b_qin, w_qt, b_qt, w_pl, b_pl, w_pc, b_pc, w_q, b_q, w_k, b_k, w_v, b_v, w_pk, b_pk, w_pv, b_pv, wes, w_mu, b_mu, w_cb, b_cb):
            d = ents.shape[-1]
            x_loc = ents
            x_ctx = jnp.broadcast_to(init_mem, ents.shape)
            var_drop = ent_mask[:, :, None]
            adj_pos = adj > 0
            q_base = jax.nn.elu(_lin(q_encoding, w_qin, b_qin))
            n_types = wes.shape[0] + 1
            for t in range(T_ITER):
                cmd = _lin(q_base, w_qt[t], b_qt[t])
                xc = x_ctx * var_drop
                pl = _lin(x_loc, w_pl, b_pl)
                pc = _lin(xc, w_pc, b_pc)
                x_joint = jnp.concatenate([x_loc, xc, pl * pc], axis=-1)
                q = _lin(x_joint, w_q, b_q)
                k = _lin(x_joint, w_k, b_k) * _lin(cmd, w_pk, b_pk)[:, None, :]
                v = _lin(x_joint, w_v, b_v) * _lin(cmd, w_pv, b_pv)[:, None, :]
                edge_score = jnp.zeros(adj.shape, jnp.float32)
                for i in range(n_types):
                    if types >> i & 1 == 1:
                        w1, w2 = (wes[i - 1, :d], wes[i - 1, d:])
                        s = (q @ w1)[:, :, None] + (k @ w2)[:, None, :]
                        edge_score = edge_score + jnp.where(adj == i, s, 0.0)
                e = jnp.where(edge_score > 0, edge_score, ALPHA * edge_score)
                logits = jnp.where(adj_pos, e, jnp.float32(-9000000000000000.0))
                prob = jax.nn.softmax(logits, axis=-1)
                message = jnp.einsum('bij,bjd->bid', prob, v)
                x_ctx = _lin(jnp.concatenate([xc, message], axis=-1), w_mu, b_mu)
            return _lin(jnp.concatenate([x_loc, x_ctx], axis=-1), w_cb, b_cb)
        return _qdgat_forward(ents, ent_mask, q_encoding, adj, types, init_mem, w_qin, b_qin, w_qt, b_qt, w_pl, b_pl, w_pc, b_pc, w_q, b_q, w_k, b_k, w_v, b_v, w_pk, b_pk, w_pv, b_pv, wes, w_mu, b_mu, w_cb, b_cb)

    def _L0_ffn_ref(x, in_proj_w, in_proj_b, out_proj_w, out_proj_b, ln1_g, ln1_b, ln2_g, ln2_b, w_group, b_group, w_expert, b_expert, w1, b1, w2, b2):
        import jax, jax.numpy as jnp
        import numpy as np
        NHEAD = 16
        NUM_GROUPS = 4
        EXPERTS_PER_GROUP = 2
        LN_EPS = 1e-05

        def _layernorm(x, g, b):
            mu = jnp.mean(x, axis=-1, keepdims=True)
            var = jnp.mean(jnp.square(x - mu), axis=-1, keepdims=True)
            return (x - mu) * jax.lax.rsqrt(var + LN_EPS) * g + b

        def _mha(x, wi, bi, wo, bo):
            B, S, D = x.shape
            hd = D // NHEAD
            qkv = x @ wi.T + bi
            q, k, v = jnp.split(qkv, 3, axis=-1)

            def heads(t):
                return t.reshape(B, S, NHEAD, hd).transpose(0, 2, 1, 3)
            q, k, v = (heads(q), heads(k), heads(v))
            scores = jnp.einsum('bhqd,bhkd->bhqk', q, k) / jnp.sqrt(jnp.asarray(hd, x.dtype))
            attn = jax.nn.softmax(scores, axis=-1)
            o = jnp.einsum('bhqk,bhkd->bhqd', attn, v)
            o = o.transpose(0, 2, 1, 3).reshape(B, S, D)
            return o @ wo.T + bo

        def _hier_moe(x, w_group, b_group, w_expert, b_expert, w1, b1, w2, b2):
            B, S, D = x.shape
            xt = x.reshape(B * S, D)
            T = xt.shape[0]
            E = NUM_GROUPS * EXPERTS_PER_GROUP
            gp = jax.nn.softmax(xt @ w_group + b_group, axis=-1)
            g_idx = jnp.argmax(gp, axis=-1)
            g_prob = jnp.max(gp, axis=-1)
            elog = jnp.einsum('td,gde->tge', xt, w_expert) + b_expert
            ep = jax.nn.softmax(elog, axis=-1)
            ep_sel = jnp.take_along_axis(ep, g_idx[:, None, None], axis=1)[:, 0, :]
            e_idx_local = jnp.argmax(ep_sel, axis=-1)
            e_prob = jnp.max(ep_sel, axis=-1)
            flat_e = g_idx * EXPERTS_PER_GROUP + e_idx_local
            combine = jax.nn.one_hot(flat_e, E, dtype=xt.dtype) * (g_prob * e_prob)[:, None]
            h = jax.nn.relu(jnp.einsum('td,edf->etf', xt, w1) + b1[:, None, :])
            y = jnp.einsum('etf,efd->etd', h, w2) + b2[:, None, :]
            out = jnp.einsum('te,etd->td', combine, y)
            return out.reshape(B, S, D)
        attn_out = _mha(x, in_proj_w, in_proj_b, out_proj_w, out_proj_b)
        x = _layernorm(x + attn_out, ln1_g, ln1_b)
        moe_out = _hier_moe(x, w_group, b_group, w_expert, b_expert, w1, b1, w2, b2)
        x = _layernorm(x + moe_out, ln2_g, ln2_b)
        return x
    x = x + _L0_ffn_ref(_L0_cond_ref(x, mask_BxS_ff1, fside_BxS_0, itok_BxSxS_0_4, 30, L0_cond_init_mem, L0_cond_w_qin, L0_cond_b_qin, fside_BxSxS_0, mask_BxS_ff0, L0_cond_w_pl, L0_cond_b_pl, L0_cond_w_pc, L0_cond_b_pc, L0_cond_w_q, L0_cond_b_q, L0_cond_w_k, L0_cond_b_k, L0_cond_w_v, L0_cond_b_v, L0_cond_w_pk, L0_cond_b_pk, L0_cond_w_pv, L0_cond_b_pv, cond_2048, L0_cond_w_mu, L0_cond_b_mu, L0_cond_w_cb, L0_cond_b_cb), L0_ffn_in_proj_w, L0_ffn_in_proj_b, L0_ffn_out_proj_w, L0_ffn_out_proj_b, L0_ffn_ln1_g, L0_ffn_ln1_b, L0_ffn_ln2_g, L0_ffn_ln2_b, L0_ffn_w_group, L0_ffn_b_group, L0_ffn_w_expert, L0_ffn_b_expert, L0_ffn_w1, L0_ffn_b1, L0_ffn_w2, L0_ffn_b2)
    return x

_drawn_inputs = setup_inputs


def setup_inputs(seed=0):
    import zlib

    import numpy as np

    out = dict(_drawn_inputs(seed))
    spreads = {'L0_cond_b_qin': (0.0, 0.1),
     'L0_cond_b_pl': (0.0, 0.1),
     'L0_cond_b_pc': (0.0, 0.8),
     'L0_cond_b_q': (0.0, 0.8),
     'L0_cond_b_k': (0.0, 0.8),
     'L0_cond_b_v': (0.0, 0.1),
     'L0_cond_b_pk': (0.0, 0.8),
     'L0_cond_b_pv': (0.0, 0.1),
     'L0_cond_b_mu': (0.0, 0.1),
     'L0_cond_b_cb': (0.0, 0.1),
     'L0_ffn_in_proj_b': (0.0, 0.1),
     'L0_ffn_out_proj_b': (0.0, 0.1),
     'L0_ffn_ln1_g': (1.0, 0.2),
     'L0_ffn_ln1_b': (0.0, 0.1),
     'L0_ffn_ln2_g': (1.0, 0.2),
     'L0_ffn_ln2_b': (0.0, 0.1),
     'L0_ffn_b_group': (0.0, 0.1),
     'L0_ffn_b_expert': (0.0, 0.464),
     'L0_ffn_b1': (0.0, 0.439),
     'L0_ffn_b2': (0.0, 0.322)}
    factors = {'L0_cond_w_k': 3.512, 'L0_cond_w_pk': 3.19}
    for name, (base, spread) in spreads.items():
        noise = np.random.default_rng([zlib.crc32(name.encode()), seed]).standard_normal(out[name].shape)
        drawn = base * np.exp(spread * noise) if base else spread * noise
        out[name] = jnp.asarray(drawn.astype(out[name].dtype))
    for name, factor in factors.items():
        out[name] = (out[name] * factor).astype(out[name].dtype)
    return out
```

```python
from contextlib import ExitStack

import numpy as np
import concourse.bass as bass
from concourse import mybir

F32 = mybir.dt.float32
BF16 = mybir.dt.bfloat16
I32 = mybir.dt.int32
ALU = mybir.AluOpType
ACT = mybir.ActivationFunctionType
AX_X = mybir.AxisListType.X

B, N, D = 32, 128, 128
TOK = B * N
GB = 4
G = B // GB
GT = GB * N
T_ITER = 4
TYPES = 4
ALPHA = 0.2
BIG = float(2.0 ** 53)
NPART = 3
QK = 2 * TYPES

WCOLS = {}


def _columns():
    at = 0
    for name, n in (("qin", D), ("pk", D), ("pv", D), ("qt", T_ITER * D), ("wq", 3 * D), ("wk", 3 * D),
                    ("fside", B), ("w1t", TYPES), ("w2t", TYPES), ("pl", D), ("pc", D), ("v", 3 * D),
                    ("mu", 2 * D), ("cb", 2 * D), ("wi", 3 * D), ("wo", D), ("gate", D),
                    ("bias", 24)):
        WCOLS[name] = (at, at + n)
        at += n
    return at


NW = _columns()
BIAS = {n: i for i, n in enumerate(("qin", "pl", "pc", "q", "k", "mu", "cb", "pk", "pv", "qt0", "qt1", "qt2",
                                    "qt3", "init", "iq", "ik", "ln1g", "ln1b"))}
RCOLS = {"bv": (0, 128), "iv": (128, 256), "bo": (256, 384), "ln1g": (384, 512), "ln1b": (512, 640),
         "ln2g": (640, 768), "ln2b": (768, 896), "gate": (896, 908)}
NR = 908
HEADS = 16
HD = D // HEADS
VW = HD + 1
VROW = 264
EXPERTS, FF = 8, 256
GROUPS_E = 4
REGION = TOK + N
ROW = 260
TILES = TOK // N + EXPERTS - 1
SLOTS = TILES + 1
RING = 8
DUMMY = EXPERTS * REGION
FAR = 1 << 20
EPS = 1e-5
CCOLS = {"ident": (0, 128), "ones": (128, 256), "kmask": (256, 260), "qind": (260, 264), "isq": (264, 268),
         "isk": (268, 272), "hmask": (272, 288), "pref": (288, 292), "iota": (292, 300), "base": (300, 308),
         "half": (308, 312), "before": (312, 440), "start": (440, 472), "upto": (472, 536), "tile": (536, 576),
         "regionT": (576, 584)}
NC = 584


WORK = 15700


def shape_constants():
    c = np.zeros((128, NC), np.float32)
    c[:, 0:128] = np.eye(128)
    c[:, 128:256] = 1.0
    for row in range(128):
        b, r = divmod(row, 32)
        part, j = divmod(r, QK)
        if part >= NPART:
            continue
        if j < TYPES:
            c[row, 260 + j] = 1.0
            c[row, 264 + b] = 1.0
        else:
            c[row, 256 + j - TYPES] = 1.0
            c[row, 268 + b] = 1.0
    for p in range(128):
        c[p, 272 + p // HD] = 1.0
    c[:, 288:292] = np.arange(GROUPS_E, 0, -1)
    c[:, 292:300] = np.arange(EXPERTS) - EXPERTS
    c[:, 300:308] = np.arange(EXPERTS) * REGION
    c[:, 308:312] = -0.5
    c[:, 312:440] = np.triu(np.ones((128, 128)), 1)
    c[:, 440:472] = np.arange(32) * N
    c[:, 472:536] = np.tril(np.ones((8, 8))).reshape(-1)
    c[:, 536:576] = np.arange(40)
    c[:, 576:584] = REGION
    return c


def build(nc, x, xT, adj, mask, weights, rowvecs, consts, ids, w1, w2, b1, b2, out):
    sorted_rows = nc.dram_tensor("sorted_rows", (DUMMY + N, ROW), F32, kind="Internal").ap()
    with ExitStack() as ctx:
        def sb(name, shape, dt=F32):
            return ctx.enter_context(nc.sbuf_tensor(name, shape, dt))

        def sem(name):
            return ctx.enter_context(nc.semaphore(name))

        x_t = sb("x_t", [128, TOK])
        ctx_t = sb("ctx_t", [128, TOK])
        w = sb("w", [128, NW])
        cst = sb("cst", [128, NC])
        rowv = sb("rowv", [128, NR])
        ident_h = sb("ident_h", [128, 128], BF16)
        room_p = sb("room_p", [128, 2 * TOK])
        room_v = sb("room_v", [128, 2 * TOK])
        room_w = sb("room_w", [128, WORK])
        penalty = room_p[:, :].bitcast(BF16).rearrange("p (b i m) -> p b i m", b=B, i=TYPES)
        pl_t = room_v[:, 0:TOK]
        adj_s = room_v[:, TOK:2 * TOK].bitcast(I32)
        vx = room_v[:, TOK:2 * TOK].rearrange("p (b d) -> p b d", b=B)
        k_m = [room_p[:, :].rearrange("p (h n) -> p h n", h=HEADS),
               room_v[:, :].rearrange("p (h n) -> p h n", h=HEADS)]
        used = {"a": 0, "b": 0, "c": 0}
        rooms = {"a": (room_w, WORK), "b": (room_w, WORK), "c": (room_p, 2 * TOK)}

        def carve(phase, shape, dt=F32):
            n = int(np.prod(shape[1:]))
            words = n if dt != BF16 else n // 2
            room, size = rooms[phase]
            ap = room[:, used[phase]:used[phase] + words]
            used[phase] += words
            assert used[phase] <= size, (phase, used[phase])
            if dt != F32:
                ap = ap.bitcast(dt)
            names = "abcde"[:len(shape) - 1]
            return ap.rearrange(f"p ({' '.join(names)}) -> p {' '.join(names)}", **dict(zip(names, shape[1:])))

        def A(*shape, dt=F32):
            return carve("a", shape, dt)

        def Bf(*shape, dt=F32):
            return carve("b", shape, dt)

        def Cf(*shape, dt=F32):
            return carve("c", shape, dt)

        mask_b = A(128, TOK)
        qkx = A(128, B, T_ITER, QK)
        w_v = A(128, 2, GB, 2, D + QK)
        ck_w2 = A(128, T_ITER * B, TYPES)
        bk_w2 = A(128, T_ITER * B * TYPES)
        key_fold = A(128, 3, T_ITER, B, TYPES)
        kbias = A(128, T_ITER, B, TYPES)
        shared = used["a"]
        w_x = A(128, B, D + TYPES + T_ITER * TYPES)
        used["a"] = shared
        plpc = A(128, 2, GT)
        v_s = A(128, 2, GB, D)
        logit = A(128, GB, N)
        leaky = A(128, GB, N)
        expo = A(128, GB, N)
        prob = A(128, GB, N)
        prob_t = A(128, GB, N)
        msg_s = A(128, GT)
        t_rhs = sb("t_rhs", [128, TYPES, N], BF16)
        t_lhs = sb("t_lhs", [128, GB, N], BF16)
        q_base = sb("q_base", [128, B])
        elu_z = sb("elu_z", [128, B])
        elu_n = sb("elu_n", [128, B])
        elu_e = sb("elu_e", [128, B])
        elu_s = sb("elu_s", [128, B])
        cmd = sb("cmd", [128, T_ITER, B])
        ck = sb("ck", [128, T_ITER * B])
        cv = sb("cv", [128, T_ITER, B])
        bq_w1 = sb("bq_w1", [128, TYPES])
        query_fold = sb("query_fold", [128, 3, TYPES])
        qbias = sb("qbias", [128, TYPES])
        qk = sb("qk", [128, GB, QK])
        res1 = sb("res1", [128, GB, QK])
        parts = sb("parts", [128, GB, 32], BF16)
        sel_s = sb("sel_s", [128, N], BF16)
        neg_top = sb("neg_top", [128, GB])
        shift = sb("shift", [128, GB])
        total = sb("total", [128, GB])
        inv = sb("inv", [128, GB])
        xc_s = Bf(128, 2, GT)
        q_s = Bf(128, 2, GT)
        k_s = Bf(128, GT)
        v_a = Bf(128, 2, GB, VROW)
        dif = Bf(128, 2, 4, N)
        ex = Bf(128, 2, 4, N)
        ex_t = Bf(128, 2, 4, N)
        o_a = Bf(128, 2, GB * HEADS, VW)
        o_n = Bf(128, GB, D)
        o_t = Bf(128, GT)
        h_s = Bf(128, GB, D)
        xn = Bf(128, GB, D)
        x1_t = Bf(128, GT)
        x1_g = Bf(128, GB, D)
        rows = Bf(128, GB, ROW)
        pad_row = Bf(128, ROW)
        top = sb("top", [128, 2, 4])
        rden = sb("rden", [128, GB * HEADS])
        stats = sb("stats", [128, GB, 6])
        mv = sb("mv", [128, GB, 2])
        ve = sb("ve", [128, GB])
        rstd = sb("rstd", [128, GB])
        id_s = sb("id_s", [128, B], I32)
        lg = sb("lg", [128, GB, 12])
        gm = sb("gm", [128, GB])
        dg = sb("dg", [128, GB, 4])
        eg = sb("eg", [128, GB, 4])
        sc = sb("sc", [128, GB, 4])
        sm = sb("sm", [128, GB])
        oh = sb("oh", [128, GB, 4])
        pr = sb("pr", [128, GB, 4, 2])
        el = sb("el", [128, GB, 2])
        de = sb("de", [128, GB])
        nd = sb("nd", [128, GB])
        ee = sb("ee", [128, GB])
        gs = sb("gs", [128, GB])
        den = sb("den", [128, GB])
        k1 = sb("k1", [128, GB])
        ev = sb("ev", [128, GB])
        OH = sb("OH", [128, GB, EXPERTS])
        oh_h = sb("oh_h", [128, GB, EXPERTS], BF16)
        cs = sb("cs", [128, GB + 1, EXPERTS])
        cs_h = sb("cs_h", [128, GB, EXPERTS], BF16)
        rk = sb("rk", [128, GB, EXPERTS])
        rk2 = sb("rk2", [128, GB, EXPERTS])
        slot = sb("slot", [128, GB])
        slot_i = sb("slot_i", [128, GB], I32)
        cnt_h = sb("cnt_h", [128, EXPERTS], BF16)
        cnt = sb("cnt", [128, EXPERTS])
        full = Cf(128, EXPERTS, 32)
        nt = sb("nt", [128, EXPERTS])
        ntu = Cf(128, EXPERTS, EXPERTS)
        cum = sb("cum", [128, EXPERTS])
        hop = sb("hop", [128, EXPERTS])
        behind = Cf(128, SLOTS, EXPERTS)
        hops = Cf(128, SLOTS, EXPERTS)
        t_exp = sb("t_exp", [128, SLOTS])
        t_hop = sb("t_hop", [128, SLOTS])
        t_row = sb("t_row", [128, SLOTS])
        pad_at = sb("pad_at", [128, EXPERTS])
        row_i = sb("row_i", [128, SLOTS], I32)
        exp_i = sb("exp_i", [128, SLOTS], I32)
        pad_i = sb("pad_i", [128, EXPERTS], I32)
        w1_s, w2_s = ctx_t[:, 0:TOK // 2], ctx_t[:, TOK // 2:TOK]
        b1_s, b2_s = x_t[:, 0:EXPERTS * FF], x_t[:, EXPERTS * FF:EXPERTS * (FF + D)]
        tile_s = Cf(128, RING, ROW)
        xt_s = Cf(128, 2, D)
        hb_s = Cf(128, 2, FF)
        ht_s = Cf(128, 2, FF)
        yb = Cf(128, 2, D)
        res = Cf(128, 2, D)
        st2 = sb("st2", [128, 2, 6])
        mv2 = sb("mv2", [128, 2, 2])
        sd2 = sb("sd2", [128, 2])
        rs2 = sb("rs2", [128, 2])
        xn2 = Cf(128, 2, D)
        xg2 = Cf(128, 2, D)
        xb2 = Cf(128, 2, D)
        fin = Cf(128, 2, D)
        eps_s = sb("eps_s", [128, 1])
        before_h = sb("before_h", [128, 128], BF16)
        ones_h = sb("ones_h", [128, 128], BF16)

        def W(name, c=0, n=D):
            a = WCOLS[name][0] + c * D
            return w[:, a:a + n]

        def bias(name):
            a = WCOLS["bias"][0] + BIAS[name]
            return w[:, a:a + 1]

        def C(name):
            a, b = CCOLS[name]
            return cst[:, a:b]

        def R(name):
            a, b = RCOLS[name]
            return rowv[:, a:b]

        def bank(name, shape, dt=F32):
            return ctx.enter_context(nc.psum_tensor(name, shape, dt))
        PC = bank("PC", [128, GT])
        V = bank("V", [128, GB, 256])
        T0 = bank("T0", [128, TYPES, N])
        T1 = bank("T1", [128, TYPES, N])
        PT = bank("PT", [128, GB, N])
        M = bank("M", [128, GB, N])
        U = bank("U", [128, GT])
        TB = [T0, T1]
        SEL = PT[:, 0, 0:N // 2].bitcast(BF16)
        SB = [T0, T1]
        PB = [PT, M]
        OB = [PC[:, :].rearrange("p (h d) -> p h d", h=4), U[:, :].rearrange("p (h d) -> p h d", h=4)]
        X0 = V[:, 0:2, :].rearrange("p a c -> p (a c)")
        X1 = V[:, 2:4, :].rearrange("p a c -> p (a c)")
        XT = [T0[:, 0, :], T1[:, 0, :]]
        HB = [PT[:, 0:2, :].rearrange("p a n -> p (a n)"), M[:, 0:2, :].rearrange("p a n -> p (a n)")]
        HT = [PC[:, 0:FF], U[:, 0:FF]]
        YB = [X0[:, 0:D], X1[:, 0:D]]

        in_w, in_x, in_adj, in_mask, in_c, in_bv = (sem(n) for n in (
            "in_w", "in_x", "in_adj", "in_mask", "in_c", "in_bv"))
        (zq_mm, zq_done, zneg_done, zexp_done, zsum_done, qbase_ready, cmd_mm, cmd_ready, ck_mm, cv_mm, ck_ready,
         cv_ready, ckw2_ready, bkw2_ready, bqw1_ready, fold_mm, fold_ready, qfold_mm, qfold_ready, kbias_mm,
         kbias_ready, qbias_mm, qbias_ready, consts_ready, wx_ready, wv_const) = (sem(n) for n in (
             "zq_mm", "zq_done", "zneg_done", "zexp_done", "zsum_done", "qbase_ready", "cmd_mm", "cmd_ready",
             "ck_mm", "cv_mm", "ck_ready", "cv_ready", "ckw2_ready", "bkw2_ready", "bqw1_ready", "fold_mm",
             "fold_ready", "qfold_mm", "qfold_ready", "kbias_mm", "kbias_ready", "qbias_mm", "qbias_ready",
             "consts_ready", "wx_ready", "wv_const"))
        pl_mm, pl_done, vx_mm, vx_read, pen_done = (sem(n) for n in (
            "pl_mm", "pl_done", "vx_mm", "vx_read", "pen_done"))
        (pc_done, plpc_done, wv_ready, v_done, qk_done, hi_done, res1_done, mid_done, parts_done,
         v_evac, sel_done, sel_copied, ops_done, t_done, red_done, top_done, shift_done, leaky_done, exp_done,
         inv_done, prob_done, pt_done, pt_evac, msg_done, msg_evac, mu_done, ctx_done) = (sem(n) for n in (
             "pc_done", "plpc_done", "wv_ready", "v_done", "qk_done", "hi_done", "res1_done", "mid_done",
             "parts_done", "v_evac", "sel_done", "sel_copied", "ops_done", "t_done", "red_done",
             "top_done", "shift_done", "leaky_done", "exp_done", "inv_done", "prob_done", "pt_done",
             "pt_evac", "msg_done", "msg_evac", "mu_done", "ctx_done"))

        sems = {}

        def S(name):
            if name not in sems:
                sems[name] = sem(name)
            return sems[name]

        STEPS = T_ITER * G
        UNITS = GB * HEADS // 4

        def groups(eng, body):
            body(0, 0, False, True)
            with eng.Fori(0, (G - 2) // 2) as pair:
                body(2 * pair + 1, 1, True, True)
                body(2 * pair + 2, 0, True, True)
            body(G - 1, 1, True, False)

        def tiles(eng, slot_of):
            for k in range(RING):
                slot_of(k, k)
            with eng.Fori(1, SLOTS // RING) as lap:
                for r in range(RING):
                    slot_of(RING * lap + r, r)
            for k in range(SLOTS, SLOTS + LAST):
                slot_of(k, k % RING)

        def tile_turn(k, r):
            return 2 * (k - r) + 16

        LAST = 4

        def rounds(eng, step):
            with eng.Fori(0, T_ITER - 1) as t:
                for g in range(G):
                    step(t, g, True, True)
            for g in range(G):
                s = (T_ITER - 1) * G + g
                step(T_ITER - 1, g, s + 1 < STEPS, s + 2 < STEPS)

        def after(t, g, k):
            return t + (g + k) // G, (g + k) % G

        block = ctx.enter_context(nc.Block())

        @block.sync
        def _(sp):
            sp.dma_start(w[:, :], weights).then_inc(in_w, 16)
            sp.dma_start(cst[:, :], consts).then_inc(in_c, 16)
            sp.dma_start(x_t[:, :], xT).then_inc(in_x, 16)
            sp.dma_start(adj_s[:, :], adj).then_inc(in_adj, 16)
            sp.dma_start(mask_b[:, :], mask.broadcast_to([128, TOK])).then_inc(in_mask, 16)
            sp.dma_start(rowv[:, :], rowvecs.broadcast_to([128, NR])).then_inc(in_bv, 16)
            sp.dma_start(id_s[:, :], ids).then_inc(S("in_ids"), 16)
            x_rows = x.rearrange("b n d -> n b d")
            sp.wait_ge(ctx_done, G + STEPS)
            sp.dma_start(rows[:, :, D:2 * D], x_rows[:, 0:GB, :]).then_inc(S("in_rows"), 16)
            with sp.Fori(1, G) as g:
                sp.wait_ge(S("scattered"), 16 * GB * g)
                sp.dma_start(rows[:, :, D:2 * D], x_rows[:, bass.ds(g * GB, GB), :]).then_inc(S("in_rows"), 16)
            sp.wait_ge(S("cond_mm"), G)
            sp.dma_start(w1_s, w1).then_inc(S("in_experts"), 16)
            sp.dma_start(w2_s, w2).then_inc(S("in_experts"), 16)
            sp.dma_start(b1_s, b1.broadcast_to([128, EXPERTS * FF])).then_inc(S("in_experts"), 16)
            sp.dma_start(b2_s, b2.broadcast_to([128, EXPERTS * D])).then_inc(S("in_experts"), 16)
            sp.wait_ge(S("pad_ready"), 2)
            sp.dma_start(sorted_rows[DUMMY:DUMMY + N, :], pad_row[:, :]).then_inc(S("padded"), 16)
            sp.wait_ge(S("table_ready"), 3)
            for e in range(EXPERTS):
                at = sp.value_load(pad_i[0:1, e:e + 1], min_val=e * REGION, max_val=e * REGION + TOK)
                sp.dma_start(sorted_rows[bass.ds(at, N), :], pad_row[:, :]).then_inc(S("padded"), 16)
            sp.wait_ge(S("padded"), 16 * (EXPERTS + 1))
            sp.wait_ge(S("scattered"), 16 * B)

            def load_tile(k, r):
                at = sp.value_load(row_i[0:1, bass.ds(k, 1)], min_val=0, max_val=DUMMY)
                sp.dma_start(tile_s[:, r, :], sorted_rows[bass.ds(at, N), :]).then_inc(S(f"in_tile{r}"), 16)
            for k in range(RING):
                load_tile(k, k)
            with sp.Fori(1, SLOTS // RING) as lap:
                for r in range(RING):
                    k = RING * lap + r
                    sp.wait_ge(S(f"sent{r}"), tile_turn(k - RING, r))
                    load_tile(k, r)
            for r in range(RING):
                sp.wait_ge(S(f"sent{r}"), 16 * (SLOTS // RING))

        @block.gpsimd
        def _(pool):
            pool.wait_ge(in_w, 16)
            pool.tensor_copy(w_x[:, :, 0:D], W("v", 0).unsqueeze(1).broadcast_to([128, B, D])).then_inc(wx_ready, 1)
            for par in range(2):
                for c in range(2):
                    pool.tensor_copy(w_v[:, par, :, c, 0:D], W("v", 1 + c).unsqueeze(1).broadcast_to([128, GB, D]))\
                        .then_inc(wv_const, 1)
            pool.wait_ge(qfold_ready, 1)
            pool.wait_ge(fold_ready, 2)
            pool.wait_ge(msg_evac, 1)
            pool.tensor_copy(w_x[:, :, D:D + TYPES],
                             query_fold[:, 0, :].unsqueeze(1).broadcast_to([128, B, TYPES])).then_inc(wx_ready, 1)
            for t in range(T_ITER):
                pool.tensor_copy(w_x[:, :, D + TYPES * (1 + t):D + TYPES * (2 + t)],
                                 key_fold[:, 0, t, :, :]).then_inc(wx_ready, 1)
            for par in range(2):
                pool.tensor_copy(w_v[:, par, :, :, D:D + TYPES],
                                 query_fold[:, 1:3, :].unsqueeze(1).broadcast_to([128, GB, 2, TYPES]))\
                    .then_inc(wv_const, 1)

            def key_columns(t, g):
                pool.tensor_copy(w_v[:, g % 2, :, :, D + TYPES:D + QK],
                                 key_fold[:, 1:3, bass.ds(t, 1), g * GB:(g + 1) * GB, :]
                                 .rearrange("p c t b i -> p (t b) c i")).then_inc(wv_ready, 1)
            key_columns(0, 0)
            key_columns(0, 1)
            pool.wait_ge(v_done, 1)
            key_columns(0, 2)

            def step(t, g, front, ahead):
                s = t * G + g
                if isinstance(t, int) and s + 3 >= STEPS:
                    return
                pool.wait_ge(v_done, s + 2)
                key_columns(*after(t, g, 3))
            rounds(pool, step)

            pool.wait_ge(ctx_done, G + STEPS)
            pool.memset(v_a[:, :, :, :], 0.0).then_inc(S("va_zero"), 1)
            pool.wait_ge(S("va_zero"), 1)
            for par in range(2):
                ones = v_a[:, par, :, 0:HEADS * VW].rearrange("p b (h c) -> p b h c", c=VW)[:, :, :, HD]
                pool.memset(ones, 1.0).then_inc(S("va_ones"), 1)
            pool.memset(pad_row[:, :], 0.0).then_inc(S("pad_ready"), 1)
            pool.wait_ge(S("pad_ready"), 1)
            pool.memset(pad_row[:, 2 * D + 1:2 * D + 2].bitcast(I32), FAR).then_inc(S("pad_ready"), 1)
            pool.wait_ge(S("in_ids"), 16)
            pool.wait_ge(in_bv, 16)

            def norm1_power(p):
                pool.wait_ge(S("var_ready"), p + 1)
                pool.tensor_tensor(rstd[:, :], ve[:, :], C("half"), ALU.pow).then_inc(S("rstd_ready"), 1)

            def rows_x1(p):
                pool.wait_ge(S("xn_ready"), p + 1)
                bc = lambda n: R(n).unsqueeze(1).broadcast_to([128, GB, D])
                pool.tensor_tensor(x1_g[:, :, :], xn[:, :, :], bc("ln1g"), ALU.mult).then_inc(S("x1g_ready"), 1)
                pool.wait_ge(S("x1g_ready"), p + 1)
                pool.wait_ge(S("in_rows"), 16 * (p + 1))
                pool.tensor_tensor(rows[:, :, 0:D], x1_g[:, :, :], bc("ln1b"), ALU.add).then_inc(S("row_x1"), 1)
                pool.tensor_copy(rows[:, :, 2 * D + 1:2 * D + 2].bitcast(I32),
                                 id_s[:, bass.ds(p * GB, GB)].unsqueeze(2)).then_inc(S("row_x1"), 1)

            def scatter(p):
                pool.wait_ge(S("slot_ready"), p + 1)
                pool.wait_ge(S("row_x1"), 2 * (p + 1)).then_inc(S("passed"), 1)
                for b in range(GB):
                    pool.indirect_dma_start(sorted_rows, bass.IndirectOffsetOnAxis(ap=slot_i[:, b:b + 1], axis=0),
                                            rows[:, b, :], None, bounds_check=DUMMY - 1, oob_is_err=False)\
                        .then_inc(S("scattered"), 16)

            def body(g, par, prev, nxt):
                if prev:
                    norm1_power(g - 1)
                    rows_x1(g - 1)
                    scatter(g - 1)
            groups(pool, body)
            norm1_power(G - 1)
            rows_x1(G - 1)
            scatter(G - 1)

            def slot_of(k, r):
                static = isinstance(k, int)
                if not (static and (k < 3 or k - 3 >= SLOTS)):
                    t, q, rr = k - 3, (r - 3) % 2, (r - 3) % RING
                    pool.wait_ge(S(f"in_tile{rr}"), tile_turn(t, rr))
                    if not (static and t < 2):
                        pool.wait_ge(S("fin_ready"), t - 1)
                    pool.tensor_tensor(xb2[:, q, :], tile_s[:, rr, D:2 * D], R("ln2b"), ALU.add).then_inc(S("xb_ready"), 1)
                if not (isinstance(k, int) and k < LAST):
                    q = (r - LAST) % RING
                    pool.wait_ge(S("fin_ready"), k - LAST + 1).then_inc(S("passed"), 1)
                    pool.indirect_dma_start(out, bass.IndirectOffsetOnAxis(
                        ap=tile_s[:, q, 2 * D + 1:2 * D + 2].bitcast(I32), axis=0), fin[:, q % 2, :], None,
                        bounds_check=TOK - 1, oob_is_err=False).then_inc(S(f"sent{q}"), 16)
            tiles(pool, slot_of)

        @block.tensor
        def _(pe):
            flat = "p a n -> p (a n)"
            pe.wait_ge(in_w, 16)
            pe.matmul(U[:, 0:B], W("qin"), w[:, WCOLS["fside"][0]:WCOLS["fside"][1]], start=True, stop=True)\
                .then_inc(zq_mm, 1)
            pe.wait_ge(qbase_ready, 1)
            for t in range(T_ITER):
                mm = pe.matmul(M[:, t, 0:B], W("qt", t), q_base[:, :], start=True, stop=True)
            mm.then_inc(cmd_mm, 1)
            pe.wait_ge(cmd_ready, T_ITER)
            cmds = cmd[:, :, :].rearrange("p t b -> p (t b)")
            pe.matmul(PT[:, 0, :], W("pk"), cmds, start=True, stop=True).then_inc(ck_mm, 1)
            pe.matmul(U[:, 0:N], W("pv"), cmds, start=True, stop=True).then_inc(cv_mm, 1)
            pe.wait_ge(ckw2_ready, 1)
            folds = ck_w2[:, :, :].rearrange("p a i -> p (a i)")
            for c, bk in enumerate((T0, T1, M)):
                pe.matmul(bk[:, :, :].rearrange(flat), W("wk", c), folds, start=True, stop=True).then_inc(fold_mm, 1)
            pe.wait_ge(cv_ready, 1)
            for c in range(3):
                mm = pe.matmul(U[:, TYPES * c:TYPES * (c + 1)], W("wq", c),
                               w[:, WCOLS["w1t"][0]:WCOLS["w1t"][1]], start=True, stop=True)
            mm.then_inc(qfold_mm, 1)
            pe.wait_ge(in_c, 16)
            pe.wait_ge(ck_ready, 1)
            pe.wait_ge(bkw2_ready, 1)
            pe.matmul(PT[:, :, :].rearrange(flat), C("ones"), bk_w2[:, :], start=True, stop=True).then_inc(kbias_mm, 1)
            pe.wait_ge(bqw1_ready, 1)
            pe.matmul(PC[:, 0:TYPES], C("ones"), bq_w1[:, :], start=True, stop=True).then_inc(qbias_mm, 1)
            pe.wait_ge(in_x, 16)
            pe.wait_ge(fold_ready, 2)
            for g in range(G):
                if g >= 2:
                    pe.wait_ge(pl_done, g - 1)
                pe.matmul(TB[g % 2][:, :, :].rearrange(flat), W("pl"), x_t[:, g * GT:(g + 1) * GT],
                          start=True, stop=True).then_inc(pl_mm, 1)
            pe.wait_ge(wx_ready, 2 + T_ITER)
            for b in range(B):
                if b % 2 == 0 and b >= GB:
                    pe.wait_ge(vx_read, b // 2 - 1)
                mm = pe.matmul(V[:, b % GB, 0:D + TYPES * (1 + T_ITER)], x_t[:, b * N:(b + 1) * N], w_x[:, b, :],
                               start=True, stop=True)
                if b % 2:
                    mm.then_inc(vx_mm, 1)

            def pc(s, g):
                pe.wait_ge(ctx_done, s + 1)
                pe.wait_ge(plpc_done, s)
                pe.matmul(PC[:, :], W("pc"), ctx_t[:, g * GT:(g + 1) * GT], start=True, stop=True).then_inc(pc_done, 1)

            def v(s, g):
                pe.wait_ge(plpc_done, s + 1)
                pe.wait_ge(wv_ready, s + 1)
                pe.wait_ge(qk_done, s)
                pe.wait_ge(v_evac, s)
                for b in range(GB):
                    pe.matmul(V[:, b, 0:D + QK], ctx_t[:, g * GT + b * N:g * GT + (b + 1) * N],
                              w_v[:, g % 2, b, 0, :], start=True, stop=False)
                    mm = pe.matmul(V[:, b, 0:D + QK], plpc[:, g % 2, b * N:(b + 1) * N],
                                   w_v[:, g % 2, b, 1, :], start=False, stop=True)
                mm.then_inc(v_done, 1)

            def sel(s):
                pe.wait_ge(parts_done, s + 1)
                pe.wait_ge(pt_evac, s)
                pe.transpose(SEL, parts[:, :, :].rearrange("p b r -> p (b r)"), ident_h[:, :]).then_inc(sel_done, 1)

            def scores(s, g):
                pe.wait_ge(ops_done, s + 1)
                for b in range(GB):
                    pe.wait_ge(red_done, s * GB + max(b - 1, 0))
                    bk = TB[b % 2][:, :, :].rearrange(flat)
                    pe.matmul(bk, ident_h[:, :], penalty[:, g * GB + b, :, :].rearrange("p i m -> p (i m)"),
                              start=True, stop=False)
                    pe.matmul(bk, t_lhs[:, b, :], t_rhs[:, :, :].rearrange("p i m -> p (i m)"),
                              start=False, stop=True).then_inc(t_done, 1)

            def turn(s):
                pe.wait_ge(prob_done, s + 1)
                pe.wait_ge(sel_copied, s + 1)
                for b in range(GB):
                    mm = pe.transpose(PT[:, b, :], prob[:, b, :], C("ident"))
                mm.then_inc(pt_done, 1)

            def message(s, g):
                pe.wait_ge(pt_evac, s + 1)
                pe.wait_ge(v_evac, s + 1)
                pe.wait_ge(msg_evac, s + 1)
                for b in range(GB):
                    mm = pe.matmul(M[:, b, :], v_s[:, g % 2, b, :], prob_t[:, b, :], start=True, stop=True)
                mm.then_inc(msg_done, 1)

            def update(s, g):
                pe.wait_ge(msg_evac, s + 2)
                pe.wait_ge(ctx_done, G + s)
                pe.matmul(U[:, :], W("mu", 0), ctx_t[:, g * GT:(g + 1) * GT], start=True, stop=False)
                pe.matmul(U[:, :], W("mu", 1), msg_s[:, :], start=False, stop=True).then_inc(mu_done, 1)

            pe.wait_ge(qbias_ready, 1)
            pe.wait_ge(kbias_ready, 1)
            pc(0, 0)
            pe.wait_ge(wv_const, 6)
            pe.wait_ge(vx_read, B // 2)
            v(0, 0)
            pc(1, 1)
            pe.wait_ge(consts_ready, 2)
            sel(0)
            pe.wait_ge(pl_done, G)
            pe.wait_ge(pen_done, TYPES)
            scores(0, 0)

            def step(t, g, front, ahead):
                s, n = t * G + g, (g + 1) % G
                if front:
                    v(s + 1, n)
                turn(s)
                if ahead:
                    pc(s + 2, (g + 2) % G)
                if front:
                    sel(s + 1)
                message(s, g)
                if front:
                    scores(s + 1, n)
                update(s, g)
            rounds(pe, step)

            def cond(g, par):
                pe.matmul(X0, W("cb", 0), x_t[:, bass.ds(g * GT, GT)], start=True, stop=False)
                pe.matmul(X0, W("cb", 1), ctx_t[:, bass.ds(g * GT, GT)], start=False, stop=True).then_inc(S("cond_mm"), 1)

            def query(g, par):
                pe.wait_ge(S("cond_ready"), g + 1)
                pe.matmul(X1, W("wi", 0), xc_s[:, par, :], start=True, stop=True).then_inc(S("query_mm"), 1)

            def key(g, par):
                pe.matmul(X0, W("wi", 1), xc_s[:, par, :], start=True, stop=True).then_inc(S("key_mm"), 1)

            def value(g, par):
                pe.wait_ge(S("query_ready"), g + 1)
                for b in range(GB):
                    mm = pe.matmul(X1[:, b * N:(b + 1) * N], xc_s[:, par, b * N:(b + 1) * N], W("wi", 2),
                                   start=True, stop=True)
                mm.then_inc(S("value_mm"), 1)

            def head_scores(u, g, par, j):
                b, q = divmod(j, 4)
                pe.wait_ge(S("query_ready"), g + 1)
                pe.wait_ge(S("km_ready"), HEADS * g + (4 * (q + 1) if b == 0 else HEADS))
                if not (isinstance(u, int) and u < 2):
                    pe.wait_ge(S("dif_ready"), u - 1)
                pe.matmul(SB[j % 2][:, :, :].rearrange(flat), q_s[:, par, b * N:(b + 1) * N],
                          k_m[par][:, 4 * q:4 * q + 4, b * N:(b + 1) * N], start=True, stop=True)\
                    .then_inc(S("scores_mm"), 1)

            def turn_exps(u, j):
                pe.wait_ge(S("ex_ready"), u + 1)
                if not (isinstance(u, int) and u < 2):
                    pe.wait_ge(S("ext_ready"), u - 1)
                for h in range(4):
                    mm = pe.transpose(PB[j % 2][:, h, :], ex[:, j % 2, h, :], C("ident"))
                mm.then_inc(S("ext_mm"), 1)

            def weigh(u, g, par, j):
                b, q = divmod(j, 4)
                pe.wait_ge(S("ext_ready"), u + 1)
                pe.wait_ge(S("value_ready"), g + 1)
                if not (isinstance(u, int) and u < 2):
                    pe.wait_ge(S("o_ready"), u - 1)
                for h in range(4):
                    at = VW * (4 * q + h)
                    mm = pe.matmul(OB[j % 2][:, h, :], ex_t[:, j % 2, h, :], v_a[:, par, b, at:at + N],
                                   start=True, stop=True)
                mm.then_inc(S("o_mm"), 1)

            def turn_heads(p):
                pe.wait_ge(S("on_ready"), p + 1)
                for b in range(GB):
                    mm = pe.transpose(X0[:, b * N:(b + 1) * N], o_n[:, b, :], C("ident"))
                mm.then_inc(S("ot_mm"), 1)

            def residual(p, par):
                pe.wait_ge(S("ot_ready"), p + 1)
                for b in range(GB):
                    cols = slice(b * N, (b + 1) * N)
                    pe.matmul(X1[:, cols], xc_s[:, par, cols], C("ident"), start=True, stop=False)
                    mm = pe.matmul(X1[:, cols], o_t[:, cols], W("wo"), start=False, stop=True)
                mm.then_inc(S("h_mm"), 1)

            def turn_norm(p):
                pe.wait_ge(S("xn_ready"), p + 1)
                for b in range(GB):
                    mm = pe.transpose(X0[:, b * N:(b + 1) * N], xn[:, b, :], C("ident"))
                mm.then_inc(S("x1t_mm"), 1)

            def gate(p):
                pe.wait_ge(S("x1t_ready"), p + 1)
                for b in range(GB):
                    mm = pe.matmul(X1[:, b * N:(b + 1) * N], x1_t[:, b * N:(b + 1) * N], W("gate"), start=True, stop=True)
                mm.then_inc(S("gate_mm"), 1)

            def rank(p):
                pe.wait_ge(S("cs_ready"), p + 1)
                cols = X0[:, 0:GB * EXPERTS]
                pe.matmul(cols, before_h[:, :], oh_h[:, :, :].rearrange("p b e -> p (b e)"), start=True, stop=False)
                pe.matmul(cols, ones_h[:, :], cs_h[:, :, :].rearrange("p b e -> p (b e)"), start=False, stop=True)\
                    .then_inc(S("rank_mm"), 1)

            pe.wait_ge(ctx_done, G + STEPS)
            pe.wait_ge(S("halves_ready"), 2)
            cond(0, 0)
            query(0, 0)
            key(0, 0)
            value(0, 0)
            head_scores(0, 0, 0, 0)
            head_scores(1, 0, 0, 1)

            def body(g, par, prev, nxt):
                for j in range(UNITS):
                    u = g * UNITS + j
                    if j + 2 < UNITS:
                        head_scores(u + 2, g, par, j + 2)
                    elif nxt:
                        head_scores(u + 2, g + 1, 1 - par, j + 2 - UNITS)
                    turn_exps(u, j)
                    if j:
                        weigh(u - 1, g, par, j - 1)
                    elif prev:
                        weigh(u - 1, g - 1, 1 - par, UNITS - 1)
                    if prev and j == 3:
                        turn_heads(g - 1)
                    if prev and j == 5:
                        residual(g - 1, 1 - par)
                    if nxt and j == 6:
                        if prev:
                            pe.wait_ge(S("ot_ready"), g)
                        cond(g + 1, 1 - par)
                    if nxt and j == 7:
                        if prev:
                            pe.wait_ge(S("h_ready"), g)
                        query(g + 1, 1 - par)
                    if nxt and j == 8:
                        key(g + 1, 1 - par)
                    if nxt and j == 9:
                        value(g + 1, 1 - par)
                    if prev and j == 10:
                        pe.wait_ge(S("key_ready"), g + 1 + nxt)
                        turn_norm(g - 1)
                    if prev and j == 12:
                        pe.wait_ge(S("value_ready"), g + 1 + nxt)
                        gate(g - 1)
                    if prev and j == 15:
                        pe.wait_ge(S("x1t_ready"), g)
                        rank(g - 1)
            groups(pe, body)
            weigh(G * UNITS - 1, G - 1, 1, UNITS - 1)
            turn_heads(G - 1)
            residual(G - 1, 1)
            turn_norm(G - 1)
            gate(G - 1)
            rank(G - 1)
            pe.wait_ge(S("cnt_h_ready"), 1)
            pe.wait_ge(S("lg_ready"), G)
            pe.matmul(X1[:, 0:EXPERTS], ones_h[:, :], cnt_h[:, :], start=True, stop=True).then_inc(S("cnt_mm"), 1)

            def slot_of(k, r):
                i = r % 2
                static = isinstance(k, int)
                if not (static and k < 3):
                    q = (i + 1) % 2
                    if not (static and k - 3 >= SLOTS):
                        e = pe.value_load(exp_i[0:1, bass.ds(k - 3, 1)], min_val=0, max_val=EXPERTS - 1)
                        if not (static and k < 5):
                            pe.wait_ge(S("yb_ready"), k - 4)
                        pe.wait_ge(S("ht_ready"), k - 2)
                        for f in range(2):
                            mm = pe.matmul(YB[q], ht_s[:, q, f * N:(f + 1) * N], w2_s[:, bass.ds(e * FF + f * D, D)],
                                           start=(f == 0), stop=(f == 1))
                        mm.then_inc(S("y_mm"), 1)
                if not (static and (k < 2 or k - 2 >= SLOTS)):
                    pe.wait_ge(S("hb_ready"), k - 1)
                    if not (static and k < 4):
                        pe.wait_ge(S("ht_ready"), k - 3)
                    for f in range(2):
                        mm = pe.transpose(HT[i][:, f * N:(f + 1) * N], hb_s[:, i, f * N:(f + 1) * N], C("ident"))
                    mm.then_inc(S("ht_mm"), 1)
                if not (static and (k < 1 or k - 1 >= SLOTS)):
                    q = (i + 1) % 2
                    e = pe.value_load(exp_i[0:1, bass.ds(k - 1, 1)], min_val=0, max_val=EXPERTS - 1)
                    pe.wait_ge(S("xt_ready"), k)
                    if not (static and k < 3):
                        pe.wait_ge(S("hb_ready"), k - 2)
                    pe.matmul(HB[q], xt_s[:, q, :], w1_s[:, bass.ds(e * FF, FF)], start=True, stop=True)\
                        .then_inc(S("hb_mm"), 1)
                if not (static and k >= SLOTS):
                    pe.wait_ge(S(f"in_tile{r}"), tile_turn(k, r))
                    if not (static and k < 2):
                        pe.wait_ge(S("xt_ready"), k - 1)
                    pe.transpose(XT[i], tile_s[:, r, 0:D], C("ident")).then_inc(S("xt_mm"), 1)
            pe.wait_ge(S("in_experts"), 64)
            pe.wait_ge(S("table_ready"), 3)
            tiles(pe, slot_of)

        @block.vector
        def _(dve):
            dve.memset(parts[:, :, :], 0.0).then_inc(consts_ready, 1)
            dve.wait_ge(in_w, 16)
            dve.wait_ge(zq_mm, 1)
            dve.tensor_scalar(elu_z[:, :], U[:, 0:B], bias("qin"), None, ALU.add).then_inc(zq_done, 1)
            dve.wait_ge(zq_done, 1)
            dve.tensor_scalar(elu_n[:, :], elu_z[:, :], 0.0, None, ALU.min).then_inc(zneg_done, 1)
            dve.wait_ge(zexp_done, 1)
            dve.scalar_tensor_tensor(elu_s[:, :], elu_z[:, :], 0.0, elu_e[:, :], ALU.max, ALU.add).then_inc(zsum_done, 1)
            dve.wait_ge(zsum_done, 1)
            dve.tensor_scalar(q_base[:, :], elu_s[:, :], -1.0, None, ALU.add).then_inc(qbase_ready, 1)
            dve.tensor_scalar(bq_w1[:, :], w[:, WCOLS["w1t"][0]:WCOLS["w1t"][1]], bias("q"), None, ALU.mult)\
                .then_inc(bqw1_ready, 1)
            dve.wait_ge(in_c, 16)
            dve.tensor_copy(ident_h[:, :], C("ident")).then_inc(consts_ready, 1)
            dve.wait_ge(ck_ready, 1)
            dve.tensor_tensor(ck_w2[:, :, :], ck[:, :].unsqueeze(2).broadcast_to([128, T_ITER * B, TYPES]),
                              w[:, WCOLS["w2t"][0]:WCOLS["w2t"][1]].unsqueeze(1).broadcast_to([128, T_ITER * B, TYPES]),
                              ALU.mult).then_inc(ckw2_ready, 1)
            dve.wait_ge(ckw2_ready, 1)
            dve.tensor_scalar(bk_w2[:, :], ck_w2[:, :, :].rearrange("p a i -> p (a i)"), bias("k"), None, ALU.mult)\
                .then_inc(bkw2_ready, 1)
            dve.wait_ge(in_mask, 16)
            dve.tensor_scalar(ctx_t[:, :], mask_b[:, :], bias("init"), None, ALU.mult).then_inc(ctx_done, G)
            dve.wait_ge(kbias_mm, 1)
            dve.tensor_copy(kbias[:, :, :, :].rearrange("p t b i -> p (t b i)"),
                            PT[:, :, :].rearrange("p a n -> p (a n)")).then_inc(kbias_ready, 1)
            dve.wait_ge(qbias_mm, 1)
            dve.tensor_copy(qbias[:, :], PC[:, 0:TYPES]).then_inc(qbias_ready, 1)
            dve.wait_ge(in_adj, 16)
            adjs = adj_s[:, :].rearrange("p (b m) -> p b m", b=B)
            for i in range(TYPES):
                dve.tensor_scalar(penalty[:, :, i, :], adjs, float(i + 1), -BIG, ALU.not_equal, ALU.mult)\
                    .then_inc(pen_done, 1)
            dve.wait_ge(in_bv, 16)
            dve.wait_ge(qbias_ready, 1)
            dve.wait_ge(kbias_ready, 1)
            dve.wait_ge(pen_done, TYPES)
            for pair in range(B // 2):
                dve.wait_ge(vx_mm, pair + 1)
                bs = slice(2 * pair, 2 * pair + 2)
                vb = V[:, 2 * (pair % 2):2 * (pair % 2) + 2, :]
                dve.tensor_tensor(vx[:, bs, :], vb[:, :, 0:D], R("bv").unsqueeze(1).broadcast_to([128, 2, D]), ALU.add)
                dve.tensor_tensor(qkx[:, bs, :, 0:TYPES],
                                  vb[:, :, D:D + TYPES].unsqueeze(2).broadcast_to([128, 2, T_ITER, TYPES]),
                                  qbias[:, :].unsqueeze(1).unsqueeze(1).broadcast_to([128, 2, T_ITER, TYPES]), ALU.add)
                dve.tensor_tensor(qkx[:, bs, :, TYPES:QK],
                                  vb[:, :, D + TYPES:D + TYPES * (1 + T_ITER)].rearrange("p b (t i) -> p b t i", i=TYPES),
                                  kbias[:, :, bs, :].rearrange("p t b i -> p b t i"), ALU.add).then_inc(vx_read, 1)
            dve.wait_ge(vx_read, B // 2)
            dve.wait_ge(pl_done, G)

            def pl_times_pc(s, g):
                dve.wait_ge(pc_done, s + 1)
                dve.scalar_tensor_tensor(plpc[:, g % 2, :], PC[:, :], bias("pc"), pl_t[:, g * GT:(g + 1) * GT],
                                         ALU.add, ALU.mult).then_inc(plpc_done, 1)

            def score_parts(s, t, g):
                dve.wait_ge(v_done, s + 1)
                dve.tensor_tensor(qk[:, :, :], V[:, :, D:D + QK],
                                  qkx[:, g * GB:(g + 1) * GB, bass.ds(t, 1), :].rearrange("p b t j -> p (b t) j"),
                                  ALU.add).then_inc(qk_done, 1)
                dve.wait_ge(qk_done, s + 1)
                dve.tensor_copy(parts[:, :, 0:QK], qk[:, :, :]).then_inc(hi_done, 1)
                dve.wait_ge(hi_done, s + 1)
                dve.tensor_tensor(res1[:, :, :], qk[:, :, :], parts[:, :, 0:QK], ALU.subtract).then_inc(res1_done, 1)
                dve.wait_ge(res1_done, s + 1)
                dve.tensor_copy(parts[:, :, QK:2 * QK], res1[:, :, :]).then_inc(mid_done, 1)
                dve.wait_ge(mid_done, s + 1)
                dve.tensor_tensor(parts[:, :, 2 * QK:3 * QK], res1[:, :, :], parts[:, :, QK:2 * QK], ALU.subtract)\
                    .then_inc(parts_done, 1)

            def v_out(s, g):
                dve.tensor_tensor(v_s[:, g % 2, :, :], V[:, :, 0:D], vx[:, g * GB:(g + 1) * GB, :], ALU.add)\
                    .then_inc(v_evac, 1)

            def score_operands(s):
                dve.wait_ge(sel_done, s + 1)
                dve.tensor_copy(sel_s[:, :], SEL).then_inc(sel_copied, 1)
                dve.wait_ge(sel_copied, s + 1)
                for i in range(TYPES):
                    dve.tensor_scalar(t_rhs[:, i, :], sel_s[:, :], C("kmask")[:, i:i + 1], C("qind")[:, i:i + 1],
                                      ALU.mult, ALU.add)
                for b in range(GB):
                    op = dve.tensor_scalar(t_lhs[:, b, :], sel_s[:, :], C("isq")[:, b:b + 1], C("isk")[:, b:b + 1],
                                           ALU.mult, ALU.add)
                op.then_inc(ops_done, 1)

            def softmax_top(s):
                for b in range(GB):
                    dve.wait_ge(t_done, s * GB + b + 1)
                    dve.tensor_reduce(logit[:, b, :], TB[b % 2][:, :, :].rearrange("p i m -> p m i"), AX_X, ALU.max)\
                        .then_inc(red_done, 1)
                dve.wait_ge(red_done, (s + 1) * GB)
                dve.tensor_reduce(neg_top[:, :], logit[:, :, :], AX_X, ALU.max, negate=True).then_inc(top_done, 1)
                dve.wait_ge(top_done, s + 1)
                dve.scalar_tensor_tensor(shift[:, :], neg_top[:, :], ALPHA, neg_top[:, :], ALU.mult, ALU.min)\
                    .then_inc(shift_done, 1)
                for h in range(2):
                    bs = slice(2 * h, 2 * h + 2)
                    dve.scalar_tensor_tensor(leaky[:, bs, :], logit[:, bs, :], ALPHA, logit[:, bs, :], ALU.mult, ALU.max)\
                        .then_inc(leaky_done, 1)

            def softmax_scale(s):
                dve.wait_ge(exp_done, (s + 1) * GB)
                dve.reciprocal(inv[:, :], total[:, :]).then_inc(inv_done, 1)
                dve.wait_ge(inv_done, s + 1)
                for b in range(GB):
                    op = dve.tensor_scalar(prob[:, b, :], expo[:, b, :], inv[:, b:b + 1], None, ALU.mult)
                op.then_inc(prob_done, 1)

            def context(s, t, g):
                dve.wait_ge(mu_done, s + 1)
                cols = slice(g * GT, (g + 1) * GT)
                if isinstance(t, int) and t == T_ITER - 1:
                    dve.tensor_scalar(ctx_t[:, cols], U[:, :], bias("mu"), None, ALU.add).then_inc(ctx_done, 1)
                else:
                    dve.scalar_tensor_tensor(ctx_t[:, cols], U[:, :], bias("mu"), mask_b[:, cols],
                                             ALU.add, ALU.mult).then_inc(ctx_done, 1)

            pl_times_pc(0, 0)
            score_parts(0, 0, 0)
            v_out(0, 0)
            pl_times_pc(1, 1)
            score_operands(0)
            softmax_top(0)
            softmax_scale(0)

            def step(t, g, front, ahead):
                s = t * G + g
                tn, n = after(t, g, 1)
                if front:
                    score_parts(s + 1, tn, n)
                    v_out(s + 1, n)
                if ahead:
                    pl_times_pc(s + 2, (g + 2) % G)
                if front:
                    score_operands(s + 1)
                    softmax_top(s + 1)
                context(s, t, g)
                if front:
                    softmax_scale(s + 1)
            rounds(dve, step)

            dve.wait_ge(ctx_done, G + STEPS)
            dve.tensor_copy(before_h[:, :], C("before")).then_inc(S("halves_ready"), 1)
            dve.tensor_copy(ones_h[:, :], C("ones")).then_inc(S("halves_ready"), 1)
            dve.memset(cs[:, :, :], 0.0).then_inc(S("cs_zero"), 1)

            def mask_heads(g, par, heads):
                dve.wait_ge(S("key_ready"), g + 1)
                for h in heads:
                    dve.tensor_scalar(k_m[par][:, h, :], k_s[:, :], C("hmask")[:, h:h + 1], None, ALU.mult)\
                        .then_inc(S("km_ready"), 1)

            def value_out(g, par):
                dve.wait_ge(S("value_mm"), g + 1)
                dve.wait_ge(S("va_ones"), 2)
                dst = v_a[:, par, :, 0:HEADS * VW].rearrange("p b (h c) -> p b h c", c=VW)
                for b in range(GB):
                    op = dve.tensor_tensor(dst[:, b, :, 0:HD],
                                           X1[:, b * N:(b + 1) * N].rearrange("p (h c) -> p h c", c=HD),
                                           R("iv").rearrange("p (h c) -> p h c", c=HD), ALU.add)
                op.then_inc(S("value_ready"), 1)

            def below_top(u, j):
                i = j % 2
                dve.wait_ge(S("scores_mm"), u + 1)
                dve.tensor_reduce(top[:, i, :], SB[i][:, :, :], AX_X, ALU.max).then_inc(S("top_ready"), 1)
                dve.wait_ge(S("top_ready"), u + 1)
                if not (isinstance(u, int) and u < 2):
                    dve.wait_ge(S("ex_ready"), u - 1)
                dve.tensor_tensor(dif[:, i, :, :], SB[i][:, :, :], top[:, i, :].unsqueeze(2).broadcast_to([128, 4, N]),
                                  ALU.subtract).then_inc(S("dif_ready"), 1)

            def sums_out(u, par, j):
                b, q = divmod(j, 4)
                dve.wait_ge(S("o_mm"), u + 1)
                dve.tensor_copy(o_a[:, par, b * HEADS + 4 * q:b * HEADS + 4 * q + 4, :], OB[j % 2][:, :, 0:VW])\
                    .then_inc(S("o_ready"), 1)

            def heads_out(p, par):
                dve.wait_ge(S("o_ready"), (p + 1) * UNITS)
                dve.reciprocal(rden[:, :], o_a[:, par, :, HD]).then_inc(S("rden_ready"), 1)
                dve.wait_ge(S("rden_ready"), p + 1)
                dve.tensor_tensor(o_n[:, :, :].rearrange("p b (h c) -> p (b h) c", c=HD), o_a[:, par, :, 0:HD],
                                  rden[:, :].unsqueeze(2).broadcast_to([128, GB * HEADS, HD]), ALU.mult)\
                    .then_inc(S("on_ready"), 1)

            def norm1(p):
                dve.wait_ge(S("h_mm"), p + 1)
                dve.tensor_tensor(h_s[:, :, :], X1.rearrange("p (b d) -> p b d", b=GB),
                                  R("bo").unsqueeze(1).broadcast_to([128, GB, D]), ALU.add).then_inc(S("h_ready"), 1)
                dve.wait_ge(S("h_ready"), p + 1)
                for b in range(GB):
                    dve.bn_stats(stats[:, b, :], h_s[:, b, :]).then_inc(S("stats_ready"), 1)
                dve.wait_ge(S("stats_ready"), (p + 1) * GB).then_inc(S("passed"), 1)
                for b in range(GB):
                    dve.bn_aggr(mv[:, b, :], stats[:, b, :]).then_inc(S("mv_ready"), 1)
                dve.wait_ge(S("mv_ready"), (p + 1) * GB)
                dve.tensor_scalar(ve[:, :], mv[:, :, 1], EPS, None, ALU.add).then_inc(S("var_ready"), 1)

            def norm1_out(p):
                dve.wait_ge(S("rstd_ready"), p + 1)
                for b in range(GB):
                    op = dve.tensor_scalar(xn[:, b, :], h_s[:, b, :], mv[:, b, 0:1], rstd[:, b:b + 1],
                                           ALU.subtract, ALU.mult)
                op.then_inc(S("xn_ready"), 1)

            CHAIN = 21
            count = [0]

            def link(p, ins, also=None):
                count[0] += 1
                ins.then_inc(S("route_chain"), 1)
                dve.wait_ge(S("route_chain"), p * CHAIN + count[0])

            def gates(p):
                count[0] = 0
                bc = lambda ap, n: ap.unsqueeze(2).broadcast_to([128, GB, n])
                dve.wait_ge(S("gate_mm"), p + 1)
                dve.tensor_tensor(lg[:, :, :], X1.rearrange("p (b d) -> p b d", b=GB)[:, :, 0:12],
                                  R("gate").unsqueeze(1).broadcast_to([128, GB, 12]), ALU.add).then_inc(S("lg_ready"), 1)
                dve.wait_ge(S("lg_ready"), p + 1)
                link(p, dve.tensor_reduce(gm[:, :], lg[:, :, 0:4], AX_X, ALU.max))
                link(p, dve.tensor_tensor(dg[:, :, :], lg[:, :, 0:4], bc(gm[:, :], 4), ALU.subtract))
                dve.tensor_scalar(sc[:, :, :], dg[:, :, :], 0.0, None, ALU.is_equal).then_inc(S("dg_ready"), 1)
                dve.wait_ge(S("dg_ready"), p + 1)
                link(p, dve.tensor_tensor(sc[:, :, :], sc[:, :, :], C("pref").unsqueeze(1).broadcast_to([128, GB, 4]), ALU.mult))
                link(p, dve.tensor_reduce(sm[:, :], sc[:, :, :], AX_X, ALU.max))
                link(p, dve.tensor_tensor(oh[:, :, :], sc[:, :, :], bc(sm[:, :], 4), ALU.is_equal))
                link(p, dve.tensor_tensor(pr[:, :, :, :], lg[:, :, 4:12].rearrange("p b (g k) -> p b g k", k=2),
                                          oh[:, :, :].unsqueeze(3).broadcast_to([128, GB, 4, 2]), ALU.mult))
                link(p, dve.tensor_reduce(el[:, :, :], pr[:, :, :, :].rearrange("p b g k -> p b k g"), AX_X, ALU.add))
                link(p, dve.tensor_tensor(de[:, :], el[:, :, 1], el[:, :, 0], ALU.subtract))
                dve.scalar_tensor_tensor(nd[:, :], de[:, :], -1.0, de[:, :], ALU.mult, ALU.min).then_inc(S("nd_ready"), 1)
                link(p, dve.tensor_scalar(k1[:, :], de[:, :], 0.0, None, ALU.is_gt))
                link(p, dve.scalar_tensor_tensor(ev[:, :], sm[:, :], -2.0, k1[:, :], ALU.mult, ALU.add))
                link(p, dve.tensor_tensor(OH[:, :, :], C("iota").unsqueeze(1).broadcast_to([128, GB, EXPERTS]),
                                          bc(ev[:, :], EXPERTS), ALU.is_equal))
                dve.tensor_copy(oh_h[:, :, :], OH[:, :, :]).then_inc(S("ohh_ready"), 1)
                dve.wait_ge(S("ohh_ready"), p + 1)
                link(p, dve.tensor_copy(cs[:, 0, :], cs[:, GB, :]))
                for b in range(GB):
                    link(p, dve.tensor_tensor(cs[:, b + 1, :], cs[:, b, :], OH[:, b, :], ALU.add))
                dve.tensor_copy(cs_h[:, :, :], cs[:, 0:GB, :]).then_inc(S("cs_ready"), 1)
                dve.wait_ge(S("cs_ready"), p + 1)
                dve.wait_ge(S("gate_exps"), 2 * (p + 1))
                link(p, dve.tensor_reduce(gs[:, :], eg[:, :, :], AX_X, ALU.add))
                link(p, dve.scalar_tensor_tensor(den[:, :], ee[:, :], 1.0, gs[:, :], ALU.add, ALU.mult))
                dve.wait_ge(S("in_rows"), 16 * (p + 1))
                link(p, dve.reciprocal(rows[:, :, 2 * D], den[:, :]))

            def slots_out(p):
                dve.wait_ge(S("rank_mm"), p + 1)
                dve.tensor_tensor(rk[:, :, :], X0[:, 0:GB * EXPERTS].rearrange("p (b e) -> p b e", b=GB),
                                  C("base").unsqueeze(1).broadcast_to([128, GB, EXPERTS]), ALU.add).then_inc(S("rank_read"), 1)
                dve.wait_ge(S("rank_read"), p + 1)
                link(p, dve.tensor_tensor(rk2[:, :, :], rk[:, :, :], OH[:, :, :], ALU.mult))
                link(p, dve.tensor_reduce(slot[:, :], rk2[:, :, :], AX_X, ALU.add))
                dve.tensor_copy(slot_i[:, :], slot[:, :]).then_inc(S("slot_ready"), 1)
                assert count[0] == CHAIN, count[0]

            dve.wait_ge(S("cs_zero"), 1)
            dve.wait_ge(S("halves_ready"), 2)
            mask_heads(0, 0, range(HEADS))
            value_out(0, 0)
            below_top(0, 0)
            below_top(1, 1)

            def body(g, par, prev, nxt):
                for j in range(UNITS):
                    u = g * UNITS + j
                    if j + 2 < UNITS or nxt:
                        below_top(u + 2, j)
                    if j:
                        sums_out(u - 1, par, j - 1)
                    elif prev:
                        sums_out(u - 1, 1 - par, UNITS - 1)
                    if prev and j == 0:
                        heads_out(g - 1, 1 - par)
                    if prev and j == 5:
                        norm1(g - 1)
                    if prev and j == 7:
                        norm1_out(g - 1)
                    if nxt and j == 9:
                        value_out(g + 1, 1 - par)
                    if nxt and 8 <= j < 16:
                        mask_heads(g + 1, 1 - par, range(2 * (j - 8), 2 * (j - 8) + 2))
                    if prev and j == 13:
                        gates(g - 1)
                    if prev and j == 15:
                        slots_out(g - 1)
            groups(dve, body)
            sums_out(G * UNITS - 1, 1, UNITS - 1)
            heads_out(G - 1, 1)
            norm1(G - 1)
            norm1_out(G - 1)
            gates(G - 1)
            dve.tensor_copy(cnt_h[:, :], cs[:, GB, :]).then_inc(S("cnt_h_ready"), 1)
            slots_out(G - 1)

            done = [0]

            def then(ins):
                done[0] += 1
                ins.then_inc(S("table_chain"), 1)
                dve.wait_ge(S("table_chain"), done[0])
            row8 = lambda ap, n: ap.unsqueeze(1).broadcast_to([128, n, EXPERTS])
            dve.wait_ge(S("cnt_mm"), 1)
            then(dve.tensor_copy(cnt[:, :], X1[:, 0:EXPERTS]))
            then(dve.tensor_tensor(full[:, :, :], C("start").unsqueeze(1).broadcast_to([128, EXPERTS, 32]),
                                   cnt[:, :].unsqueeze(2).broadcast_to([128, EXPERTS, 32]), ALU.is_lt))
            then(dve.tensor_reduce(nt[:, :], full[:, :, :], AX_X, ALU.add))
            then(dve.tensor_tensor(ntu[:, :, :], C("upto").rearrange("p (a b) -> p a b", a=EXPERTS),
                                   row8(nt[:, :], EXPERTS), ALU.mult))
            then(dve.tensor_reduce(cum[:, :], ntu[:, :, :], AX_X, ALU.add))
            then(dve.tensor_scalar(hop[:, :], nt[:, :], float(-N), float(REGION), ALU.mult, ALU.add))
            then(dve.tensor_tensor(behind[:, :, :], C("tile").unsqueeze(2).broadcast_to([128, SLOTS, EXPERTS]),
                                   row8(cum[:, :], SLOTS), ALU.is_ge))
            then(dve.tensor_reduce(t_exp[:, :], behind[:, :, :], AX_X, ALU.add))
            then(dve.tensor_tensor(hops[:, :, :], behind[:, :, :], row8(hop[:, :], SLOTS), ALU.mult))
            then(dve.tensor_reduce(t_hop[:, :], hops[:, :, :], AX_X, ALU.add))
            then(dve.scalar_tensor_tensor(t_row[:, :], C("tile"), float(N), t_hop[:, :], ALU.mult, ALU.add))
            then(dve.tensor_tensor(pad_at[:, :], cnt[:, :], C("base"), ALU.add))
            dve.tensor_scalar(row_i[:, 0:SLOTS], t_row[:, :], float(DUMMY), None, ALU.min).then_inc(S("table_ready"), 1)
            dve.tensor_scalar(exp_i[:, 0:SLOTS], t_exp[:, :], float(EXPERTS - 1), None, ALU.min).then_inc(S("table_ready"), 1)
            dve.tensor_copy(pad_i[:, :], pad_at[:, :]).then_inc(S("table_ready"), 1)
            dve.memset(eps_s[:, :], EPS).then_inc(S("eps_ready"), 1)
            dve.wait_ge(S("table_ready"), 3)
            dve.wait_ge(S("in_experts"), 64)

            def slot_of(k, r):
                i = r % 2
                static = isinstance(k, int)
                if not (static and (k < 1 or k - 1 >= SLOTS)):
                    q = 1 - i
                    e = dve.value_load(exp_i[0:1, bass.ds(k - 1, 1)], min_val=0, max_val=EXPERTS - 1)
                    dve.wait_ge(S("hb_mm"), k)
                    dve.tensor_tensor(hb_s[:, q, :], HB[q], b1_s[:, bass.ds(e * FF, FF)], ALU.add).then_inc(S("hb_ready"), 1)
                if not (static and (k < LAST)):
                    t = k - LAST
                    q, rr = i, (r - LAST) % RING
                    dve.wait_ge(S("sd_ready"), t + 1)
                    dve.reciprocal(rs2[:, q:q + 1], sd2[:, q:q + 1]).then_inc(S("norm2_chain"), 1)
                    dve.wait_ge(S("norm2_chain"), 3 * t + 1)
                    dve.tensor_scalar(xn2[:, q, :], res[:, q, :], mv2[:, q, 0:1], rs2[:, q:q + 1],
                                      ALU.subtract, ALU.mult).then_inc(S("norm2_chain"), 1)
                    dve.wait_ge(S("norm2_chain"), 3 * t + 2)
                    dve.tensor_tensor(xg2[:, q, :], xn2[:, q, :], R("ln2g"), ALU.mult).then_inc(S("norm2_chain"), 1)
                    dve.wait_ge(S("norm2_chain"), 3 * t + 3)
                    dve.wait_ge(S("xb_ready"), t + 1)
                    if not (static and t < 2):
                        dve.wait_ge(S(f"sent{(rr - 2) % RING}"), tile_turn(t - 2, (rr - 2) % RING))
                    dve.tensor_tensor(fin[:, q, :], xg2[:, q, :], xb2[:, q, :], ALU.add).then_inc(S("fin_ready"), 1)
                if not (static and (k < 3 or k - 3 >= SLOTS)):
                    t = k - 3
                    q, rr = 1 - i, (r - 3) % RING
                    e = dve.value_load(exp_i[0:1, bass.ds(t, 1)], min_val=0, max_val=EXPERTS - 1)
                    dve.wait_ge(S("y_mm"), t + 1)
                    dve.tensor_tensor(yb[:, q, :], YB[q], b2_s[:, bass.ds(e * D, D)], ALU.add).then_inc(S("yb_ready"), 1)
                    dve.wait_ge(S("yb_ready"), t + 1)
                    dve.scalar_tensor_tensor(res[:, q, :], yb[:, q, :], tile_s[:, rr, 2 * D:2 * D + 1],
                                             tile_s[:, rr, 0:D], ALU.mult, ALU.add).then_inc(S("res_chain"), 1)
                    dve.wait_ge(S("res_chain"), 2 * t + 1)
                    dve.bn_stats(st2[:, q, :], res[:, q, :]).then_inc(S("res_chain"), 1)
                    dve.wait_ge(S("res_chain"), 2 * t + 2).then_inc(S("passed"), 1)
                    dve.bn_aggr(mv2[:, q, :], st2[:, q, :]).then_inc(S("mv2_ready"), 1)
            tiles(dve, slot_of)

        @block.scalar
        def _(act):
            act.wait_ge(zneg_done, 1)
            act.activation(elu_e[:, :], elu_n[:, :], ACT.Exp).then_inc(zexp_done, 1)
            act.wait_ge(in_w, 16)
            act.wait_ge(cmd_mm, 1)
            for t in range(T_ITER):
                act.activation(cmd[:, t, :], M[:, t, 0:B], ACT.Identity, bias=bias(f"qt{t}")).then_inc(cmd_ready, 1)
            act.wait_ge(ck_mm, 1)
            act.activation(ck[:, :], PT[:, 0, :], ACT.Identity, bias=bias("pk")).then_inc(ck_ready, 1)
            act.wait_ge(cv_mm, 1)
            act.activation(cv[:, :, :].rearrange("p t b -> p (t b)"), U[:, 0:N], ACT.Identity, bias=bias("pv"))\
                .then_inc(cv_ready, 1)
            for c, bk in enumerate((T0, T1, M)):
                act.wait_ge(fold_mm, c + 1)
                act.activation(key_fold[:, c, :, :, :].rearrange("p t b i -> p (t b i)"),
                               bk[:, :, :].rearrange("p a n -> p (a n)"), ACT.Copy)\
                    .then_inc(fold_ready if c < 2 else msg_evac, 1)
            act.wait_ge(qfold_mm, 1)
            act.activation(query_fold[:, :, :].rearrange("p c i -> p (c i)"), U[:, 0:3 * TYPES], ACT.Copy)\
                .then_inc(qfold_ready, 1)
            for g in range(G):
                act.wait_ge(pl_mm, g + 1)
                act.activation(pl_t[:, g * GT:(g + 1) * GT], TB[g % 2][:, :, :].rearrange("p a n -> p (a n)"),
                               ACT.Identity, bias=bias("pl")).then_inc(pl_done, 1)

            def probabilities_out(s):
                act.wait_ge(pt_done, s + 1)
                act.activation(prob_t[:, :, :], PT[:, :, :], ACT.Copy).then_inc(pt_evac, 1)

            def message_out(s, t, g):
                act.wait_ge(msg_done, s + 1)
                for b in range(GB):
                    scale = cv[:, bass.ds(t, 1), g * GB + b:g * GB + b + 1].rearrange("p t b -> p (t b)")
                    op = act.activation(msg_s[:, b * N:(b + 1) * N], M[:, b, :], ACT.Copy, scale=scale)
                op.then_inc(msg_evac, 1)

            def exps(s):
                act.wait_ge(shift_done, s + 1)
                for b in range(GB):
                    act.wait_ge(leaky_done, 2 * s + b // 2 + 1)
                    act.activation(expo[:, b, :], leaky[:, b, :], ACT.Exp, bias=shift[:, b:b + 1],
                                   accum_out=total[:, b:b + 1]).then_inc(exp_done, 1)

            act.wait_ge(cv_ready, 1)
            exps(0)

            def step(t, g, front, ahead):
                s = t * G + g
                probabilities_out(s)
                message_out(s, t, g)
                if front:
                    exps(s + 1)
            rounds(act, step)

            act.wait_ge(ctx_done, G + STEPS)

            def cond_out(g, par):
                act.wait_ge(S("cond_mm"), g + 1)
                act.activation(xc_s[:, par, :], X0, ACT.Identity, bias=bias("cb")).then_inc(S("cond_ready"), 1)

            def query_out(g, par):
                act.wait_ge(S("query_mm"), g + 1)
                act.activation(q_s[:, par, :], X1, ACT.Identity, bias=bias("iq")).then_inc(S("query_ready"), 1)

            def key_out(g, par):
                act.wait_ge(S("key_mm"), g + 1)
                act.activation(k_s[:, :], X0, ACT.Identity, bias=bias("ik")).then_inc(S("key_ready"), 1)

            def exponentials(u, j):
                i = j % 2
                act.wait_ge(S("dif_ready"), u + 1)
                if not (isinstance(u, int) and u < 2):
                    act.wait_ge(S("ext_mm"), u - 1)
                act.activation(ex[:, i, :, :], dif[:, i, :, :], ACT.Exp, scale=float(HD) ** -0.5)\
                    .then_inc(S("ex_ready"), 1)

            def turned_out(u, j):
                i = j % 2
                act.wait_ge(S("ext_mm"), u + 1)
                if not (isinstance(u, int) and u < 2):
                    act.wait_ge(S("o_mm"), u - 1)
                act.activation(ex_t[:, i, :, :], PB[i][:, :, :], ACT.Copy).then_inc(S("ext_ready"), 1)

            def heads_turned(p):
                act.wait_ge(S("ot_mm"), p + 1)
                act.activation(o_t[:, :], X0, ACT.Copy).then_inc(S("ot_ready"), 1)

            def norm1_turned(p):
                act.wait_ge(S("x1t_mm"), p + 1)
                act.activation(x1_t[:, :], X0, ACT.Identity, scale=bias("ln1g"), bias=bias("ln1b"))\
                    .then_inc(S("x1t_ready"), 1)

            def gate_exps(p):
                act.wait_ge(S("dg_ready"), p + 1)
                act.activation(eg[:, :, :], dg[:, :, :], ACT.Exp).then_inc(S("gate_exps"), 1)
                act.wait_ge(S("nd_ready"), p + 1)
                act.activation(ee[:, :], nd[:, :], ACT.Exp).then_inc(S("gate_exps"), 1)

            cond_out(0, 0)
            query_out(0, 0)
            key_out(0, 0)
            exponentials(0, 0)
            exponentials(1, 1)

            def body(g, par, prev, nxt):
                for j in range(UNITS):
                    u = g * UNITS + j
                    turned_out(u, j)
                    if j + 2 < UNITS or nxt:
                        exponentials(u + 2, j)
                    if prev and j == 3:
                        heads_turned(g - 1)
                    if nxt and j == 6:
                        cond_out(g + 1, 1 - par)
                    if nxt and j == 7:
                        query_out(g + 1, 1 - par)
                    if nxt and j == 8:
                        key_out(g + 1, 1 - par)
                    if prev and j == 10:
                        norm1_turned(g - 1)
                    if prev and j == 13:
                        gate_exps(g - 1)
            groups(act, body)
            heads_turned(G - 1)
            norm1_turned(G - 1)
            gate_exps(G - 1)

            act.wait_ge(S("eps_ready"), 1)

            def slot_of(k, r):
                i = r % 2
                static = isinstance(k, int)
                if not (static and (k < 3 or k - 3 >= SLOTS)):
                    q = 1 - i
                    act.wait_ge(S("mv2_ready"), k - 2)
                    act.activation(sd2[:, q:q + 1], mv2[:, q, 1:2], ACT.Sqrt, bias=eps_s[:, :]).then_inc(S("sd_ready"), 1)
                if not (static and (k < 2 or k - 2 >= SLOTS)):
                    act.wait_ge(S("ht_mm"), k - 1)
                    act.activation(ht_s[:, i, :], HT[i], ACT.Relu).then_inc(S("ht_ready"), 1)
                if not (static and k >= SLOTS):
                    act.wait_ge(S("xt_mm"), k + 1)
                    act.activation(xt_s[:, i, :], XT[i], ACT.Copy).then_inc(S("xt_ready"), 1)
            tiles(act, slot_of)


def kernel(**inputs):
    import concourse.bacc as bacc
    from concourse.bass_utils import run_bass_kernel_spmd
    a = {k: np.asarray(v) for k, v in inputs.items()}
    nc = bacc.Bacc("TRN2", target_bir_lowering=False, num_devices=1)
    arrays = layouts(a)
    aps = {n: nc.dram_tensor(n, v.shape, mybir.dt.from_np(v.dtype), kind="ExternalInput").ap()
           for n, v in arrays.items()}
    aps["out"] = nc.dram_tensor("out", (TOK, D), F32, kind="ExternalOutput").ap()
    build(nc, **aps)
    r = run_bass_kernel_spmd(nc, [arrays], core_ids=[0])
    return r.results[0]["out"].reshape(B, N, D)


def layouts(a):
    c = {k[8:]: v for k, v in a.items() if k.startswith("L0_cond_")}
    f = {k[7:]: v for k, v in a.items() if k.startswith("L0_ffn_")}
    qt, bqt, wes = a["fside_BxSxS_0"], a["mask_BxS_ff0"], a["cond_2048"]

    def chunks(m):
        return m.reshape(m.shape[0], -1, 128).transpose(2, 1, 0).reshape(128, -1)
    cols = np.zeros((128, 24), np.float32)
    for n, v in (("qin", c["b_qin"]), ("pl", c["b_pl"]), ("pc", c["b_pc"]), ("q", c["b_q"]), ("k", c["b_k"]),
                 ("mu", c["b_mu"]), ("cb", c["b_cb"]), ("pk", c["b_pk"]), ("pv", c["b_pv"]), ("qt0", bqt[0]),
                 ("qt1", bqt[1]), ("qt2", bqt[2]), ("qt3", bqt[3]), ("init", c["init_mem"][0]),
                 ("iq", f["in_proj_b"][:D]), ("ik", f["in_proj_b"][D:2 * D]), ("ln1g", f["ln1_g"]),
                 ("ln1b", f["ln1_b"])):
        cols[:, BIAS[n]] = v
    gates = np.zeros((128, D), np.float32)
    gates[:, 0:GROUPS_E] = f["w_group"]
    gates[:, GROUPS_E:GROUPS_E + EXPERTS] = f["w_expert"].transpose(1, 0, 2).reshape(D, EXPERTS)
    pieces = {"qin": c["w_qin"].T, "pk": c["w_pk"].T, "pv": c["w_pv"].T,
              "qt": qt[:T_ITER].transpose(2, 0, 1).reshape(128, -1), "wq": c["w_q"], "wk": c["w_k"],
              "fside": a["fside_BxS_0"].T, "w1t": wes[:TYPES, :D].T, "w2t": wes[:TYPES, D:].T,
              "pl": c["w_pl"].T, "pc": c["w_pc"].T, "v": chunks(c["w_v"]), "mu": chunks(c["w_mu"]),
              "cb": chunks(c["w_cb"]), "wi": f["in_proj_w"].T, "wo": f["out_proj_w"].T, "gate": gates, "bias": cols}
    rowvecs = np.concatenate([c["b_v"], f["in_proj_b"][2 * D:], f["out_proj_b"], f["ln1_g"], f["ln1_b"], f["ln2_g"],
                              f["ln2_b"], f["b_group"], f["b_expert"].reshape(-1)]).reshape(1, NR)
    return {"xT": np.ascontiguousarray(a["x"].transpose(2, 0, 1).reshape(128, TOK)),
            "adj": np.ascontiguousarray(a["itok_BxSxS_0_4"].transpose(1, 0, 2).reshape(128, TOK)),
            "mask": np.ascontiguousarray(a["mask_BxS_ff1"].reshape(1, TOK)),
            "weights": np.ascontiguousarray(np.concatenate([pieces[n] for n in WCOLS], axis=1)),
            "rowvecs": rowvecs, "consts": shape_constants(),
            "ids": (np.arange(B)[None, :] * N + np.arange(N)[:, None]).astype(np.int32),
            "x": np.ascontiguousarray(a["x"]),
            "w1": np.ascontiguousarray(f["w1"].transpose(1, 0, 2).reshape(128, EXPERTS * FF)),
            "w2": np.ascontiguousarray(f["w2"].reshape(EXPERTS, 2, 128, D).transpose(2, 0, 1, 3).reshape(128, -1)),
            "b1": np.ascontiguousarray(f["b1"].reshape(1, EXPERTS * FF)),
            "b2": np.ascontiguousarray(f["b2"].reshape(1, EXPERTS * D))}
```

```python
from contextlib import ExitStack

import numpy as np
import concourse.bass as bass
from concourse import mybir

F32 = mybir.dt.float32
BF16 = mybir.dt.bfloat16
I32 = mybir.dt.int32
ALU = mybir.AluOpType
ACT = mybir.ActivationFunctionType
AX_X = mybir.AxisListType.X

B, N, D = 32, 128, 128
TOK = B * N
GB = 4
G = B // GB
GT = GB * N
T_ITER = 4
TYPES = 4
ALPHA = 0.2
BIG = float(2.0 ** 53)
NPART = 3
QK = 2 * TYPES

WCOLS = {}


def _columns():
    at = 0
    for name, n in (("qin", D), ("pk", D), ("pv", D), ("qt", T_ITER * D), ("wq", 3 * D), ("wk", 3 * D),
                    ("fside", B), ("w1t", TYPES), ("w2t", TYPES), ("pl", D), ("pc", D), ("v", 3 * D),
                    ("mu", 2 * D), ("cb", 2 * D), ("wi", 3 * D), ("wo", D), ("gate", D),
                    ("bias", 24)):
        WCOLS[name] = (at, at + n)
        at += n
    return at


NW = _columns()
BIAS = {n: i for i, n in enumerate(("qin", "pl", "pc", "q", "k", "mu", "cb", "pk", "pv", "qt0", "qt1", "qt2",
                                    "qt3", "init", "iq", "ik", "ln1g", "ln1b"))}
RCOLS = {"bv": (0, 128), "iv": (128, 256), "bo": (256, 384), "ln1g": (384, 512), "ln1b": (512, 640),
         "ln2g": (640, 768), "ln2b": (768, 896), "gate": (896, 908)}
NR = 908
HEADS = 16
HD = D // HEADS
VW = HD + 1
VWIN = 64
VROW = 208
EXPERTS, FF = 8, 256
GROUPS_E = 4
REGION = TOK + N
ROW = 260
TILES = TOK // N + EXPERTS - 1
SLOTS = TILES + 1
RING = 8
DUMMY = EXPERTS * REGION
W1ROW = FF + FF // 128
FAR = 1 << 20
EPS = 1e-5
CCOLS = {"ident": (0, 128), "ones": (128, 256), "kmask": (256, 260), "qind": (260, 264), "isq": (264, 268),
         "isk": (268, 272), "hmask": (272, 288), "pref": (288, 292), "iota": (292, 300), "base": (300, 308),
         "half": (308, 312), "before": (312, 440), "start": (440, 472), "upto": (472, 536), "tile": (536, 576),
         "regionT": (576, 584)}
NC = 584


WORK = 15700


def shape_constants():
    c = np.zeros((128, NC), np.float32)
    c[:, 0:128] = np.eye(128)
    c[:, 128:256] = 1.0
    for row in range(128):
        b, r = divmod(row, 32)
        part, j = divmod(r, QK)
        if part >= NPART:
            continue
        if j < TYPES:
            c[row, 260 + j] = 1.0
            c[row, 264 + b] = 1.0
        else:
            c[row, 256 + j - TYPES] = 1.0
            c[row, 268 + b] = 1.0
    for p in range(128):
        c[p, 272 + p // HD] = 1.0
    c[:, 288:292] = np.arange(GROUPS_E, 0, -1)
    c[:, 292:300] = np.arange(EXPERTS) - EXPERTS
    c[:, 300:308] = np.arange(EXPERTS) * REGION
    c[:, 308:312] = -0.5
    c[:, 312:440] = np.triu(np.ones((128, 128)), 1)
    c[:, 440:472] = np.arange(32) * N
    c[:, 472:536] = np.tril(np.ones((8, 8))).reshape(-1)
    c[:, 536:576] = np.arange(40)
    c[:, 576:584] = REGION
    return c


def build(nc, x, xT, adj, mask, weights, rowvecs, consts, ids, w1, w2, b2, out):
    sorted_rows = nc.dram_tensor("sorted_rows", (DUMMY + N, ROW), F32, kind="Internal").ap()
    with ExitStack() as ctx:
        def sb(name, shape, dt=F32):
            return ctx.enter_context(nc.sbuf_tensor(name, shape, dt))

        def sem(name):
            return ctx.enter_context(nc.semaphore(name))

        x_t = sb("x_t", [128, TOK])
        ctx_t = sb("ctx_t", [128, TOK])
        w = sb("w", [128, NW])
        cst = sb("cst", [128, NC])
        rowv = sb("rowv", [128, NR])
        ident_h = sb("ident_h", [128, 128], BF16)
        room_p = sb("room_p", [128, 2 * TOK])
        room_v = sb("room_v", [128, 2 * TOK])
        room_w = sb("room_w", [128, WORK])
        penalty = room_p[:, :].bitcast(BF16).rearrange("p (b i m) -> p b i m", b=B, i=TYPES)
        pl_t = room_v[:, 0:TOK]
        adj_s = room_v[:, TOK:2 * TOK].bitcast(I32)
        vx = room_v[:, TOK:2 * TOK].rearrange("p (b d) -> p b d", b=B)
        k_m = [room_p[:, :].rearrange("p (h n) -> p h n", h=HEADS),
               room_v[:, :].rearrange("p (h n) -> p h n", h=HEADS)]
        used = {"a": 0, "b": 0, "c": 0}
        rooms = {"a": (room_w, WORK), "b": (room_w, WORK), "c": (room_p, 2 * TOK)}

        def carve(phase, shape, dt=F32):
            n = int(np.prod(shape[1:]))
            words = n if dt != BF16 else n // 2
            room, size = rooms[phase]
            ap = room[:, used[phase]:used[phase] + words]
            used[phase] += words
            assert used[phase] <= size, (phase, used[phase])
            if dt != F32:
                ap = ap.bitcast(dt)
            names = "abcde"[:len(shape) - 1]
            return ap.rearrange(f"p ({' '.join(names)}) -> p {' '.join(names)}", **dict(zip(names, shape[1:])))

        def A(*shape, dt=F32):
            return carve("a", shape, dt)

        def Bf(*shape, dt=F32):
            return carve("b", shape, dt)

        def Cf(*shape, dt=F32):
            return carve("c", shape, dt)

        mask_b = A(128, TOK)
        qkx = A(128, B, T_ITER, QK)
        w_v = A(128, 2, GB, 2, D + QK)
        ck_w2 = A(128, T_ITER * B, TYPES)
        bk_w2 = A(128, T_ITER * B * TYPES)
        key_fold = A(128, 3, T_ITER, B, TYPES)
        kbias = A(128, T_ITER, B, TYPES)
        shared = used["a"]
        w_x = A(128, B, D + TYPES + T_ITER * TYPES)
        used["a"] = shared
        plpc = A(128, 2, GT)
        v_s = A(128, 2, GB, D)
        logit = A(128, GB, N)
        leaky = A(128, GB, N)
        expo = A(128, GB, N)
        prob = A(128, GB, N)
        prob_t = A(128, GB, N)
        msg_s = A(128, GT)
        t_rhs = sb("t_rhs", [128, TYPES, N], BF16)
        t_lhs = sb("t_lhs", [128, GB, N], BF16)
        q_base = sb("q_base", [128, B])
        elu_z = sb("elu_z", [128, B])
        elu_n = sb("elu_n", [128, B])
        elu_e = sb("elu_e", [128, B])
        elu_s = sb("elu_s", [128, B])
        cmd = sb("cmd", [128, T_ITER, B])
        ck = sb("ck", [128, T_ITER * B])
        cv = sb("cv", [128, T_ITER, B])
        bq_w1 = sb("bq_w1", [128, TYPES])
        query_fold = sb("query_fold", [128, 3, TYPES])
        qbias = sb("qbias", [128, TYPES])
        qk = sb("qk", [128, GB, QK])
        res1 = sb("res1", [128, GB, QK])
        parts = sb("parts", [128, GB, 32], BF16)
        sel_s = sb("sel_s", [128, N], BF16)
        neg_top = sb("neg_top", [128, GB])
        shift = sb("shift", [128, GB])
        total = sb("total", [128, GB])
        inv = sb("inv", [128, GB])
        xc_s = Bf(128, 2, GT)
        q_s = Bf(128, 2, GT)
        k_s = Bf(128, GT)
        v_a = Bf(128, 2, GB, VROW)
        ex = Bf(128, 2, 4, N)
        ex_t = Bf(128, 2, 4, N)
        o_a = Bf(128, 2, GB * HEADS, VW)
        o_n = Bf(128, GB, D)
        o_t = Bf(128, GT)
        h_s = Bf(128, GB, D)
        xn = Bf(128, GB, D)
        x1_t = Bf(128, GT)
        x1_g = Bf(128, GB, D)
        rows = Bf(128, GB, ROW)
        pad_row = Bf(128, ROW)
        neg_head = sb("neg_head", [128, 2, 4])
        iq_s = sb("iq_s", [128, 1])
        rden = sb("rden", [128, GB * HEADS])
        stats = sb("stats", [128, GB, 6])
        mv = sb("mv", [128, GB, 2])
        ve = sb("ve", [128, GB])
        rstd = sb("rstd", [128, GB])
        id_s = sb("id_s", [128, B], I32)
        lg = sb("lg", [128, GB, 12])
        gm = sb("gm", [128, GB])
        dg = sb("dg", [128, GB, 4])
        eg = sb("eg", [128, GB, 4])
        pick = sb("pick", [128, GB, 4])
        sm = sb("sm", [128, GB])
        oh = sb("oh", [128, GB, 4])
        pr = sb("pr", [128, GB, 4, 2])
        el = sb("el", [128, GB, 2])
        de = sb("de", [128, GB])
        nd = sb("nd", [128, GB])
        ee = sb("ee", [128, GB])
        gs = sb("gs", [128, GB])
        den = sb("den", [128, GB])
        m2s = sb("m2s", [128, GB])
        ev = sb("ev", [128, GB])
        oh_h = sb("oh_h", [128, GB, EXPERTS], BF16)
        csum = sb("csum", [128, EXPERTS])
        cs = sb("cs", [128, EXPERTS])
        cs_h = sb("cs_h", [128, EXPERTS], BF16)
        rk = sb("rk", [128, GB, EXPERTS])
        rk2 = sb("rk2", [128, GB, EXPERTS])
        slot = sb("slot", [128, GB])
        slot_i = sb("slot_i", [128, GB], I32)
        cnt = sb("cnt", [128, EXPERTS])
        full = Cf(128, EXPERTS, 32)
        nt = sb("nt", [128, EXPERTS])
        ntu = Cf(128, EXPERTS, EXPERTS)
        cum = sb("cum", [128, EXPERTS])
        hop = sb("hop", [128, EXPERTS])
        behind = Cf(128, SLOTS, EXPERTS)
        hops = Cf(128, SLOTS, EXPERTS)
        t_exp = sb("t_exp", [128, SLOTS])
        t_hop = sb("t_hop", [128, SLOTS])
        t_row = sb("t_row", [128, SLOTS])
        pad_at = sb("pad_at", [128, EXPERTS])
        row_i = sb("row_i", [128, SLOTS], I32)
        exp_i = sb("exp_i", [128, SLOTS], I32)
        pad_i = sb("pad_i", [128, EXPERTS], I32)
        w1_s, w2_s = x_t[:, 0:EXPERTS * W1ROW], ctx_t[:, 0:EXPERTS * FF]
        b2_s = ctx_t[:, EXPERTS * FF:EXPERTS * (FF + D)]
        tile_s = Cf(128, RING, ROW)
        xt_s = Cf(128, 2, D)
        w1_r = Cf(128, 4, W1ROW)
        ht_s = Cf(128, 2, FF)
        id_r = sb("id_r", [128, RING], I32)
        yb = Cf(128, 2, D)
        res = Cf(128, 4, D)
        xn2 = Cf(128, 2, D)
        xg2 = Cf(128, 2, D)
        xb2 = Cf(128, 4, D)
        fin = Cf(128, 4, D)
        st2 = sb("st2", [128, 2, 6])
        mv2 = sb("mv2", [128, 4, 2])
        sd2 = sb("sd2", [128, 4])
        rs2 = sb("rs2", [128, 4])
        eps_s = sb("eps_s", [128, 1])
        before_h = sb("before_h", [128, 128], BF16)
        ones_h = sb("ones_h", [128, 128], BF16)

        def W(name, c=0, n=D):
            a = WCOLS[name][0] + c * D
            return w[:, a:a + n]

        def bias(name):
            a = WCOLS["bias"][0] + BIAS[name]
            return w[:, a:a + 1]

        def C(name):
            a, b = CCOLS[name]
            return cst[:, a:b]

        def R(name):
            a, b = RCOLS[name]
            return rowv[:, a:b]

        def bank(name, shape, dt=F32):
            return ctx.enter_context(nc.psum_tensor(name, shape, dt))
        PC = bank("PC", [128, GT])
        V = bank("V", [128, GB, 256])
        T0 = bank("T0", [128, TYPES, N])
        T1 = bank("T1", [128, TYPES, N])
        PT = bank("PT", [128, GB, N])
        M = bank("M", [128, GB, N])
        U = bank("U", [128, GT])
        TB = [T0, T1]
        SEL = PT[:, 0, 0:N // 2].bitcast(BF16)
        SB = [T0, T1]
        PB = [PT, M]
        OB = [PC[:, :].rearrange("p (h d) -> p h d", h=4), U[:, :].rearrange("p (h d) -> p h d", h=4)]
        X0 = V[:, 0:2, :].rearrange("p a c -> p (a c)")
        X1 = V[:, 2:4, :].rearrange("p a c -> p (a c)")
        XT = [T0[:, 0, :], T1[:, 0, :]]
        HT = [PC[:, 0:FF], U[:, 0:FF]]
        YB = [X0[:, 0:D], X1[:, 0:D]]

        in_w, in_x, in_adj, in_mask, in_c, in_bv = (sem(n) for n in (
            "in_w", "in_x", "in_adj", "in_mask", "in_c", "in_bv"))
        (zq_mm, zq_done, zneg_done, zexp_done, zsum_done, qbase_ready, cmd_mm, cmd_ready, ck_mm, cv_mm, ck_ready,
         cv_ready, ckw2_ready, bkw2_ready, bqw1_ready, fold_mm, fold_ready, qfold_mm, qfold_ready, kbias_mm,
         kbias_ready, qbias_mm, qbias_ready, consts_ready, wx_ready, wv_const) = (sem(n) for n in (
             "zq_mm", "zq_done", "zneg_done", "zexp_done", "zsum_done", "qbase_ready", "cmd_mm", "cmd_ready",
             "ck_mm", "cv_mm", "ck_ready", "cv_ready", "ckw2_ready", "bkw2_ready", "bqw1_ready", "fold_mm",
             "fold_ready", "qfold_mm", "qfold_ready", "kbias_mm", "kbias_ready", "qbias_mm", "qbias_ready",
             "consts_ready", "wx_ready", "wv_const"))
        pl_mm, pl_done, vx_mm, vx_read, pen_done = (sem(n) for n in (
            "pl_mm", "pl_done", "vx_mm", "vx_read", "pen_done"))
        (pc_done, plpc_done, wv_ready, v_done, qk_done, hi_done, res1_done, mid_done, parts_done,
         v_evac, sel_done, sel_copied, ops_done, t_done, red_done, top_done, shift_done, leaky_done, exp_done,
         inv_done, prob_done, pt_done, pt_evac, msg_done, msg_evac, mu_done, ctx_done) = (sem(n) for n in (
             "pc_done", "plpc_done", "wv_ready", "v_done", "qk_done", "hi_done", "res1_done", "mid_done",
             "parts_done", "v_evac", "sel_done", "sel_copied", "ops_done", "t_done", "red_done",
             "top_done", "shift_done", "leaky_done", "exp_done", "inv_done", "prob_done", "pt_done",
             "pt_evac", "msg_done", "msg_evac", "mu_done", "ctx_done"))

        sems = {}

        def S(name):
            if name not in sems:
                sems[name] = sem(name)
            return sems[name]

        STEPS = T_ITER * G
        UNITS = GB * HEADS // 4

        def groups(eng, body):
            body(0, 0, False, True)
            with eng.Fori(0, (G - 2) // 2) as pair:
                body(2 * pair + 1, 1, True, True)
                body(2 * pair + 2, 0, True, True)
            body(G - 1, 1, True, False)

        def tiles(eng, slot_of):
            for k in range(RING):
                slot_of(k, k)
            with eng.Fori(1, SLOTS // RING) as lap:
                for r in range(RING):
                    slot_of(RING * lap + r, r)
            for k in range(SLOTS, SLOTS + LAST):
                slot_of(k, k % RING)

        def tile_turn(k, r):
            return 2 * (k - r) + 16

        ROUTE = 23
        TOP_LINK, DIFF_LINK, HOT_LINK, SLOT_LINK = 1, 11, 13, 21
        LAST = 6

        def rounds(eng, step):
            with eng.Fori(0, T_ITER - 1) as t:
                for g in range(G):
                    step(t, g, True, True)
            for g in range(G):
                s = (T_ITER - 1) * G + g
                step(T_ITER - 1, g, s + 1 < STEPS, s + 2 < STEPS)

        def after(t, g, k):
            return t + (g + k) // G, (g + k) % G

        block = ctx.enter_context(nc.Block())

        @block.sync
        def _(sp):
            sp.dma_start(w[:, :], weights).then_inc(in_w, 16)
            sp.dma_start(cst[:, :], consts).then_inc(in_c, 16)
            sp.dma_start(x_t[:, :], xT).then_inc(in_x, 16)
            sp.dma_start(adj_s[:, :], adj).then_inc(in_adj, 16)
            sp.dma_start(mask_b[:, :], mask.broadcast_to([128, TOK])).then_inc(in_mask, 16)
            sp.dma_start(rowv[:, :], rowvecs.broadcast_to([128, NR])).then_inc(in_bv, 16)
            sp.dma_start(id_s[:, :], ids).then_inc(S("in_ids"), 16)
            x_rows = x.rearrange("b n d -> n b d")
            sp.wait_ge(ctx_done, G + STEPS)
            sp.dma_start(rows[:, :, D:2 * D], x_rows[:, 0:GB, :]).then_inc(S("in_rows"), 16)
            with sp.Fori(1, G) as g:
                sp.wait_ge(S("scattered"), 16 * GB * g)
                sp.dma_start(rows[:, :, D:2 * D], x_rows[:, bass.ds(g * GB, GB), :]).then_inc(S("in_rows"), 16)
            sp.wait_ge(S("cond_mm"), G)
            sp.dma_start(w1_s, w1).then_inc(S("in_experts"), 16)
            sp.dma_start(w2_s, w2).then_inc(S("in_experts"), 16)
            sp.dma_start(b2_s, b2.broadcast_to([128, EXPERTS * D])).then_inc(S("in_experts"), 16)
            sp.wait_ge(S("pad_ready"), 2)
            sp.dma_start(sorted_rows[DUMMY:DUMMY + N, :], pad_row[:, :]).then_inc(S("padded"), 16)
            sp.wait_ge(S("pads_known"), 1)
            for e in range(EXPERTS // 2):
                at = sp.value_load(pad_i[0:1, e:e + 1], min_val=e * REGION, max_val=e * REGION + TOK)
                sp.dma_start(sorted_rows[bass.ds(at, N), :], pad_row[:, :]).then_inc(S("padded"), 16)
            sp.wait_ge(S("table_ready"), 2)
            sp.wait_ge(S("padded"), 16 * (EXPERTS + 1))
            sp.wait_ge(S("scattered"), 16 * B)

            def load_tile(k, r):
                at = sp.value_load(row_i[0:1, bass.ds(k, 1)], min_val=0, max_val=DUMMY)
                sp.dma_start(tile_s[:, r, :], sorted_rows[bass.ds(at, N), :]).then_inc(S(f"in_tile{r}"), 16)
            for k in range(RING):
                load_tile(k, k)
            with sp.Fori(1, SLOTS // RING) as lap:
                for r in range(RING):
                    k = RING * lap + r
                    sp.wait_ge(S("res_chain"), 2 * (k - RING) + 1).then_inc(S("passed"), 1)
                    sp.wait_ge(S("id_kept"), k - RING + 1).then_inc(S("passed"), 1)
                    load_tile(k, r)
            for r in range(4):
                sp.wait_ge(S(f"sent{r}"), 16 * (SLOTS // 4))

        @block.gpsimd
        def _(pool):
            pool.wait_ge(in_w, 16)
            pool.tensor_copy(w_x[:, :, 0:D], W("v", 0).unsqueeze(1).broadcast_to([128, B, D])).then_inc(wx_ready, 1)
            for par in range(2):
                for c in range(2):
                    pool.tensor_copy(w_v[:, par, :, c, 0:D], W("v", 1 + c).unsqueeze(1).broadcast_to([128, GB, D]))\
                        .then_inc(wv_const, 1)
            pool.wait_ge(qfold_ready, 1)
            pool.wait_ge(fold_ready, 2)
            pool.wait_ge(msg_evac, 1)
            pool.tensor_copy(w_x[:, :, D:D + TYPES],
                             query_fold[:, 0, :].unsqueeze(1).broadcast_to([128, B, TYPES])).then_inc(wx_ready, 1)
            for t in range(T_ITER):
                pool.tensor_copy(w_x[:, :, D + TYPES * (1 + t):D + TYPES * (2 + t)],
                                 key_fold[:, 0, t, :, :]).then_inc(wx_ready, 1)
            for par in range(2):
                pool.tensor_copy(w_v[:, par, :, :, D:D + TYPES],
                                 query_fold[:, 1:3, :].unsqueeze(1).broadcast_to([128, GB, 2, TYPES]))\
                    .then_inc(wv_const, 1)

            def key_columns(t, g):
                pool.tensor_copy(w_v[:, g % 2, :, :, D + TYPES:D + QK],
                                 key_fold[:, 1:3, bass.ds(t, 1), g * GB:(g + 1) * GB, :]
                                 .rearrange("p c t b i -> p (t b) c i")).then_inc(wv_ready, 1)
            key_columns(0, 0)
            key_columns(0, 1)
            pool.wait_ge(v_done, 1)
            key_columns(0, 2)

            def step(t, g, front, ahead):
                s = t * G + g
                if isinstance(t, int) and s + 3 >= STEPS:
                    return
                pool.wait_ge(v_done, s + 2)
                key_columns(*after(t, g, 3))
            rounds(pool, step)

            pool.wait_ge(ctx_done, G + STEPS)
            pool.memset(v_a[:, :, :, :], 0.0).then_inc(S("va_zero"), 1)
            pool.wait_ge(S("va_zero"), 1)
            for par in range(2):
                ones = v_a[:, par, :, 0:HEADS * VW].rearrange("p b (h c) -> p b h c", c=VW)[:, :, :, HD]
                pool.memset(ones, 1.0).then_inc(S("va_ones"), 1)
            pool.memset(pad_row[:, :], 0.0).then_inc(S("pad_ready"), 1)
            pool.wait_ge(S("pad_ready"), 1)
            pool.memset(pad_row[:, 2 * D + 1:2 * D + 2].bitcast(I32), FAR).then_inc(S("pad_ready"), 1)
            pool.wait_ge(S("in_ids"), 16)
            pool.wait_ge(in_bv, 16)

            def norm1_power(p):
                pool.wait_ge(S("var_ready"), p + 1)
                pool.tensor_tensor(rstd[:, :], ve[:, :], C("half"), ALU.pow).then_inc(S("rstd_ready"), 1)

            def rows_x1(p):
                pool.wait_ge(S("xn_ready"), p + 1)
                bc = lambda n: R(n).unsqueeze(1).broadcast_to([128, GB, D])
                pool.tensor_tensor(x1_g[:, :, :], xn[:, :, :], bc("ln1g"), ALU.mult).then_inc(S("x1g_ready"), 1)
                pool.wait_ge(S("x1g_ready"), p + 1)
                pool.wait_ge(S("in_rows"), 16 * (p + 1))
                pool.tensor_tensor(rows[:, :, 0:D], x1_g[:, :, :], bc("ln1b"), ALU.add).then_inc(S("row_x1"), 1)
                pool.tensor_copy(rows[:, :, 2 * D + 1:2 * D + 2].bitcast(I32),
                                 id_s[:, bass.ds(p * GB, GB)].unsqueeze(2)).then_inc(S("row_x1"), 1)

            def scatter(p):
                pool.wait_ge(S("route_chain"), p * ROUTE + SLOT_LINK)
                pool.wait_ge(S("row_x1"), 2 * (p + 1)).then_inc(S("passed"), 1)
                for b in range(GB):
                    pool.indirect_dma_start(sorted_rows, bass.IndirectOffsetOnAxis(ap=slot_i[:, b:b + 1], axis=0),
                                            rows[:, b, :], None, bounds_check=DUMMY - 1, oob_is_err=False)\
                        .then_inc(S("scattered"), 16)

            def mask_heads(g, par):
                pool.wait_ge(S("key_ready"), g + 1)
                for h in (4, 5, 6, 7, 12, 13, 14, 15):
                    pool.tensor_tensor(k_m[par][:, h, :], k_s[:, :], C("hmask")[:, h:h + 1].broadcast_to([128, GT]),
                                       ALU.mult).then_inc(S("km_pool"), 1)

            def body(g, par, prev, nxt):
                if prev:
                    norm1_power(g - 1)
                    rows_x1(g - 1)
                if nxt:
                    mask_heads(g + 1, 1 - par)
                if prev:
                    scatter(g - 1)
            mask_heads(0, 0)
            groups(pool, body)
            norm1_power(G - 1)
            rows_x1(G - 1)
            scatter(G - 1)

            def slot_of(k, r):
                static = isinstance(k, int)
                if not (static and (k < 3 or k - 3 >= SLOTS)):
                    t, rr = k - 3, (r - 3) % RING
                    pool.wait_ge(S(f"in_tile{rr}"), tile_turn(t, rr))
                    if not (static and t < 4):
                        pool.wait_ge(S("fin_ready"), t - 3)
                    pool.tensor_tensor(xb2[:, rr % 4, :], tile_s[:, rr, D:2 * D], R("ln2b"), ALU.add)\
                        .then_inc(S("xb_ready"), 1)
                    if not (static and t < RING):
                        pool.wait_ge(S(f"sent{rr % 4}"), 4 * (t - RING - rr % 4) + 16).then_inc(S("passed"), 1)
                    pool.tensor_copy(id_r[:, rr:rr + 1], tile_s[:, rr, 2 * D + 1:2 * D + 2].bitcast(I32))\
                        .then_inc(S("id_kept"), 1)
                if not (static and k < LAST):
                    t, rr = k - LAST, (r - LAST) % RING
                    pool.wait_ge(S("id_kept"), t + 1)
                    pool.wait_ge(S("fin_ready"), t + 1).then_inc(S("passed"), 1)
                    pool.indirect_dma_start(out, bass.IndirectOffsetOnAxis(ap=id_r[:, rr:rr + 1], axis=0),
                                            fin[:, rr % 4, :], None, bounds_check=TOK - 1, oob_is_err=False)\
                        .then_inc(S(f"sent{rr % 4}"), 16)
            tiles(pool, slot_of)

        @block.tensor
        def _(pe):
            flat = "p a n -> p (a n)"
            pe.wait_ge(in_w, 16)
            pe.matmul(U[:, 0:B], W("qin"), w[:, WCOLS["fside"][0]:WCOLS["fside"][1]], start=True, stop=True)\
                .then_inc(zq_mm, 1)
            pe.wait_ge(qbase_ready, 1)
            for t in range(T_ITER):
                mm = pe.matmul(M[:, t, 0:B], W("qt", t), q_base[:, :], start=True, stop=True)
            mm.then_inc(cmd_mm, 1)
            pe.wait_ge(cmd_ready, T_ITER)
            cmds = cmd[:, :, :].rearrange("p t b -> p (t b)")
            pe.matmul(PT[:, 0, :], W("pk"), cmds, start=True, stop=True).then_inc(ck_mm, 1)
            pe.matmul(U[:, 0:N], W("pv"), cmds, start=True, stop=True).then_inc(cv_mm, 1)
            pe.wait_ge(ckw2_ready, 1)
            folds = ck_w2[:, :, :].rearrange("p a i -> p (a i)")
            for c, bk in enumerate((T0, T1, M)):
                pe.matmul(bk[:, :, :].rearrange(flat), W("wk", c), folds, start=True, stop=True).then_inc(fold_mm, 1)
            pe.wait_ge(cv_ready, 1)
            for c in range(3):
                mm = pe.matmul(U[:, TYPES * c:TYPES * (c + 1)], W("wq", c),
                               w[:, WCOLS["w1t"][0]:WCOLS["w1t"][1]], start=True, stop=True)
            mm.then_inc(qfold_mm, 1)
            pe.wait_ge(in_c, 16)
            pe.wait_ge(ck_ready, 1)
            pe.wait_ge(bkw2_ready, 1)
            pe.matmul(PT[:, :, :].rearrange(flat), C("ones"), bk_w2[:, :], start=True, stop=True).then_inc(kbias_mm, 1)
            pe.wait_ge(bqw1_ready, 1)
            pe.matmul(PC[:, 0:TYPES], C("ones"), bq_w1[:, :], start=True, stop=True).then_inc(qbias_mm, 1)
            pe.wait_ge(in_x, 16)
            pe.wait_ge(fold_ready, 2)
            for g in range(G):
                if g >= 2:
                    pe.wait_ge(pl_done, g - 1)
                pe.matmul(TB[g % 2][:, :, :].rearrange(flat), W("pl"), x_t[:, g * GT:(g + 1) * GT],
                          start=True, stop=True).then_inc(pl_mm, 1)
            pe.wait_ge(wx_ready, 2 + T_ITER)
            for b in range(B):
                if b % 2 == 0 and b >= GB:
                    pe.wait_ge(vx_read, b // 2 - 1)
                mm = pe.matmul(V[:, b % GB, 0:D + TYPES * (1 + T_ITER)], x_t[:, b * N:(b + 1) * N], w_x[:, b, :],
                               start=True, stop=True)
                if b % 2:
                    mm.then_inc(vx_mm, 1)

            def pc(s, g):
                pe.wait_ge(ctx_done, s + 1)
                pe.wait_ge(plpc_done, s)
                pe.matmul(PC[:, :], W("pc"), ctx_t[:, g * GT:(g + 1) * GT], start=True, stop=True).then_inc(pc_done, 1)

            def v(s, g):
                pe.wait_ge(plpc_done, s + 1)
                pe.wait_ge(wv_ready, s + 1)
                pe.wait_ge(qk_done, s)
                pe.wait_ge(v_evac, s)
                for b in range(GB):
                    pe.matmul(V[:, b, 0:D + QK], ctx_t[:, g * GT + b * N:g * GT + (b + 1) * N],
                              w_v[:, g % 2, b, 0, :], start=True, stop=False)
                    mm = pe.matmul(V[:, b, 0:D + QK], plpc[:, g % 2, b * N:(b + 1) * N],
                                   w_v[:, g % 2, b, 1, :], start=False, stop=True)
                mm.then_inc(v_done, 1)

            def sel(s):
                pe.wait_ge(parts_done, s + 1)
                pe.wait_ge(pt_evac, s)
                pe.transpose(SEL, parts[:, :, :].rearrange("p b r -> p (b r)"), ident_h[:, :]).then_inc(sel_done, 1)

            def scores(s, g):
                pe.wait_ge(ops_done, s + 1)
                for b in range(GB):
                    pe.wait_ge(red_done, s * GB + max(b - 1, 0))
                    bk = TB[b % 2][:, :, :].rearrange(flat)
                    pe.matmul(bk, ident_h[:, :], penalty[:, g * GB + b, :, :].rearrange("p i m -> p (i m)"),
                              start=True, stop=False)
                    pe.matmul(bk, t_lhs[:, b, :], t_rhs[:, :, :].rearrange("p i m -> p (i m)"),
                              start=False, stop=True).then_inc(t_done, 1)

            def turn(s):
                pe.wait_ge(prob_done, s + 1)
                pe.wait_ge(sel_copied, s + 1)
                for b in range(GB):
                    mm = pe.transpose(PT[:, b, :], prob[:, b, :], C("ident"))
                mm.then_inc(pt_done, 1)

            def message(s, g):
                pe.wait_ge(pt_evac, s + 1)
                pe.wait_ge(v_evac, s + 1)
                pe.wait_ge(msg_evac, s + 1)
                for b in range(GB):
                    mm = pe.matmul(M[:, b, :], v_s[:, g % 2, b, :], prob_t[:, b, :], start=True, stop=True)
                mm.then_inc(msg_done, 1)

            def update(s, g):
                pe.wait_ge(msg_evac, s + 2)
                pe.wait_ge(ctx_done, G + s)
                pe.matmul(U[:, :], W("mu", 0), ctx_t[:, g * GT:(g + 1) * GT], start=True, stop=False)
                pe.matmul(U[:, :], W("mu", 1), msg_s[:, :], start=False, stop=True).then_inc(mu_done, 1)

            pe.wait_ge(qbias_ready, 1)
            pe.wait_ge(kbias_ready, 1)
            pc(0, 0)
            pe.wait_ge(wv_const, 6)
            pe.wait_ge(vx_read, B // 2)
            v(0, 0)
            pc(1, 1)
            pe.wait_ge(consts_ready, 2)
            sel(0)
            pe.wait_ge(pl_done, G)
            pe.wait_ge(pen_done, TYPES)
            scores(0, 0)

            def step(t, g, front, ahead):
                s, n = t * G + g, (g + 1) % G
                if front:
                    v(s + 1, n)
                turn(s)
                if ahead:
                    pc(s + 2, (g + 2) % G)
                if front:
                    sel(s + 1)
                message(s, g)
                if front:
                    scores(s + 1, n)
                update(s, g)
            rounds(pe, step)

            def cond(g, par):
                pe.matmul(X0, W("cb", 0), x_t[:, bass.ds(g * GT, GT)], start=True, stop=False)

            def cond_rest(g):
                pe.matmul(X0, W("cb", 1), ctx_t[:, bass.ds(g * GT, GT)], start=False, stop=True).then_inc(S("cond_mm"), 1)

            def query(g, par):
                pe.wait_ge(S("cond_ready"), g + 1)
                pe.matmul(X1, W("wi", 0), xc_s[:, par, :], start=True, stop=True).then_inc(S("query_mm"), 1)

            def key(g, par):
                pe.wait_ge(S("cond_ready"), g + 1)
                pe.matmul(X0, W("wi", 1), xc_s[:, par, :], start=True, stop=True).then_inc(S("key_mm"), 1)

            def value(g, par):
                pe.wait_ge(S("key_ready"), g + 1)
                for b in range(GB):
                    mm = pe.matmul(X0[:, b * N:(b + 1) * N], xc_s[:, par, b * N:(b + 1) * N], W("wi", 2),
                                   start=True, stop=True)
                mm.then_inc(S("value_mm"), 1)

            def head_scores(u, g, par, j):
                b, q = divmod(j, 4)
                pe.wait_ge(S("query_ready"), g + 1)
                if b == 0:
                    pe.wait_ge(S("km_dve") if q % 2 == 0 else S("km_pool"), 8 * g + 4 * (q // 2 + 1))
                if not (isinstance(u, int) and u < 2):
                    pe.wait_ge(S("ex_ready"), 4 * (u - 1))
                pe.matmul(SB[j % 2][:, :, :].rearrange(flat), q_s[:, par, b * N:(b + 1) * N],
                          k_m[par][:, 4 * q:4 * q + 4, b * N:(b + 1) * N], start=True, stop=True)\
                    .then_inc(S("scores_mm"), 1)

            def turn_exps(u, j):
                pe.wait_ge(S("ex_ready"), 4 * (u + 1))
                if not (isinstance(u, int) and u < 2):
                    pe.wait_ge(S("ext_ready"), u - 1)
                for h in range(4):
                    mm = pe.transpose(PB[j % 2][:, h, :], ex[:, j % 2, h, :], C("ident"))
                mm.then_inc(S("ext_mm"), 1)

            def weigh(u, g, par, j):
                b, q = divmod(j, 4)
                pe.wait_ge(S("ext_ready"), u + 1)
                pe.wait_ge(S("value_ready"), g + 1)
                if not (isinstance(u, int) and u < 2):
                    pe.wait_ge(S("o_ready"), u - 1)
                for h in range(4):
                    at = VW * (4 * q + h)
                    mm = pe.matmul(OB[j % 2][:, h, 0:VWIN], ex_t[:, j % 2, h, :], v_a[:, par, b, at:at + VWIN],
                                   start=True, stop=True)
                mm.then_inc(S("o_mm"), 1)

            def turn_heads(p):
                pe.wait_ge(S("on_ready"), p + 1)
                for b in range(GB):
                    mm = pe.transpose(X0[:, b * N:(b + 1) * N], o_n[:, b, :], C("ident"))
                mm.then_inc(S("ot_mm"), 1)

            def residual(p, par, b):
                pe.wait_ge(S("ot_ready"), p + 1)
                cols = slice(b * N, (b + 1) * N)
                pe.matmul(X1[:, cols], xc_s[:, par, cols], C("ident"), start=True, stop=False)
                pe.matmul(X1[:, cols], o_t[:, cols], W("wo"), start=False, stop=True).then_inc(S("h_mm"), 1)

            def turn_norm(p):
                pe.wait_ge(S("xn_ready"), p + 1)
                for b in range(GB):
                    mm = pe.transpose(X1[:, b * N:(b + 1) * N], xn[:, b, :], C("ident"))
                mm.then_inc(S("x1t_mm"), 1)

            def gate(p):
                pe.wait_ge(S("x1t_ready"), p + 1)
                for b in range(GB):
                    mm = pe.matmul(X0[:, b * N:b * N + 12], x1_t[:, b * N:(b + 1) * N], W("gate")[:, 0:12],
                                   start=True, stop=True)
                mm.then_inc(S("gate_mm"), 1)

            def rank(p):
                pe.wait_ge(S("route_chain"), p * ROUTE + HOT_LINK)
                pe.matmul(X1[:, 0:GB * EXPERTS], before_h[:, :], oh_h[:, :, :].rearrange("p b e -> p (b e)"),
                          start=True, stop=False)
                for b in range(GB - 1):
                    later = GB - 1 - b
                    pe.matmul(X1[:, (b + 1) * EXPERTS:GB * EXPERTS].rearrange("p (b e) -> p b e", b=later),
                              ones_h[:, :], oh_h[:, b, :].unsqueeze(1).broadcast_to([128, later, EXPERTS]),
                              start=False, stop=False)
                pe.matmul(X1[:, 0:GB * EXPERTS].rearrange("p (b e) -> p b e", b=GB), ones_h[:, :],
                          cs_h[:, :].unsqueeze(1).broadcast_to([128, GB, EXPERTS]), start=False, stop=True)\
                    .then_inc(S("rank_mm"), 1)

            pe.wait_ge(ctx_done, G + STEPS)
            pe.wait_ge(S("halves_ready"), 2)
            cond(0, 0)
            cond_rest(0)
            query(0, 0)
            key(0, 0)
            value(0, 0)
            head_scores(0, 0, 0, 0)
            head_scores(1, 0, 0, 1)

            def body(g, par, prev, nxt):
                for j in range(UNITS):
                    u = g * UNITS + j
                    if j + 2 < UNITS:
                        head_scores(u + 2, g, par, j + 2)
                    elif nxt:
                        head_scores(u + 2, g + 1, 1 - par, j + 2 - UNITS)
                    turn_exps(u, j)
                    if j:
                        weigh(u - 1, g, par, j - 1)
                    elif prev:
                        weigh(u - 1, g - 1, 1 - par, UNITS - 1)
                    if prev and j == 1:
                        turn_heads(g - 1)
                    if prev and j in (2, 3):
                        residual(g - 1, 1 - par, 2 * (j - 2))
                        residual(g - 1, 1 - par, 2 * (j - 2) + 1)
                    if nxt and j == 4:
                        if prev:
                            pe.wait_ge(S("ot_ready"), g)
                        cond(g + 1, 1 - par)
                    if nxt and j == 5:
                        cond_rest(g + 1)
                    if nxt and j == 6:
                        key(g + 1, 1 - par)
                    if prev and j == 7:
                        turn_norm(g - 1)
                    if prev and j == 9:
                        pe.wait_ge(S("key_ready"), g + 1 + nxt)
                        gate(g - 1)
                    if nxt and j == 10:
                        if prev:
                            pe.wait_ge(S("x1t_ready"), g)
                        query(g + 1, 1 - par)
                    if nxt and j == 11:
                        if prev:
                            pe.wait_ge(S("route_chain"), (g - 1) * ROUTE + TOP_LINK)
                        value(g + 1, 1 - par)
                    if prev and j == 13:
                        pe.wait_ge(S("query_ready"), g + 1 + nxt)
                        rank(g - 1)
            groups(pe, body)
            weigh(G * UNITS - 1, G - 1, 1, UNITS - 1)
            turn_heads(G - 1)
            for b in range(GB):
                residual(G - 1, 1, b)
            turn_norm(G - 1)
            gate(G - 1)
            rank(G - 1)
            pe.wait_ge(S("route_chain"), G * ROUTE)
            pe.matmul(X1[:, 0:EXPERTS], ones_h[:, :], cs_h[:, :], start=True, stop=True).then_inc(S("cnt_mm"), 1)

            def slot_of(k, r):
                i = r % 2
                static = isinstance(k, int)
                if not (static and k >= SLOTS):
                    pe.wait_ge(S(f"in_tile{r}"), tile_turn(k, r))
                    if not (static and k < 2):
                        pe.wait_ge(S("xt_ready"), k - 1)
                    pe.transpose(XT[i], tile_s[:, r, 0:D], C("ident")).then_inc(S("xt_mm"), 1)
                if not (static and (k < 2 or k - 2 >= SLOTS)):
                    pe.wait_ge(S("xt_ready"), k - 1)
                    pe.wait_ge(S("w1_ready"), k - 1)
                    if not (static and k < 4):
                        pe.wait_ge(S("ht_ready"), 2 * (k - 3))
                    for f in range(2):
                        mm = pe.matmul(HT[i][:, f * N:(f + 1) * N], w1_r[:, (r - 2) % 4, f * 128:(f + 1) * 128],
                                       xt_s[:, i, :], start=True, stop=True)
                    mm.then_inc(S("ht_mm"), 1)
                if not (static and (k < 4 or k - 4 >= SLOTS)):
                    e = pe.value_load(exp_i[0:1, bass.ds(k - 4, 1)], min_val=0, max_val=EXPERTS - 1)
                    if not (static and k < 6):
                        pe.wait_ge(S("yb_ready"), k - 5)
                    pe.wait_ge(S("ht_ready"), 2 * (k - 3))
                    for f in range(2):
                        mm = pe.matmul(YB[i], ht_s[:, i, f * N:(f + 1) * N], w2_s[:, bass.ds(e * FF + f * D, D)],
                                       start=(f == 0), stop=(f == 1))
                    mm.then_inc(S("y_mm"), 1)
            pe.wait_ge(S("in_experts"), 48)
            pe.wait_ge(S("table_ready"), 2)
            tiles(pe, slot_of)

        @block.vector
        def _(dve):
            dve.memset(parts[:, :, :], 0.0).then_inc(consts_ready, 1)
            dve.wait_ge(in_w, 16)
            dve.wait_ge(zq_mm, 1)
            dve.tensor_scalar(elu_z[:, :], U[:, 0:B], bias("qin"), None, ALU.add).then_inc(zq_done, 1)
            dve.wait_ge(zq_done, 1)
            dve.tensor_scalar(elu_n[:, :], elu_z[:, :], 0.0, None, ALU.min).then_inc(zneg_done, 1)
            dve.wait_ge(zexp_done, 1)
            dve.scalar_tensor_tensor(elu_s[:, :], elu_z[:, :], 0.0, elu_e[:, :], ALU.max, ALU.add).then_inc(zsum_done, 1)
            dve.wait_ge(zsum_done, 1)
            dve.tensor_scalar(q_base[:, :], elu_s[:, :], -1.0, None, ALU.add).then_inc(qbase_ready, 1)
            dve.tensor_scalar(bq_w1[:, :], w[:, WCOLS["w1t"][0]:WCOLS["w1t"][1]], bias("q"), None, ALU.mult)\
                .then_inc(bqw1_ready, 1)
            dve.wait_ge(in_c, 16)
            dve.tensor_copy(ident_h[:, :], C("ident")).then_inc(consts_ready, 1)
            dve.wait_ge(ck_ready, 1)
            dve.tensor_tensor(ck_w2[:, :, :], ck[:, :].unsqueeze(2).broadcast_to([128, T_ITER * B, TYPES]),
                              w[:, WCOLS["w2t"][0]:WCOLS["w2t"][1]].unsqueeze(1).broadcast_to([128, T_ITER * B, TYPES]),
                              ALU.mult).then_inc(ckw2_ready, 1)
            dve.wait_ge(ckw2_ready, 1)
            dve.tensor_scalar(bk_w2[:, :], ck_w2[:, :, :].rearrange("p a i -> p (a i)"), bias("k"), None, ALU.mult)\
                .then_inc(bkw2_ready, 1)
            dve.wait_ge(in_mask, 16)
            dve.tensor_scalar(ctx_t[:, :], mask_b[:, :], bias("init"), None, ALU.mult).then_inc(ctx_done, G)
            dve.wait_ge(kbias_mm, 1)
            dve.tensor_copy(kbias[:, :, :, :].rearrange("p t b i -> p (t b i)"),
                            PT[:, :, :].rearrange("p a n -> p (a n)")).then_inc(kbias_ready, 1)
            dve.wait_ge(qbias_mm, 1)
            dve.tensor_copy(qbias[:, :], PC[:, 0:TYPES]).then_inc(qbias_ready, 1)
            dve.wait_ge(in_adj, 16)
            adjs = adj_s[:, :].rearrange("p (b m) -> p b m", b=B)
            for i in range(TYPES):
                dve.tensor_scalar(penalty[:, :, i, :], adjs, float(i + 1), -BIG, ALU.not_equal, ALU.mult)\
                    .then_inc(pen_done, 1)
            dve.wait_ge(in_bv, 16)
            dve.wait_ge(qbias_ready, 1)
            dve.wait_ge(kbias_ready, 1)
            dve.wait_ge(pen_done, TYPES)
            for pair in range(B // 2):
                dve.wait_ge(vx_mm, pair + 1)
                bs = slice(2 * pair, 2 * pair + 2)
                vb = V[:, 2 * (pair % 2):2 * (pair % 2) + 2, :]
                dve.tensor_tensor(vx[:, bs, :], vb[:, :, 0:D], R("bv").unsqueeze(1).broadcast_to([128, 2, D]), ALU.add)
                dve.tensor_tensor(qkx[:, bs, :, 0:TYPES],
                                  vb[:, :, D:D + TYPES].unsqueeze(2).broadcast_to([128, 2, T_ITER, TYPES]),
                                  qbias[:, :].unsqueeze(1).unsqueeze(1).broadcast_to([128, 2, T_ITER, TYPES]), ALU.add)
                dve.tensor_tensor(qkx[:, bs, :, TYPES:QK],
                                  vb[:, :, D + TYPES:D + TYPES * (1 + T_ITER)].rearrange("p b (t i) -> p b t i", i=TYPES),
                                  kbias[:, :, bs, :].rearrange("p t b i -> p b t i"), ALU.add).then_inc(vx_read, 1)
            dve.wait_ge(vx_read, B // 2)
            dve.wait_ge(pl_done, G)

            def pl_times_pc(s, g):
                dve.wait_ge(pc_done, s + 1)
                dve.scalar_tensor_tensor(plpc[:, g % 2, :], PC[:, :], bias("pc"), pl_t[:, g * GT:(g + 1) * GT],
                                         ALU.add, ALU.mult).then_inc(plpc_done, 1)

            def score_parts(s, t, g):
                dve.wait_ge(v_done, s + 1)
                dve.tensor_tensor(qk[:, :, :], V[:, :, D:D + QK],
                                  qkx[:, g * GB:(g + 1) * GB, bass.ds(t, 1), :].rearrange("p b t j -> p (b t) j"),
                                  ALU.add).then_inc(qk_done, 1)
                dve.wait_ge(qk_done, s + 1)
                dve.tensor_copy(parts[:, :, 0:QK], qk[:, :, :]).then_inc(hi_done, 1)
                dve.wait_ge(hi_done, s + 1)
                dve.tensor_tensor(res1[:, :, :], qk[:, :, :], parts[:, :, 0:QK], ALU.subtract).then_inc(res1_done, 1)
                dve.wait_ge(res1_done, s + 1)
                dve.tensor_copy(parts[:, :, QK:2 * QK], res1[:, :, :]).then_inc(mid_done, 1)
                dve.wait_ge(mid_done, s + 1)
                dve.tensor_tensor(parts[:, :, 2 * QK:3 * QK], res1[:, :, :], parts[:, :, QK:2 * QK], ALU.subtract)\
                    .then_inc(parts_done, 1)

            def v_out(s, g):
                dve.tensor_tensor(v_s[:, g % 2, :, :], V[:, :, 0:D], vx[:, g * GB:(g + 1) * GB, :], ALU.add)\
                    .then_inc(v_evac, 1)

            def score_operands(s):
                dve.wait_ge(sel_done, s + 1)
                dve.tensor_copy(sel_s[:, :], SEL).then_inc(sel_copied, 1)
                dve.wait_ge(sel_copied, s + 1)
                for i in range(TYPES):
                    dve.tensor_scalar(t_rhs[:, i, :], sel_s[:, :], C("kmask")[:, i:i + 1], C("qind")[:, i:i + 1],
                                      ALU.mult, ALU.add)
                for b in range(GB):
                    op = dve.tensor_scalar(t_lhs[:, b, :], sel_s[:, :], C("isq")[:, b:b + 1], C("isk")[:, b:b + 1],
                                           ALU.mult, ALU.add)
                op.then_inc(ops_done, 1)

            def softmax_top(s):
                for b in range(GB):
                    dve.wait_ge(t_done, s * GB + b + 1)
                    dve.tensor_reduce(logit[:, b, :], TB[b % 2][:, :, :].rearrange("p i m -> p m i"), AX_X, ALU.max)\
                        .then_inc(red_done, 1)
                dve.wait_ge(red_done, (s + 1) * GB)
                dve.tensor_reduce(neg_top[:, :], logit[:, :, :], AX_X, ALU.max, negate=True).then_inc(top_done, 1)
                dve.wait_ge(top_done, s + 1)
                dve.scalar_tensor_tensor(shift[:, :], neg_top[:, :], ALPHA, neg_top[:, :], ALU.mult, ALU.min)\
                    .then_inc(shift_done, 1)
                for h in range(2):
                    bs = slice(2 * h, 2 * h + 2)
                    dve.scalar_tensor_tensor(leaky[:, bs, :], logit[:, bs, :], ALPHA, logit[:, bs, :], ALU.mult, ALU.max)\
                        .then_inc(leaky_done, 1)

            def softmax_scale(s):
                dve.wait_ge(exp_done, (s + 1) * GB)
                dve.reciprocal(inv[:, :], total[:, :]).then_inc(inv_done, 1)
                dve.wait_ge(inv_done, s + 1)
                for b in range(GB):
                    op = dve.tensor_scalar(prob[:, b, :], expo[:, b, :], inv[:, b:b + 1], None, ALU.mult)
                op.then_inc(prob_done, 1)

            def context(s, t, g):
                dve.wait_ge(mu_done, s + 1)
                cols = slice(g * GT, (g + 1) * GT)
                if isinstance(t, int) and t == T_ITER - 1:
                    dve.tensor_scalar(ctx_t[:, cols], U[:, :], bias("mu"), None, ALU.add).then_inc(ctx_done, 1)
                else:
                    dve.scalar_tensor_tensor(ctx_t[:, cols], U[:, :], bias("mu"), mask_b[:, cols],
                                             ALU.add, ALU.mult).then_inc(ctx_done, 1)

            pl_times_pc(0, 0)
            score_parts(0, 0, 0)
            v_out(0, 0)
            pl_times_pc(1, 1)
            score_operands(0)
            softmax_top(0)
            softmax_scale(0)

            def step(t, g, front, ahead):
                s = t * G + g
                tn, n = after(t, g, 1)
                if front:
                    score_parts(s + 1, tn, n)
                    v_out(s + 1, n)
                if ahead:
                    pl_times_pc(s + 2, (g + 2) % G)
                if front:
                    score_operands(s + 1)
                    softmax_top(s + 1)
                context(s, t, g)
                if front:
                    softmax_scale(s + 1)
            rounds(dve, step)

            dve.wait_ge(ctx_done, G + STEPS)
            dve.tensor_copy(before_h[:, :], C("before")).then_inc(S("halves_ready"), 1)
            dve.tensor_copy(ones_h[:, :], C("ones")).then_inc(S("halves_ready"), 1)
            dve.memset(cs[:, :], 0.0).then_inc(S("cs_zero"), 1)
            dve.memset(cs_h[:, :], 0.0).then_inc(S("cs_zero"), 1)

            def mask_heads(g, par, heads):
                dve.wait_ge(S("key_ready"), g + 1)
                for h in heads:
                    dve.tensor_scalar(k_m[par][:, h, :], k_s[:, :], C("hmask")[:, h:h + 1], None, ALU.mult)\
                        .then_inc(S("km_dve"), 1)

            def value_out(g, par):
                dve.wait_ge(S("value_mm"), g + 1)
                dve.wait_ge(S("va_ones"), 2)
                dst = v_a[:, par, :, 0:HEADS * VW].rearrange("p b (h c) -> p b h c", c=VW)
                for b in range(GB):
                    op = dve.tensor_tensor(dst[:, b, :, 0:HD],
                                           X0[:, b * N:(b + 1) * N].rearrange("p (h c) -> p h c", c=HD),
                                           R("iv").rearrange("p (h c) -> p h c", c=HD), ALU.add)
                op.then_inc(S("value_ready"), 1)

            def row_tops(u, j):
                i = j % 2
                dve.wait_ge(S("scores_mm"), u + 1)
                if not (isinstance(u, int) and u < 2):
                    dve.wait_ge(S("ex_ready"), 4 * (u - 1))
                dve.tensor_reduce(neg_head[:, i, :], SB[i][:, :, :], AX_X, ALU.max, negate=True)\
                    .then_inc(S("top_ready"), 1)

            def sums_out(u, par, j):
                b, q = divmod(j, 4)
                dve.wait_ge(S("o_mm"), u + 1)
                dve.tensor_copy(o_a[:, par, b * HEADS + 4 * q:b * HEADS + 4 * q + 4, :], OB[j % 2][:, :, 0:VW])\
                    .then_inc(S("o_ready"), 1)

            def heads_out(p, par):
                dve.wait_ge(S("o_ready"), (p + 1) * UNITS)
                dve.reciprocal(rden[:, :], o_a[:, par, :, HD]).then_inc(S("rden_ready"), 1)
                dve.wait_ge(S("rden_ready"), p + 1)
                dve.tensor_tensor(o_n[:, :, :].rearrange("p b (h c) -> p (b h) c", c=HD), o_a[:, par, :, 0:HD],
                                  rden[:, :].unsqueeze(2).broadcast_to([128, GB * HEADS, HD]), ALU.mult)\
                    .then_inc(S("on_ready"), 1)

            def residual_out(p):
                dve.wait_ge(S("h_mm"), (p + 1) * GB)
                dve.tensor_tensor(h_s[:, :, :], X1.rearrange("p (b d) -> p b d", b=GB),
                                  R("bo").unsqueeze(1).broadcast_to([128, GB, D]), ALU.add).then_inc(S("h_ready"), 1)

            def norm1_stats(p):
                dve.wait_ge(S("h_ready"), p + 1)
                for b in range(GB):
                    op = dve.bn_stats(stats[:, b, :], h_s[:, b, :])
                op.then_inc(S("stats_ready"), 1)

            def norm1_variance(p):
                dve.wait_ge(S("stats_ready"), p + 1).then_inc(S("passed"), 1)
                for b in range(GB):
                    op = dve.bn_aggr(mv[:, b, :], stats[:, b, :])
                op.then_inc(S("mv_ready"), 1)
                dve.wait_ge(S("mv_ready"), p + 1)
                dve.tensor_scalar(ve[:, :], mv[:, :, 1], EPS, None, ALU.add).then_inc(S("var_ready"), 1)

            def norm1_out(p):
                dve.wait_ge(S("rstd_ready"), p + 1)
                for b in range(GB):
                    op = dve.tensor_scalar(xn[:, b, :], h_s[:, b, :], mv[:, b, 0:1], rstd[:, b:b + 1],
                                           ALU.subtract, ALU.mult)
                op.then_inc(S("xn_ready"), 1)

            def route(p, links):
                bc = lambda ap, n: ap.unsqueeze(2).broadcast_to([128, GB, n])
                per_batch = lambda ap, n: ap.unsqueeze(1).broadcast_to([128, GB, n])
                for n in links:
                    if n > 0:
                        dve.wait_ge(S("route_chain"), p * ROUTE + n)
                    if n == 0:
                        dve.wait_ge(S("gate_mm"), p + 1)
                        op = dve.tensor_tensor(lg[:, :, :], X0.rearrange("p (b d) -> p b d", b=GB)[:, :, 0:12],
                                               per_batch(R("gate"), 12), ALU.add)
                    elif n == 1:
                        op = dve.tensor_reduce(gm[:, :], lg[:, :, 0:4], AX_X, ALU.max)
                    elif n == 2:
                        op = dve.tensor_tensor(dg[:, :, :], lg[:, :, 0:4], bc(gm[:, :], 4), ALU.subtract)
                    elif n == 3:
                        op = dve.scalar_tensor_tensor(pick[:, :, :], dg[:, :, :], 0.0, per_batch(C("pref"), 4),
                                                      ALU.is_equal, ALU.mult)
                    elif n == 4:
                        op = dve.tensor_reduce(sm[:, :], pick[:, :, :], AX_X, ALU.max)
                    elif n == 5:
                        op = dve.tensor_tensor(oh[:, :, :], pick[:, :, :], bc(sm[:, :], 4), ALU.is_equal)
                    elif n == 6:
                        op = dve.tensor_tensor(pr[:, :, :, :], lg[:, :, 4:12].rearrange("p b (g k) -> p b g k", k=2),
                                               oh[:, :, :].unsqueeze(3).broadcast_to([128, GB, 4, 2]), ALU.mult)
                    elif n == 7:
                        op = dve.tensor_scalar(m2s[:, :], sm[:, :], -2.0, None, ALU.mult)
                    elif n == 8:
                        op = dve.tensor_reduce(el[:, :, :], pr[:, :, :, :].rearrange("p b g k -> p b k g"), AX_X, ALU.add)
                    elif n == 9:
                        op = dve.tensor_tensor(de[:, :], el[:, :, 1], el[:, :, 0], ALU.subtract)
                    elif n == 10:
                        op = dve.scalar_tensor_tensor(nd[:, :], de[:, :], -1.0, de[:, :], ALU.mult, ALU.min)
                    elif n == 11:
                        op = dve.scalar_tensor_tensor(ev[:, :], de[:, :], 0.0, m2s[:, :], ALU.is_gt, ALU.add)
                    elif n == 12:
                        op = dve.tensor_tensor(oh_h[:, :, :], per_batch(C("iota"), EXPERTS), bc(ev[:, :], EXPERTS),
                                               ALU.is_equal)
                    elif n == 13:
                        dve.wait_ge(S("gate_exps"), 2 * (p + 1))
                        op = dve.tensor_reduce(gs[:, :], eg[:, :, :], AX_X, ALU.add)
                    elif n == 14:
                        op = dve.scalar_tensor_tensor(den[:, :], ee[:, :], 1.0, gs[:, :], ALU.add, ALU.mult)
                    elif n == 15:
                        dve.wait_ge(S("in_rows"), 16 * (p + 1))
                        op = dve.reciprocal(rows[:, :, 2 * D], den[:, :])
                    elif n == 16:
                        op = dve.tensor_reduce(csum[:, :], oh_h[:, :, :].rearrange("p b e -> p e b"), AX_X, ALU.add)
                    elif n == 17:
                        dve.wait_ge(S("rank_mm"), p + 1)
                        op = dve.tensor_tensor(rk[:, :, :], X1[:, 0:GB * EXPERTS].rearrange("p (b e) -> p b e", b=GB),
                                               per_batch(C("base"), EXPERTS), ALU.add)
                    elif n == 18:
                        op = dve.tensor_tensor(rk2[:, :, :], rk[:, :, :], oh_h[:, :, :], ALU.mult)
                    elif n == 19:
                        op = dve.tensor_reduce(slot[:, :], rk2[:, :, :], AX_X, ALU.add)
                    elif n == 20:
                        op = dve.tensor_copy(slot_i[:, :], slot[:, :])
                    elif n == 21:
                        op = dve.tensor_tensor(cs[:, :], cs[:, :], csum[:, :], ALU.add)
                    else:
                        op = dve.tensor_copy(cs_h[:, :], cs[:, :])
                    op.then_inc(S("route_chain"), 1)

            dve.wait_ge(S("cs_zero"), 2)
            dve.wait_ge(S("halves_ready"), 2)
            mask_heads(0, 0, (0, 1, 2, 3, 8, 9, 10, 11))
            value_out(0, 0)
            row_tops(0, 0)
            row_tops(1, 1)

            def body(g, par, prev, nxt):
                for j in range(UNITS):
                    u = g * UNITS + j
                    if j + 2 < UNITS or nxt:
                        row_tops(u + 2, j)
                    if j >= 2:
                        sums_out(u - 2, par, j - 2)
                    if j == 0 and prev:
                        sums_out(u - 2, 1 - par, UNITS - 2)
                        sums_out(u - 1, 1 - par, UNITS - 1)
                        heads_out(g - 1, 1 - par)
                    if prev and j == 3:
                        residual_out(g - 1)
                    if prev and j == 4:
                        norm1_stats(g - 1)
                    if prev and j == 5:
                        norm1_variance(g - 1)
                    if prev and j == 6:
                        norm1_out(g - 1)
                    if nxt and 8 <= j < 14:
                        mask_heads(g + 1, 1 - par, ((0, 1), (2, 3), (8,), (9,), (10,), (11,))[j - 8])
                    if prev and j >= 10:
                        route(g - 1, ROUTE_SLOTS[j])
                    if nxt and j == 12:
                        value_out(g + 1, 1 - par)
            ROUTE_SLOTS = {10: range(0, 5), 11: range(5, 10), 12: range(10, 13), 13: (), 14: range(13, 19),
                           15: range(19, ROUTE)}
            groups(dve, body)
            sums_out(G * UNITS - 2, 1, UNITS - 2)
            sums_out(G * UNITS - 1, 1, UNITS - 1)
            heads_out(G - 1, 1)
            residual_out(G - 1)
            norm1_stats(G - 1)
            norm1_variance(G - 1)
            norm1_out(G - 1)
            route(G - 1, range(ROUTE))

            done = [0]

            def then(ins):
                done[0] += 1
                ins.then_inc(S("table_chain"), 1)
                dve.wait_ge(S("table_chain"), done[0])
            row8 = lambda ap, n: ap.unsqueeze(1).broadcast_to([128, n, EXPERTS])
            dve.wait_ge(S("cnt_mm"), 1)
            then(dve.tensor_copy(cnt[:, :], X1[:, 0:EXPERTS]))
            then(dve.tensor_tensor(pad_at[:, :], cnt[:, :], C("base"), ALU.add))
            dve.tensor_copy(pad_i[:, :], pad_at[:, :]).then_inc(S("pads_known"), 1)
            then(dve.tensor_tensor(full[:, :, :], C("start").unsqueeze(1).broadcast_to([128, EXPERTS, 32]),
                                   cnt[:, :].unsqueeze(2).broadcast_to([128, EXPERTS, 32]), ALU.is_lt))
            then(dve.tensor_reduce(nt[:, :], full[:, :, :], AX_X, ALU.add))
            then(dve.tensor_tensor(ntu[:, :, :], C("upto").rearrange("p (a b) -> p a b", a=EXPERTS),
                                   row8(nt[:, :], EXPERTS), ALU.mult))
            then(dve.tensor_reduce(cum[:, :], ntu[:, :, :], AX_X, ALU.add))
            then(dve.tensor_scalar(hop[:, :], nt[:, :], float(-N), float(REGION), ALU.mult, ALU.add))
            then(dve.tensor_tensor(behind[:, :, :], C("tile").unsqueeze(2).broadcast_to([128, SLOTS, EXPERTS]),
                                   row8(cum[:, :], SLOTS), ALU.is_ge))
            then(dve.tensor_reduce(t_exp[:, :], behind[:, :, :], AX_X, ALU.add))
            then(dve.tensor_tensor(hops[:, :, :], behind[:, :, :], row8(hop[:, :], SLOTS), ALU.mult))
            then(dve.tensor_reduce(t_hop[:, :], hops[:, :, :], AX_X, ALU.add))
            then(dve.scalar_tensor_tensor(t_row[:, :], C("tile"), float(N), t_hop[:, :], ALU.mult, ALU.add))
            dve.tensor_scalar(row_i[:, 0:SLOTS], t_row[:, :], float(DUMMY), None, ALU.min).then_inc(S("table_ready"), 1)
            dve.tensor_scalar(exp_i[:, 0:SLOTS], t_exp[:, :], float(EXPERTS - 1), None, ALU.min).then_inc(S("table_ready"), 1)
            dve.memset(eps_s[:, :], EPS).then_inc(S("eps_ready"), 1)
            dve.wait_ge(S("table_ready"), 2)
            dve.wait_ge(S("in_experts"), 48)

            def slot_of(k, r):
                static = isinstance(k, int)
                last, i, ri = k - LAST, r % 2, (r - LAST) % 4
                fresh, qi, qq = k - 4, (r - 4) % 4, (r - 4) % RING
                ends = not (static and k < LAST)
                starts = not (static and (k < 4 or fresh >= SLOTS))
                if ends:
                    dve.wait_ge(S("sd_ready"), last + 1)
                    dve.reciprocal(rs2[:, ri:ri + 1], sd2[:, ri:ri + 1]).then_inc(S("norm2_chain"), 1)
                if starts:
                    e = dve.value_load(exp_i[0:1, bass.ds(fresh, 1)], min_val=0, max_val=EXPERTS - 1)
                    dve.wait_ge(S("y_mm"), fresh + 1)
                    dve.tensor_tensor(yb[:, i, :], YB[i], b2_s[:, bass.ds(e * D, D)], ALU.add).then_inc(S("yb_ready"), 1)
                if ends:
                    dve.wait_ge(S("norm2_chain"), 3 * last + 1)
                    dve.tensor_scalar(xn2[:, i, :], res[:, ri, :], mv2[:, ri, 0:1], rs2[:, ri:ri + 1],
                                      ALU.subtract, ALU.mult).then_inc(S("norm2_chain"), 1)
                if starts:
                    dve.wait_ge(S("yb_ready"), fresh + 1)
                    dve.scalar_tensor_tensor(res[:, qi, :], yb[:, i, :], tile_s[:, qq, 2 * D:2 * D + 1],
                                             tile_s[:, qq, 0:D], ALU.mult, ALU.add).then_inc(S("res_chain"), 1)
                if ends:
                    dve.wait_ge(S("norm2_chain"), 3 * last + 2)
                    dve.tensor_tensor(xg2[:, i, :], xn2[:, i, :], R("ln2g"), ALU.mult).then_inc(S("norm2_chain"), 1)
                if starts:
                    dve.wait_ge(S("res_chain"), 2 * fresh + 1)
                    dve.bn_stats(st2[:, i, :], res[:, qi, :]).then_inc(S("res_chain"), 1)
                if ends:
                    dve.wait_ge(S("norm2_chain"), 3 * last + 3)
                    dve.wait_ge(S("xb_ready"), last + 1)
                    if not (static and last < 4):
                        dve.wait_ge(S(f"sent{ri}"), 4 * (last - 4 - ri) + 16)
                    dve.tensor_tensor(fin[:, ri, :], xg2[:, i, :], xb2[:, ri, :], ALU.add).then_inc(S("fin_ready"), 1)
                if starts:
                    dve.wait_ge(S("res_chain"), 2 * fresh + 2).then_inc(S("passed"), 1)
                    dve.bn_aggr(mv2[:, qi, :], st2[:, i, :]).then_inc(S("mv2_ready"), 1)
            tiles(dve, slot_of)

        @block.scalar
        def _(act):
            act.wait_ge(zneg_done, 1)
            act.activation(elu_e[:, :], elu_n[:, :], ACT.Exp).then_inc(zexp_done, 1)
            act.wait_ge(in_w, 16)
            act.wait_ge(cmd_mm, 1)
            for t in range(T_ITER):
                act.activation(cmd[:, t, :], M[:, t, 0:B], ACT.Identity, bias=bias(f"qt{t}")).then_inc(cmd_ready, 1)
            act.wait_ge(ck_mm, 1)
            act.activation(ck[:, :], PT[:, 0, :], ACT.Identity, bias=bias("pk")).then_inc(ck_ready, 1)
            act.wait_ge(cv_mm, 1)
            act.activation(cv[:, :, :].rearrange("p t b -> p (t b)"), U[:, 0:N], ACT.Identity, bias=bias("pv"))\
                .then_inc(cv_ready, 1)
            for c, bk in enumerate((T0, T1, M)):
                act.wait_ge(fold_mm, c + 1)
                act.activation(key_fold[:, c, :, :, :].rearrange("p t b i -> p (t b i)"),
                               bk[:, :, :].rearrange("p a n -> p (a n)"), ACT.Copy)\
                    .then_inc(fold_ready if c < 2 else msg_evac, 1)
            act.wait_ge(qfold_mm, 1)
            act.activation(query_fold[:, :, :].rearrange("p c i -> p (c i)"), U[:, 0:3 * TYPES], ACT.Copy)\
                .then_inc(qfold_ready, 1)
            for g in range(G):
                act.wait_ge(pl_mm, g + 1)
                act.activation(pl_t[:, g * GT:(g + 1) * GT], TB[g % 2][:, :, :].rearrange("p a n -> p (a n)"),
                               ACT.Identity, bias=bias("pl")).then_inc(pl_done, 1)

            def probabilities_out(s):
                act.wait_ge(pt_done, s + 1)
                act.activation(prob_t[:, :, :], PT[:, :, :], ACT.Copy).then_inc(pt_evac, 1)

            def message_out(s, t, g):
                act.wait_ge(msg_done, s + 1)
                for b in range(GB):
                    scale = cv[:, bass.ds(t, 1), g * GB + b:g * GB + b + 1].rearrange("p t b -> p (t b)")
                    op = act.activation(msg_s[:, b * N:(b + 1) * N], M[:, b, :], ACT.Copy, scale=scale)
                op.then_inc(msg_evac, 1)

            def exps(s):
                act.wait_ge(shift_done, s + 1)
                for b in range(GB):
                    act.wait_ge(leaky_done, 2 * s + b // 2 + 1)
                    act.activation(expo[:, b, :], leaky[:, b, :], ACT.Exp, bias=shift[:, b:b + 1],
                                   accum_out=total[:, b:b + 1]).then_inc(exp_done, 1)

            act.wait_ge(cv_ready, 1)
            exps(0)

            def step(t, g, front, ahead):
                s = t * G + g
                probabilities_out(s)
                message_out(s, t, g)
                if front:
                    exps(s + 1)
            rounds(act, step)

            act.wait_ge(ctx_done, G + STEPS)

            def cond_out(g, par):
                act.wait_ge(S("cond_mm"), g + 1)
                act.activation(xc_s[:, par, :], X0, ACT.Identity, bias=bias("cb")).then_inc(S("cond_ready"), 1)

            def query_out(g, par):
                act.wait_ge(S("query_mm"), g + 1)
                act.activation(q_s[:, par, :], X1, ACT.Identity, scale=float(HD) ** -0.5, bias=iq_s[:, :]).then_inc(S("query_ready"), 1)

            def key_out(g, par):
                act.wait_ge(S("key_mm"), g + 1)
                act.activation(k_s[:, :], X0, ACT.Identity, bias=bias("ik")).then_inc(S("key_ready"), 1)

            def exponentials(u, j):
                i = j % 2
                act.wait_ge(S("top_ready"), u + 1)
                if not (isinstance(u, int) and u < 2):
                    act.wait_ge(S("ext_mm"), u - 1)
                for h in range(4):
                    act.activation(ex[:, i, h, :], SB[i][:, h, :], ACT.Exp, bias=neg_head[:, i, h:h + 1])\
                        .then_inc(S("ex_ready"), 1)

            def turned_out(u, j):
                i = j % 2
                act.wait_ge(S("ext_mm"), u + 1)
                if not (isinstance(u, int) and u < 2):
                    act.wait_ge(S("o_mm"), u - 1)
                act.activation(ex_t[:, i, :, :], PB[i][:, :, :], ACT.Copy).then_inc(S("ext_ready"), 1)

            def heads_turned(p):
                act.wait_ge(S("ot_mm"), p + 1)
                act.activation(o_t[:, :], X0, ACT.Copy).then_inc(S("ot_ready"), 1)

            def norm1_turned(p):
                act.wait_ge(S("x1t_mm"), p + 1)
                act.activation(x1_t[:, :], X1, ACT.Identity, scale=bias("ln1g"), bias=bias("ln1b"))\
                    .then_inc(S("x1t_ready"), 1)

            def gate_exps(p):
                act.wait_ge(S("route_chain"), p * ROUTE + DIFF_LINK)
                act.activation(eg[:, :, :], dg[:, :, :], ACT.Exp).then_inc(S("gate_exps"), 1)
                act.activation(ee[:, :], nd[:, :], ACT.Exp).then_inc(S("gate_exps"), 1)

            act.activation(iq_s[:, :], bias("iq"), ACT.Copy, scale=float(HD) ** -0.5).then_inc(S("iq_ready"), 1)
            cond_out(0, 0)
            act.wait_ge(S("iq_ready"), 1)
            query_out(0, 0)
            key_out(0, 0)
            exponentials(0, 0)
            exponentials(1, 1)

            def body(g, par, prev, nxt):
                for j in range(UNITS):
                    u = g * UNITS + j
                    turned_out(u, j)
                    if j + 2 < UNITS or nxt:
                        exponentials(u + 2, j)
                    if prev and j == 1:
                        heads_turned(g - 1)
                    if nxt and j == 5:
                        cond_out(g + 1, 1 - par)
                    if nxt and j == 6:
                        key_out(g + 1, 1 - par)
                    if prev and j == 8:
                        norm1_turned(g - 1)
                    if nxt and j == 10:
                        query_out(g + 1, 1 - par)
                    if prev and j == 13:
                        gate_exps(g - 1)
            groups(act, body)
            heads_turned(G - 1)
            norm1_turned(G - 1)
            gate_exps(G - 1)

            act.wait_ge(S("pad_ready"), 2)
            act.wait_ge(S("pads_known"), 1)
            for e in range(EXPERTS // 2, EXPERTS):
                at = act.value_load(pad_i[0:1, e:e + 1], min_val=e * REGION, max_val=e * REGION + TOK)
                act.dma_start(sorted_rows[bass.ds(at, N), :], pad_row[:, :]).then_inc(S("padded"), 16)

            act.wait_ge(S("eps_ready"), 1)
            act.wait_ge(S("in_experts"), 48)
            act.wait_ge(S("table_ready"), 2)

            def slot_of(k, r):
                static = isinstance(k, int)
                if not (static and k >= SLOTS):
                    e = act.value_load(exp_i[0:1, bass.ds(k, 1)], min_val=0, max_val=EXPERTS - 1)
                    if not (static and k < 4):
                        act.wait_ge(S("ht_ready"), 2 * (k - 3)).then_inc(S("passed"), 1)
                    act.activation(w1_r[:, r % 4, :], w1_s[:, bass.ds(e * W1ROW, W1ROW)], ACT.Copy)\
                        .then_inc(S("w1_ready"), 1)
                if not (static and (k < 1 or k - 1 >= SLOTS)):
                    q = (r - 1) % 2
                    act.wait_ge(S("xt_mm"), k)
                    if not (static and k < 3):
                        act.wait_ge(S("ht_mm"), k - 2)
                    act.activation(xt_s[:, q, :], XT[q], ACT.Copy).then_inc(S("xt_ready"), 1)
                if not (static and (k < 5 or k - 5 >= SLOTS)):
                    ri = (r - 5) % 4
                    act.wait_ge(S("mv2_ready"), k - 4)
                    act.activation(sd2[:, ri:ri + 1], mv2[:, ri, 1:2], ACT.Sqrt, bias=eps_s[:, :]).then_inc(S("sd_ready"), 1)
                if not (static and (k < 3 or k - 3 >= SLOTS)):
                    q = (r - 3) % 2
                    act.wait_ge(S("ht_mm"), k - 2)
                    if not (static and k < 5):
                        act.wait_ge(S("y_mm"), k - 4)
                    for f in range(2):
                        act.activation(ht_s[:, q, f * N:(f + 1) * N], HT[q][:, f * N:(f + 1) * N], ACT.Relu,
                                       bias=w1_r[:, (r - 3) % 4, FF + f:FF + f + 1]).then_inc(S("ht_ready"), 1)
            tiles(act, slot_of)


def kernel(**inputs):
    import concourse.bacc as bacc
    from concourse.bass_utils import run_bass_kernel_spmd
    a = {k: np.asarray(v) for k, v in inputs.items()}
    nc = bacc.Bacc("TRN2", target_bir_lowering=False, num_devices=1)
    arrays = layouts(a)
    aps = {n: nc.dram_tensor(n, v.shape, mybir.dt.from_np(v.dtype), kind="ExternalInput").ap()
           for n, v in arrays.items()}
    aps["out"] = nc.dram_tensor("out", (TOK, D), F32, kind="ExternalOutput").ap()
    build(nc, **aps)
    r = run_bass_kernel_spmd(nc, [arrays], core_ids=[0])
    return r.results[0]["out"].reshape(B, N, D)


def layouts(a):
    c = {k[8:]: v for k, v in a.items() if k.startswith("L0_cond_")}
    f = {k[7:]: v for k, v in a.items() if k.startswith("L0_ffn_")}
    qt, bqt, wes = a["fside_BxSxS_0"], a["mask_BxS_ff0"], a["cond_2048"]

    def chunks(m):
        return m.reshape(m.shape[0], -1, 128).transpose(2, 1, 0).reshape(128, -1)
    cols = np.zeros((128, 24), np.float32)
    for n, v in (("qin", c["b_qin"]), ("pl", c["b_pl"]), ("pc", c["b_pc"]), ("q", c["b_q"]), ("k", c["b_k"]),
                 ("mu", c["b_mu"]), ("cb", c["b_cb"]), ("pk", c["b_pk"]), ("pv", c["b_pv"]), ("qt0", bqt[0]),
                 ("qt1", bqt[1]), ("qt2", bqt[2]), ("qt3", bqt[3]), ("init", c["init_mem"][0]),
                 ("iq", f["in_proj_b"][:D]), ("ik", f["in_proj_b"][D:2 * D]), ("ln1g", f["ln1_g"]),
                 ("ln1b", f["ln1_b"])):
        cols[:, BIAS[n]] = v
    gates = np.zeros((128, D), np.float32)
    gates[:, 0:GROUPS_E] = f["w_group"]
    gates[:, GROUPS_E:GROUPS_E + EXPERTS] = f["w_expert"].transpose(1, 0, 2).reshape(D, EXPERTS)
    pieces = {"qin": c["w_qin"].T, "pk": c["w_pk"].T, "pv": c["w_pv"].T,
              "qt": qt[:T_ITER].transpose(2, 0, 1).reshape(128, -1), "wq": c["w_q"], "wk": c["w_k"],
              "fside": a["fside_BxS_0"].T, "w1t": wes[:TYPES, :D].T, "w2t": wes[:TYPES, D:].T,
              "pl": c["w_pl"].T, "pc": c["w_pc"].T, "v": chunks(c["w_v"]), "mu": chunks(c["w_mu"]),
              "cb": chunks(c["w_cb"]), "wi": f["in_proj_w"].T, "wo": f["out_proj_w"].T, "gate": gates, "bias": cols}
    rowvecs = np.concatenate([c["b_v"], f["in_proj_b"][2 * D:], f["out_proj_b"], f["ln1_g"], f["ln1_b"], f["ln2_g"],
                              f["ln2_b"], f["b_group"], f["b_expert"].reshape(-1)]).reshape(1, NR)
    return {"xT": np.ascontiguousarray(a["x"].transpose(2, 0, 1).reshape(128, TOK)),
            "adj": np.ascontiguousarray(a["itok_BxSxS_0_4"].transpose(1, 0, 2).reshape(128, TOK)),
            "mask": np.ascontiguousarray(a["mask_BxS_ff1"].reshape(1, TOK)),
            "weights": np.ascontiguousarray(np.concatenate([pieces[n] for n in WCOLS], axis=1)),
            "rowvecs": rowvecs, "consts": shape_constants(),
            "ids": (np.arange(B)[None, :] * N + np.arange(N)[:, None]).astype(np.int32),
            "x": np.ascontiguousarray(a["x"]),
            "w1": np.ascontiguousarray(np.concatenate(
                [f["w1"].transpose(1, 0, 2), f["b1"].reshape(EXPERTS, 2, 128).transpose(2, 0, 1)], axis=2)
                .reshape(128, EXPERTS * W1ROW)),
            "w2": np.ascontiguousarray(f["w2"].reshape(EXPERTS, 2, 128, D).transpose(2, 0, 1, 3).reshape(128, -1)),
            "b2": np.ascontiguousarray(f["b2"].reshape(1, EXPERTS * D))}
```

```python
from contextlib import ExitStack

import numpy as np
import concourse.bass as bass
from concourse import mybir

F32 = mybir.dt.float32
BF16 = mybir.dt.bfloat16
I32 = mybir.dt.int32
ALU = mybir.AluOpType
ACT = mybir.ActivationFunctionType
AX_X = mybir.AxisListType.X

B, N, D = 32, 128, 128
TOK = B * N
GB = 4
G = B // GB
GT = GB * N
T_ITER = 4
TYPES = 4
ALPHA = 0.2
BIG = float(2.0 ** 53)
NPART = 3
QK = 2 * TYPES

WCOLS = {}


def _columns():
    at = 0
    for name, n in (("bias", 24), ("fside", B), ("qin", D), ("qt", T_ITER * D), ("pk", D), ("pv", D),
                    ("w1t", TYPES), ("w2t", TYPES), ("wk", 3 * D), ("wq", 3 * D), ("v", 3 * D), ("pl", D), ("pc", D),
                    ("mu", 2 * D), ("cb", 2 * D), ("wi", 3 * D), ("wo", D), ("gate", D)):
        WCOLS[name] = (at, at + n)
        at += n
    return at


NW = _columns()
BIAS = {n: i for i, n in enumerate(("qin", "pl", "pc", "q", "k", "mu", "cb", "pk", "pv", "qt0", "qt1", "qt2",
                                    "qt3", "init", "iq", "ik", "ln1g", "ln1b"))}
NW_FIRST = WCOLS["wk"][0]
RCOLS = {"iv": (0, 128), "bo": (128, 256), "ln1g": (256, 384), "ln1b": (384, 512), "ln2g": (512, 640),
         "ln2b": (640, 768), "gate": (768, 780), "bv": (780, 908)}
NR = 908
HEADS = 16
HD = D // HEADS
VW = HD + 1
VWIN = 56
VROW = 192
EXPERTS, FF = 8, 256
GROUPS_E = 4
REGION = TOK + N
ROW = 260
TILES = TOK // N + EXPERTS - 1
SLOTS = TILES + 1
RING = 8
DUMMY = EXPERTS * REGION
W1ROW = FF + FF // 128
FAR = 1 << 20
EPS = 1e-5
CCOLS = {"ident": (0, 128), "ones": (128, 256), "kmask": (256, 260), "qind": (260, 264), "isq": (264, 268),
         "isk": (268, 272), "hmask": (272, 288), "pref": (288, 292), "iota": (292, 300), "base": (300, 308),
         "half": (308, 312), "before": (312, 440), "start": (440, 472), "upto": (472, 536), "tile": (536, 576),
         "regionT": (576, 584)}
NC = 584


WORK = 17024


def shape_constants():
    c = np.zeros((128, NC), np.float32)
    c[:, 0:128] = np.eye(128)
    c[:, 128:256] = 1.0
    for row in range(128):
        b, r = divmod(row, 32)
        part, j = divmod(r, QK)
        if part >= NPART:
            continue
        if j < TYPES:
            c[row, 260 + j] = 1.0
            c[row, 264 + b] = 1.0
        else:
            c[row, 256 + j - TYPES] = 1.0
            c[row, 268 + b] = 1.0
    for p in range(128):
        c[p, 272 + p // HD] = 1.0
    c[:, 288:292] = np.arange(GROUPS_E, 0, -1)
    c[:, 292:300] = np.arange(EXPERTS) - EXPERTS
    c[:, 300:308] = np.arange(EXPERTS) * REGION
    c[:, 308:312] = -0.5
    c[:, 312:440] = np.triu(np.ones((128, 128)), 1)
    c[:, 440:472] = np.arange(32) * N
    c[:, 472:536] = np.tril(np.ones((8, 8))).reshape(-1)
    c[:, 536:576] = np.arange(40)
    c[:, 576:584] = REGION
    return c


def build(nc, x, xT, adj, mask, weights, rowvecs, consts, ids, w1, w2, b2, out):
    sorted_rows = nc.dram_tensor("sorted_rows", (DUMMY + N, ROW), F32, kind="Internal").ap()
    with ExitStack() as ctx:
        def sb(name, shape, dt=F32):
            return ctx.enter_context(nc.sbuf_tensor(name, shape, dt))

        def sem(name):
            return ctx.enter_context(nc.semaphore(name))

        x_t = sb("x_t", [128, TOK])
        ctx_t = sb("ctx_t", [128, TOK])
        w = sb("w", [128, NW])
        cst = sb("cst", [128, NC])
        rowv = sb("rowv", [128, NR])
        ident_h = sb("ident_h", [128, 128], BF16)
        room_p = sb("room_p", [128, 2 * TOK])
        room_v = sb("room_v", [128, 2 * TOK])
        room_w = sb("room_w", [128, WORK])
        penalty = room_p[:, :].bitcast(BF16).rearrange("p (b i m) -> p b i m", b=B, i=TYPES)
        pl_t = room_v[:, 0:TOK]
        adj_s = ctx_t[:, :].bitcast(I32)
        vx = room_v[:, TOK:2 * TOK].rearrange("p (b d) -> p b d", b=B)
        k_m = [room_p[:, :].rearrange("p (h n) -> p h n", h=HEADS),
               room_v[:, :].rearrange("p (h n) -> p h n", h=HEADS)]
        used = {"a": 0, "b": 0, "c": 0}
        rooms = {"a": (room_w, WORK), "b": (room_w, WORK), "c": (room_p, 2 * TOK)}

        def carve(phase, shape, dt=F32):
            n = int(np.prod(shape[1:]))
            words = n if dt != BF16 else n // 2
            room, size = rooms[phase]
            ap = room[:, used[phase]:used[phase] + words]
            used[phase] += words
            assert used[phase] <= size, (phase, used[phase])
            if dt != F32:
                ap = ap.bitcast(dt)
            names = "abcde"[:len(shape) - 1]
            return ap.rearrange(f"p ({' '.join(names)}) -> p {' '.join(names)}", **dict(zip(names, shape[1:])))

        def A(*shape, dt=F32):
            return carve("a", shape, dt)

        def Bf(*shape, dt=F32):
            return carve("b", shape, dt)

        def Cf(*shape, dt=F32):
            return carve("c", shape, dt)

        mask_b = A(128, TOK)
        qkx = A(128, B, T_ITER, QK)
        w_v = A(128, 2, GB, 2, D + QK)
        ck_w2 = A(128, T_ITER * B, TYPES)
        bk_w2 = A(128, T_ITER * B * TYPES)
        key_fold = A(128, 3, T_ITER, B, TYPES)
        kbias = A(128, T_ITER, B, TYPES)
        shared = used["a"]
        w_x = A(128, B, D + TYPES + T_ITER * TYPES)
        used["a"] = shared
        plpc = A(128, 2, GT)
        v_s = A(128, 4, GB, D)
        logit = A(128, GB, N)
        leaky = A(128, GB, N)
        expo = A(128, GB, N)
        prob = A(128, GB, N)
        prob_t = A(128, GB, N)
        msg_s = A(128, GT)
        ctx_raw = A(128, GT)
        t_rhs = sb("t_rhs", [128, TYPES, N], BF16)
        t_lhs = sb("t_lhs", [128, GB, N], BF16)
        q_base = sb("q_base", [128, B])
        elu_z = sb("elu_z", [128, B])
        elu_n = sb("elu_n", [128, B])
        elu_e = sb("elu_e", [128, B])
        elu_s = sb("elu_s", [128, B])
        cmd = sb("cmd", [128, T_ITER, B])
        ck = sb("ck", [128, T_ITER * B])
        cv = sb("cv", [128, T_ITER, B])
        bq_w1 = sb("bq_w1", [128, TYPES])
        query_fold = sb("query_fold", [128, 3, TYPES])
        qbias = sb("qbias", [128, TYPES])
        qk = sb("qk", [128, GB, QK])
        res1 = sb("res1", [128, GB, QK])
        parts = sb("parts", [128, GB, 32], BF16)
        sel_s = sb("sel_s", [128, N], BF16)
        neg_top = sb("neg_top", [128, GB])
        shift = sb("shift", [128, GB])
        total = sb("total", [128, GB])
        inv = sb("inv", [128, GB])
        xc_s = Bf(128, 2, GT)
        q_s = Bf(128, 2, GT)
        k_s = Bf(128, GT)
        v_a = Bf(128, 2, GB, VROW)
        ex = Bf(128, 2, 4, N)
        ex_t = Bf(128, 2, 4, N)
        o_a = Bf(128, 2, GB * HEADS, VW)
        o_n = Bf(128, GB, D)
        o_t = Bf(128, GT)
        h_s = Bf(128, GB, D)
        xn = Bf(128, GB, D)
        x1_t = Bf(128, GT)
        x1_g = Bf(128, GB, D)
        rows = Bf(128, GB, ROW)
        pad_row = Bf(128, ROW)
        neg_head = sb("neg_head", [128, 2, 4])
        iq_s = sb("iq_s", [128, 1])
        rden = sb("rden", [128, GB * HEADS])
        stats = sb("stats", [128, GB, 6])
        mv = sb("mv", [128, GB, 2])
        ve = sb("ve", [128, GB])
        rstd = sb("rstd", [128, GB])
        id_s = sb("id_s", [128, B], I32)
        lg = sb("lg", [128, GB, 12])
        gm = sb("gm", [128, GB])
        dg = sb("dg", [128, GB, 4])
        eg = sb("eg", [128, GB, 4])
        pick = sb("pick", [128, GB, 4])
        sm = sb("sm", [128, GB])
        oh = sb("oh", [128, GB, 4])
        pr = sb("pr", [128, GB, 4, 2])
        el = sb("el", [128, GB, 2])
        de = sb("de", [128, GB])
        nd = sb("nd", [128, GB])
        ee = sb("ee", [128, GB])
        gs = sb("gs", [128, GB])
        den = sb("den", [128, GB])
        m2s = sb("m2s", [128, GB])
        ev = sb("ev", [128, GB])
        oh_h = sb("oh_h", [128, GB, EXPERTS], BF16)
        csum = sb("csum", [128, EXPERTS])
        cs = sb("cs", [128, EXPERTS])
        cs_h = sb("cs_h", [128, EXPERTS], BF16)
        rk = sb("rk", [128, GB, EXPERTS])
        rk2 = sb("rk2", [128, GB, EXPERTS])
        slot = sb("slot", [128, GB])
        slot_i = sb("slot_i", [128, GB], I32)
        cnt = sb("cnt", [128, EXPERTS])
        full = Cf(128, EXPERTS, 32)
        nt = sb("nt", [128, EXPERTS])
        ntu = Cf(128, EXPERTS, EXPERTS)
        cum = sb("cum", [128, EXPERTS])
        hop = sb("hop", [128, EXPERTS])
        behind = Cf(128, SLOTS, EXPERTS)
        hops = Cf(128, SLOTS, EXPERTS)
        t_exp = sb("t_exp", [128, SLOTS])
        t_hop = sb("t_hop", [128, SLOTS])
        t_row = sb("t_row", [128, SLOTS])
        pad_at = sb("pad_at", [128, EXPERTS])
        row_i = sb("row_i", [128, SLOTS], I32)
        exp_i = sb("exp_i", [128, SLOTS], I32)
        pad_i = sb("pad_i", [128, EXPERTS], I32)
        w1_s, w2_s = x_t[:, 0:EXPERTS * W1ROW], ctx_t[:, 0:EXPERTS * FF]
        b2_s = ctx_t[0:1, EXPERTS * FF:EXPERTS * (FF + D)]
        tile_s = Cf(128, RING, ROW)
        xt_s = Cf(128, 2, D)
        w1_r = Cf(128, 4, W1ROW)
        ht_s = Cf(128, 2, FF)
        id_r = sb("id_r", [128, RING], I32)
        res = Cf(128, 4, D)
        xn2 = Cf(128, 2, D)
        xg2 = Cf(128, 2, D)
        xb2 = Cf(128, 4, D)
        fin = Cf(128, 4, D)
        st2 = sb("st2", [128, 2, 6])
        mv2 = sb("mv2", [128, 4, 2])
        sd2 = sb("sd2", [128, 4])
        rs2 = sb("rs2", [128, 4])
        eps_s = sb("eps_s", [128, 1])
        before_h = sb("before_h", [128, 128], BF16)
        ones_h = sb("ones_h", [128, 128], BF16)

        def W(name, c=0, n=D):
            a = WCOLS[name][0] + c * D
            return w[:, a:a + n]

        def bias(name):
            a = WCOLS["bias"][0] + BIAS[name]
            return w[:, a:a + 1]

        def C(name):
            a, b = CCOLS[name]
            return cst[:, a:b]

        def R(name):
            a, b = RCOLS[name]
            return rowv[:, a:b]

        def bank(name, shape, dt=F32):
            return ctx.enter_context(nc.psum_tensor(name, shape, dt))
        PC = bank("PC", [128, GT])
        V = bank("V", [128, GB, 256])
        T0 = bank("T0", [128, TYPES, N])
        T1 = bank("T1", [128, TYPES, N])
        PT = bank("PT", [128, GB, N])
        M = bank("M", [128, GB, N])
        U = bank("U", [128, GT])
        TB = [T0, T1]
        SEL = PT[:, 0, 0:N // 2].bitcast(BF16)
        SB = [T0, T1]
        PB = [PT, M]
        OB = [PC[:, :].rearrange("p (h d) -> p h d", h=4), U[:, :].rearrange("p (h d) -> p h d", h=4)]
        X0 = V[:, 0:2, :].rearrange("p a c -> p (a c)")
        X1 = V[:, 2:4, :].rearrange("p a c -> p (a c)")
        XT = [T0[:, 0, :], T1[:, 0, :]]
        HT = [PC[:, 0:FF], U[:, 0:FF]]
        YB = [X0[:, 0:D], X1[:, 0:D]]

        in_w, in_w2, in_x, in_adj, in_mask, in_c, in_bv = (sem(n) for n in (
            "in_w", "in_w2", "in_x", "in_adj", "in_mask", "in_c", "in_bv"))
        (zq_mm, zq_done, zneg_done, zexp_done, zsum_done, qbase_ready, cmd_mm, cmd_ready, ck_mm, cv_mm, ck_ready,
         cv_ready, ckw2_ready, bkw2_ready, bqw1_ready, fold_mm, fold_ready, qfold_mm, kbias_mm,
         kbias_ready, qbias_mm, qbias_ready, consts_ready, wx_ready, wv_const) = (sem(n) for n in (
             "zq_mm", "zq_done", "zneg_done", "zexp_done", "zsum_done", "qbase_ready", "cmd_mm", "cmd_ready",
             "ck_mm", "cv_mm", "ck_ready", "cv_ready", "ckw2_ready", "bkw2_ready", "bqw1_ready", "fold_mm",
             "fold_ready", "qfold_mm", "kbias_mm", "kbias_ready", "qbias_mm", "qbias_ready",
             "consts_ready", "wx_ready", "wv_const"))
        pl_mm, pl_done, vx_mm, vx_act, vx_dve, pen_done = (sem(n) for n in (
            "pl_mm", "pl_done", "vx_mm", "vx_act", "vx_dve", "pen_done"))
        (pc_done, plpc_done, wv_ready, v_done, qk_done, hi_done, res1_done, mid_done, parts_done,
         v_evac, sel_done, sel_copied, ops_done, t_done, red_done, top_done, shift_done, leaky_done, exp_done,
         inv_done, prob_done, pt_done, pt_evac, msg_done, msg_evac, mu_done, ctx_done) = (sem(n) for n in (
             "pc_done", "plpc_done", "wv_ready", "v_done", "qk_done", "hi_done", "res1_done", "mid_done",
             "parts_done", "v_evac", "sel_done", "sel_copied", "ops_done", "t_done", "red_done",
             "top_done", "shift_done", "leaky_done", "exp_done", "inv_done", "prob_done", "pt_done",
             "pt_evac", "msg_done", "msg_evac", "mu_done", "ctx_done"))

        sems = {}

        def S(name):
            if name not in sems:
                sems[name] = sem(name)
            return sems[name]

        STEPS = T_ITER * G
        UNITS = GB * HEADS // 4

        def groups(eng, body):
            body(0, 0, False, True)
            with eng.Fori(0, (G - 2) // 2) as pair:
                body(2 * pair + 1, 1, True, True)
                body(2 * pair + 2, 0, True, True)
            body(G - 1, 1, True, False)

        def tiles(eng, slot_of):
            for k in range(RING):
                slot_of(k, k)
            with eng.Fori(RING, SLOTS - RING + 1, RING) as first:
                for r in range(RING):
                    slot_of(first + r, r)
            for k in range(SLOTS, SLOTS + LAST):
                slot_of(k, k % RING)

        def tile_turn(k, r):
            return 2 * (k - r) + 16

        ROUTE = 23
        TOP_LINK, DIFF_LINK, HOT_LINK, SUM_LINK = 1, 11, 13, 18
        LAST = 6

        def rounds(eng, step):
            with eng.Fori(0, T_ITER - 1) as t:
                for g in range(G):
                    step(t, g, True, True)
            for g in range(G):
                s = (T_ITER - 1) * G + g
                step(T_ITER - 1, g, s + 1 < STEPS, s + 2 < STEPS)

        def after(t, g, k):
            return t + (g + k) // G, (g + k) % G

        def vx_out(copy, eng, read, pair):
            eng.wait_ge(vx_mm, pair + 1)
            bs = slice(2 * pair, 2 * pair + 2)
            vb = V[:, 2 * (pair % 2):2 * (pair % 2) + 2, :]
            copy(vx[:, bs, :], vb[:, :, 0:D])
            copy(qkx[:, bs, :, 0:TYPES], vb[:, :, D:D + TYPES].unsqueeze(2).broadcast_to([128, 2, T_ITER, TYPES]))
            copy(qkx[:, bs, :, TYPES:QK], vb[:, :, D + TYPES:D + TYPES * (1 + T_ITER)]
                 .rearrange("p b (t i) -> p b t i", i=TYPES)).then_inc(read, 1)

        block = ctx.enter_context(nc.Block())

        @block.sync
        def _(sp):
            sp.dma_start(w[:, 0:NW_FIRST], weights[:, 0:NW_FIRST]).then_inc(in_w, 16)
            sp.dma_start(cst[:, :], consts).then_inc(in_c, 16)
            sp.dma_start(w[:, NW_FIRST:NW], weights[:, NW_FIRST:NW]).then_inc(in_w2, 16)
            sp.dma_start(adj_s[:, :], adj).then_inc(in_adj, 16)
            sp.dma_start(x_t[:, :], xT).then_inc(in_x, 16)
            sp.dma_start(mask_b[:, :], mask.broadcast_to([128, TOK])).then_inc(in_mask, 16)
            sp.dma_start(rowv[:, :], rowvecs.broadcast_to([128, NR])).then_inc(in_bv, 16)
            sp.dma_start(id_s[:, :], ids).then_inc(S("in_ids"), 16)
            x_rows = x.rearrange("b n d -> n b d")
            sp.wait_ge(S("u_out"), STEPS + 1)
            sp.dma_start(rows[:, :, D:2 * D], x_rows[:, 0:GB, :]).then_inc(S("in_rows"), 16)
            with sp.Fori(1, G) as g:
                sp.wait_ge(S("scattered"), 16 * GB * g)
                sp.dma_start(rows[:, :, D:2 * D], x_rows[:, bass.ds(g * GB, GB), :]).then_inc(S("in_rows"), 16)
            sp.wait_ge(S("cond_mm"), G)
            sp.dma_start(w1_s, w1).then_inc(S("in_experts"), 16)
            sp.dma_start(w2_s, w2).then_inc(S("in_experts"), 16)
            sp.dma_start(b2_s, b2).then_inc(S("in_experts"), 16)
            sp.wait_ge(S("pad_ready"), 2)
            sp.dma_start(sorted_rows[DUMMY:DUMMY + N, :], pad_row[:, :]).then_inc(S("padded"), 16)
            sp.wait_ge(S("pads_known"), 1)
            for e in range(EXPERTS // 2):
                at = sp.value_load(pad_i[0:1, e:e + 1], min_val=e * REGION, max_val=e * REGION + TOK)
                sp.dma_start(sorted_rows[bass.ds(at, N), :], pad_row[:, :]).then_inc(S("padded"), 16)
            sp.wait_ge(S("table_ready"), 2)
            first_row = sp.value_load(row_i[0:1, 0:1], min_val=0, max_val=DUMMY)
            sp.wait_ge(S("padded"), 16 * (EXPERTS + 1))
            sp.wait_ge(S("scattered"), 16 * B)

            def load_tile(k, r, at=None):
                if at is None:
                    at = sp.value_load(row_i[0:1, bass.ds(k, 1)], min_val=0, max_val=DUMMY)
                sp.dma_start(tile_s[:, r, :], sorted_rows[bass.ds(at, N), :]).then_inc(S(f"in_tile{r}"), 16)
            load_tile(0, 0, first_row)
            for k in range(1, RING):
                load_tile(k, k)
            with sp.Fori(RING, SLOTS - RING + 1, RING) as first:
                for r in range(RING):
                    k = first + r
                    sp.wait_ge(S("res_ready"), k - RING + 1).then_inc(S("passed"), 1)
                    sp.wait_ge(S("id_kept"), k - RING + 1).then_inc(S("passed"), 1)
                    load_tile(k, r)
            for r in range(4):
                sp.wait_ge(S(f"sent{r}"), 16 * (SLOTS // 4))

        @block.gpsimd
        def _(pool):
            pool.wait_ge(S("u_out"), 1)
            pool.wait_ge(fold_ready, 2)
            pool.wait_ge(msg_evac, 1)
            pool.tensor_copy(w_x[:, :, D:D + TYPES],
                             query_fold[:, 0, :].unsqueeze(1).broadcast_to([128, B, TYPES])).then_inc(wx_ready, 1)
            for t in range(T_ITER):
                pool.tensor_copy(w_x[:, :, D + TYPES * (1 + t):D + TYPES * (2 + t)],
                                 key_fold[:, 0, t, :, :]).then_inc(wx_ready, 1)
            for par in range(2):
                pool.tensor_copy(w_v[:, par, :, :, D:D + TYPES],
                                 query_fold[:, 1:3, :].unsqueeze(1).broadcast_to([128, GB, 2, TYPES]))\
                    .then_inc(S("wv_query"), 1)

            def key_columns(t, g):
                pool.tensor_copy(w_v[:, g % 2, :, :, D + TYPES:D + QK],
                                 key_fold[:, 1:3, bass.ds(t, 1), g * GB:(g + 1) * GB, :]
                                 .rearrange("p c t b i -> p (t b) c i")).then_inc(wv_ready, 1)
            key_columns(0, 0)
            key_columns(0, 1)
            pool.wait_ge(in_bv, 16)
            for g in range(G):
                pool.wait_ge(vx_act, g + 1)
                pool.wait_ge(vx_dve, g + 1)
                bs = slice(g * GB, (g + 1) * GB)
                pool.tensor_tensor(vx[:, bs, :], vx[:, bs, :], R("bv").unsqueeze(1).broadcast_to([128, GB, D]), ALU.add)\
                    .then_inc(S("vx_ready"), 1)
            pool.wait_ge(v_done, 1)
            key_columns(0, 2)

            def masked_context(s, t, g):
                pool.wait_ge(S("u_out"), s + 2)
                cols = slice(g * GT, (g + 1) * GT)
                pool.tensor_tensor(ctx_t[:, cols], ctx_raw[:, :], mask_b[:, cols], ALU.mult).then_inc(ctx_done, 1)

            def step(t, g, front, ahead):
                s = t * G + g
                last_round = isinstance(t, int) and t == T_ITER - 1
                if not (last_round and s + 3 >= STEPS):
                    pool.wait_ge(v_done, s + 2)
                    key_columns(*after(t, g, 3))
                if not last_round:
                    masked_context(s, t, g)
            rounds(pool, step)

            pool.wait_ge(ctx_done, STEPS)
            pool.memset(v_a[:, :, :, :], 0.0).then_inc(S("va_zero"), 1)
            pool.wait_ge(S("va_zero"), 1)
            for par in range(2):
                ones = v_a[:, par, :, 0:HEADS * VW].rearrange("p b (h c) -> p b h c", c=VW)[:, :, :, HD]
                pool.memset(ones, 1.0).then_inc(S("va_ones"), 1)

            def norm1_power(p):
                pool.wait_ge(S("var_ready"), p + 1)
                pool.tensor_tensor(rstd[:, :], ve[:, :], C("half"), ALU.pow).then_inc(S("rstd_ready"), 1)

            def rows_x1(p):
                pool.wait_ge(S("xn_ready"), p + 1)
                bc = lambda n: R(n).unsqueeze(1).broadcast_to([128, GB, D])
                pool.tensor_tensor(x1_g[:, :, :], xn[:, :, :], bc("ln1g"), ALU.mult).then_inc(S("x1g_ready"), 1)
                pool.wait_ge(S("x1g_ready"), p + 1)
                pool.wait_ge(S("in_rows"), 16 * (p + 1))
                pool.tensor_tensor(rows[:, :, 0:D], x1_g[:, :, :], bc("ln1b"), ALU.add).then_inc(S("row_x1"), 1)
                pool.tensor_copy(rows[:, :, 2 * D + 1:2 * D + 2].bitcast(I32),
                                 id_s[:, bass.ds(p * GB, GB)].unsqueeze(2)).then_inc(S("row_x1"), 1)

            def scatter(p):
                pool.wait_ge(S("route_chain"), (p + 1) * ROUTE)
                pool.wait_ge(S("row_x1"), 2 * (p + 1)).then_inc(S("passed"), 1)
                for b in range(GB):
                    pool.indirect_dma_start(sorted_rows, bass.IndirectOffsetOnAxis(ap=slot_i[:, b:b + 1], axis=0),
                                            rows[:, b, :], None, bounds_check=DUMMY - 1, oob_is_err=False)\
                        .then_inc(S("scattered"), 16)

            def mask_heads(g, par):
                pool.wait_ge(S("key_ready"), g + 1)
                for h in (4, 5, 6, 7, 12, 13, 14, 15):
                    pool.tensor_tensor(k_m[par][:, h, :], k_s[:, :], C("hmask")[:, h:h + 1].broadcast_to([128, GT]),
                                       ALU.mult).then_inc(S("km_pool"), 1)

            def body(g, par, prev, nxt):
                if prev:
                    norm1_power(g - 1)
                    rows_x1(g - 1)
                if nxt:
                    mask_heads(g + 1, 1 - par)
                if prev:
                    scatter(g - 1)
            mask_heads(0, 0)
            pool.wait_ge(S("u_out"), STEPS + 1)
            pool.memset(pad_row[:, :], 0.0).then_inc(S("pad_ready"), 1)
            pool.wait_ge(S("pad_ready"), 1)
            pool.memset(pad_row[:, 2 * D + 1:2 * D + 2].bitcast(I32), FAR).then_inc(S("pad_ready"), 1)
            pool.wait_ge(S("in_ids"), 16)
            pool.wait_ge(in_bv, 16)
            groups(pool, body)
            norm1_power(G - 1)
            rows_x1(G - 1)
            scatter(G - 1)

            def slot_of(k, r):
                static = isinstance(k, int)
                if not (static and (k < 3 or k - 3 >= SLOTS)):
                    t, rr = k - 3, (r - 3) % RING
                    pool.wait_ge(S(f"in_tile{rr}"), tile_turn(t, rr))
                    if not (static and t < 4):
                        pool.wait_ge(S("fin_ready"), t - 3)
                    pool.tensor_tensor(xb2[:, rr % 4, :], tile_s[:, rr, D:2 * D], R("ln2b"), ALU.add)\
                        .then_inc(S("xb_ready"), 1)
                    if not (static and t < RING):
                        pool.wait_ge(S(f"sent{rr % 4}"), 4 * (t - RING - rr % 4) + 16).then_inc(S("passed"), 1)
                    pool.tensor_copy(id_r[:, rr:rr + 1], tile_s[:, rr, 2 * D + 1:2 * D + 2].bitcast(I32))\
                        .then_inc(S("id_kept"), 1)
                if not (static and k < LAST):
                    t, rr = k - LAST, (r - LAST) % RING
                    pool.wait_ge(S("id_kept"), t + 1)
                    pool.wait_ge(S("fin_ready"), t + 1).then_inc(S("passed"), 1)
                    pool.indirect_dma_start(out, bass.IndirectOffsetOnAxis(ap=id_r[:, rr:rr + 1], axis=0),
                                            fin[:, rr % 4, :], None, bounds_check=TOK - 1, oob_is_err=False)\
                        .then_inc(S(f"sent{rr % 4}"), 16)
            tiles(pool, slot_of)

        @block.tensor
        def _(pe):
            flat = "p a n -> p (a n)"
            pe.wait_ge(in_w, 16)
            pe.matmul(U[:, 0:B], W("qin"), w[:, WCOLS["fside"][0]:WCOLS["fside"][1]], start=True, stop=True)\
                .then_inc(zq_mm, 1)
            pe.wait_ge(qbase_ready, 1)
            for t in range(T_ITER):
                mm = pe.matmul(M[:, t, 0:B], W("qt", t), q_base[:, :], start=True, stop=True)
            mm.then_inc(cmd_mm, 1)
            pe.wait_ge(cmd_ready, T_ITER)
            cmds = cmd[:, :, :].rearrange("p t b -> p (t b)")
            pe.matmul(PT[:, 0, :], W("pk"), cmds, start=True, stop=True).then_inc(ck_mm, 1)
            pe.matmul(U[:, 0:N], W("pv"), cmds, start=True, stop=True).then_inc(cv_mm, 1)
            pe.wait_ge(in_w2, 16)
            pe.wait_ge(ckw2_ready, 1)
            folds = ck_w2[:, :, :].rearrange("p a i -> p (a i)")
            for c, bk in enumerate((T0, T1, M)):
                pe.matmul(bk[:, :, :].rearrange(flat), W("wk", c), folds, start=True, stop=True).then_inc(fold_mm, 1)
            pe.wait_ge(cv_ready, 1)
            for c in range(3):
                mm = pe.matmul(U[:, TYPES * c:TYPES * (c + 1)], W("wq", c),
                               w[:, WCOLS["w1t"][0]:WCOLS["w1t"][1]], start=True, stop=True)
            mm.then_inc(qfold_mm, 1)
            pe.wait_ge(in_c, 16)
            pe.wait_ge(ck_ready, 1)
            pe.wait_ge(bkw2_ready, 1)
            pe.matmul(PT[:, :, :].rearrange(flat), C("ones"), bk_w2[:, :], start=True, stop=True).then_inc(kbias_mm, 1)
            pe.wait_ge(bqw1_ready, 1)
            pe.matmul(PC[:, 0:TYPES], C("ones"), bq_w1[:, :], start=True, stop=True).then_inc(qbias_mm, 1)
            pe.wait_ge(in_x, 16)
            pe.wait_ge(fold_ready, 2)
            for g in range(G):
                if g >= 2:
                    pe.wait_ge(pl_done, g - 1)
                pe.matmul(TB[g % 2][:, :, :].rearrange(flat), W("pl"), x_t[:, g * GT:(g + 1) * GT],
                          start=True, stop=True).then_inc(pl_mm, 1)
            pe.wait_ge(wx_ready, 1 + T_ITER)
            pe.wait_ge(wv_const, 4)
            for b in range(B):
                if b % 2 == 0 and b >= GB:
                    pe.wait_ge(vx_act if b % GB == 0 else vx_dve, b // GB)
                mm = pe.matmul(V[:, b % GB, 0:D + TYPES * (1 + T_ITER)], x_t[:, b * N:(b + 1) * N], w_x[:, b, :],
                               start=True, stop=True)
                if b % 2:
                    mm.then_inc(vx_mm, 1)

            def pc(s, g):
                pe.wait_ge(ctx_done, s + 1)
                pe.wait_ge(plpc_done, s)
                pe.matmul(PC[:, :], W("pc"), ctx_t[:, g * GT:(g + 1) * GT], start=True, stop=True).then_inc(pc_done, 1)

            def v_context(s, g, b):
                pe.wait_ge(wv_ready, s + 1)
                pe.wait_ge(qk_done, s)
                pe.wait_ge(v_evac, s)
                pe.matmul(V[:, b, 0:D + QK], ctx_t[:, g * GT + b * N:g * GT + (b + 1) * N],
                          w_v[:, g % 2, b, 0, :], start=b % 2 == 0, stop=False)

            def v_product(s, g):
                pe.wait_ge(plpc_done, s + 1)
                for b in range(GB):
                    mm = pe.matmul(V[:, b, 0:D + QK], plpc[:, g % 2, b * N:(b + 1) * N],
                                   w_v[:, g % 2, b, 1, :], start=False, stop=b % 2 == 1)
                mm.then_inc(v_done, 1)

            def sel(s):
                pe.wait_ge(parts_done, s + 1)
                if not (isinstance(s, int) and s < 2):
                    pe.wait_ge(pt_evac, s - 1)
                pe.transpose(SEL, parts[:, :, :].rearrange("p b r -> p (b r)"), ident_h[:, :]).then_inc(sel_done, 1)

            def penalties(s, g, bs):
                for b in bs:
                    pe.wait_ge(red_done, s * GB + max(b - 1, 0))
                    pe.matmul(TB[b % 2][:, :, :].rearrange(flat), ident_h[:, :],
                              penalty[:, g * GB + b, :, :].rearrange("p i m -> p (i m)"), start=True, stop=False)

            def score_products(s, bs):
                for b in bs:
                    pe.matmul(TB[b % 2][:, :, :].rearrange(flat), t_lhs[:, b, :],
                              t_rhs[:, :, :].rearrange("p i m -> p (i m)"), start=False, stop=True).then_inc(t_done, 1)

            def first_scores(s, g):
                pe.wait_ge(ops_done, s + 1)
                score_products(s, (0, 1))

            def last_scores(s, g):
                pe.wait_ge(S("lhs_done"), s + 1)
                for b in (2, 3):
                    penalties(s, g, (b,))
                    score_products(s, (b,))

            def turn(s):
                pe.wait_ge(prob_done, s + 1)
                pe.wait_ge(sel_copied, STEPS if isinstance(s, int) and s + 1 == STEPS else s + 2)
                for b in range(GB):
                    mm = pe.transpose(PT[:, b, :], prob[:, b, :], C("ident"))
                mm.then_inc(pt_done, 1)

            def message(s, g):
                pe.wait_ge(pt_evac, s + 1)
                pe.wait_ge(v_evac, s + 1)
                pe.wait_ge(msg_evac, s + 1)
                for b in range(GB):
                    mm = pe.matmul(M[:, b, :], v_s[:, g % 4, b, :], prob_t[:, b, :], start=True, stop=True)
                mm.then_inc(msg_done, 1)

            def update_context(s, g):
                pe.wait_ge(S("u_out"), s + 1)
                pe.matmul(U[:, :], W("mu", 0), ctx_t[:, g * GT:(g + 1) * GT], start=True, stop=False)

            def update_message(s, g):
                pe.wait_ge(msg_evac, s + 2)
                pe.matmul(U[:, :], W("mu", 1), msg_s[:, :], start=False, stop=True).then_inc(mu_done, 1)

            pe.wait_ge(qbias_ready, 1)
            pe.wait_ge(kbias_ready, 1)
            pc(0, 0)
            pe.wait_ge(S("wv_query"), 2)
            pe.wait_ge(vx_act, B // GB)
            pe.wait_ge(vx_dve, B // GB)
            for b in range(GB):
                v_context(0, 0, b)
            v_product(0, 0)
            pc(1, 1)
            pe.wait_ge(consts_ready, 2)
            sel(0)
            for b in range(GB):
                v_context(1, 1, b)
            v_product(1, 1)
            pe.wait_ge(pl_done, G)
            pe.wait_ge(pen_done, TYPES)
            penalties(0, 0, (0, 1))
            first_scores(0, 0)
            last_scores(0, 0)
            pe.wait_ge(sel_copied, 1)
            sel(1)
            penalties(1, 1, (0, 1))
            pc(2, 2)

            def step(t, g, front, ahead):
                s, n, m = t * G + g, (g + 1) % G, (g + 2) % G
                last_round = isinstance(t, int)
                if last_round and g == G - 1:
                    query(0, 0)
                    key(0, 0)
                if front:
                    first_scores(s + 1, n)
                turn(s)
                if front:
                    last_scores(s + 1, n)
                if ahead:
                    for b in range(GB):
                        v_context(s + 2, m, b)
                    v_product(s + 2, m)
                message(s, g)
                if not (last_round and s + 3 >= STEPS):
                    pc(s + 3, (g + 3) % G)
                if ahead:
                    sel(s + 2)
                if ahead:
                    penalties(s + 2, m, (0, 1))
                update_context(s, g)
                if last_round and g == G - 2:
                    pe.wait_ge(qk_done, STEPS)
                    pe.wait_ge(v_evac, STEPS)
                    pe.wait_ge(S("u_out"), STEPS - G + 2)
                    cond(0, 0)
                    cond_rest(0)
                if last_round and g == G - 1:
                    value(0, 0)
                update_message(s, g)

            def cond(g, par):
                pe.matmul(X0, W("cb", 0), x_t[:, bass.ds(g * GT, GT)], start=True, stop=False)

            def cond_rest(g):
                pe.matmul(X0, W("cb", 1), ctx_t[:, bass.ds(g * GT, GT)], start=False, stop=True).then_inc(S("cond_mm"), 1)

            def query(g, par):
                pe.wait_ge(S("cond_ready"), g + 1)
                pe.matmul(X1, W("wi", 0), xc_s[:, par, :], start=True, stop=True).then_inc(S("query_mm"), 1)

            def key(g, par):
                pe.wait_ge(S("cond_ready"), g + 1)
                pe.matmul(X0, W("wi", 1), xc_s[:, par, :], start=True, stop=True).then_inc(S("key_mm"), 1)

            def value(g, par):
                pe.wait_ge(S("key_ready"), g + 1)
                for b in range(GB):
                    mm = pe.matmul(X0[:, b * N:(b + 1) * N], xc_s[:, par, b * N:(b + 1) * N], W("wi", 2),
                                   start=True, stop=True)
                mm.then_inc(S("value_mm"), 1)

            def head_scores(u, g, par, j):
                b, q = divmod(j, 4)
                pe.wait_ge(S("query_ready"), g + 1)
                if b == 0:
                    pe.wait_ge(S("km_dve") if q % 2 == 0 else S("km_pool"), 8 * g + 4 * (q // 2 + 1))
                if not (isinstance(u, int) and u < 2):
                    pe.wait_ge(S("ex_ready"), 4 * (u - 1))
                pe.matmul(SB[j % 2][:, :, :].rearrange(flat), q_s[:, par, b * N:(b + 1) * N],
                          k_m[par][:, 4 * q:4 * q + 4, b * N:(b + 1) * N], start=True, stop=True)\
                    .then_inc(S("scores_mm"), 1)

            def turn_exps(u, j):
                pe.wait_ge(S("ex_ready"), 4 * (u + 1))
                if not (isinstance(u, int) and u < 2):
                    pe.wait_ge(S("ext_ready"), u - 1)
                for h in range(4):
                    mm = pe.transpose(PB[j % 2][:, h, :], ex[:, j % 2, h, :], C("ident"))
                mm.then_inc(S("ext_mm"), 1)

            def weigh(u, g, par, j):
                b, q = divmod(j, 4)
                pe.wait_ge(S("ext_ready"), u + 1)
                pe.wait_ge(S("value_ready"), g + 1)
                if not (isinstance(u, int) and u < 2):
                    pe.wait_ge(S("o_ready"), u - 1)
                for h in range(4):
                    at = VW * (4 * q + h)
                    mm = pe.matmul(OB[j % 2][:, h, 0:VWIN], ex_t[:, j % 2, h, :], v_a[:, par, b, at:at + VWIN],
                                   start=True, stop=True)
                mm.then_inc(S("o_mm"), 1)

            def turn_heads(p):
                pe.wait_ge(S("on_ready"), p + 1)
                for b in range(GB):
                    mm = pe.transpose(X0[:, b * N:(b + 1) * N], o_n[:, b, :], C("ident"))
                mm.then_inc(S("ot_mm"), 1)

            def residual(p, par, b):
                pe.wait_ge(S("ot_ready"), p + 1)
                cols = slice(b * N, (b + 1) * N)
                pe.matmul(X1[:, cols], xc_s[:, par, cols], C("ident"), start=True, stop=False)
                pe.matmul(X1[:, cols], o_t[:, cols], W("wo"), start=False, stop=True).then_inc(S("h_mm"), 1)

            def turn_norm(p):
                pe.wait_ge(S("xn_ready"), p + 1)
                for b in range(GB):
                    mm = pe.transpose(X1[:, b * N:(b + 1) * N], xn[:, b, :], C("ident"))
                mm.then_inc(S("x1t_mm"), 1)

            def gate(p):
                pe.wait_ge(S("x1t_ready"), p + 1)
                for b in range(GB):
                    mm = pe.matmul(X0[:, b * N:b * N + 12], x1_t[:, b * N:(b + 1) * N], W("gate")[:, 0:12],
                                   start=True, stop=True)
                mm.then_inc(S("gate_mm"), 1)

            def rank(p):
                pe.wait_ge(S("route_chain"), p * ROUTE + HOT_LINK)
                pe.matmul(X1[:, 0:GB * EXPERTS], before_h[:, :], oh_h[:, :, :].rearrange("p b e -> p (b e)"),
                          start=True, stop=False)
                for b in range(GB - 1):
                    later = GB - 1 - b
                    pe.matmul(X1[:, (b + 1) * EXPERTS:GB * EXPERTS].rearrange("p (b e) -> p b e", b=later),
                              ones_h[:, :], oh_h[:, b, :].unsqueeze(1).broadcast_to([128, later, EXPERTS]),
                              start=False, stop=False)
                pe.matmul(X1[:, 0:GB * EXPERTS].rearrange("p (b e) -> p b e", b=GB), ones_h[:, :],
                          cs_h[:, :].unsqueeze(1).broadcast_to([128, GB, EXPERTS]), start=False, stop=True)\
                    .then_inc(S("rank_mm"), 1)

            rounds(pe, step)
            pe.wait_ge(S("u_out"), STEPS + 1)
            pe.wait_ge(S("halves_ready"), 2)
            head_scores(0, 0, 0, 0)
            head_scores(1, 0, 0, 1)

            def body(g, par, prev, nxt):
                for j in range(UNITS):
                    u = g * UNITS + j
                    if j + 2 < UNITS:
                        head_scores(u + 2, g, par, j + 2)
                    elif nxt:
                        head_scores(u + 2, g + 1, 1 - par, j + 2 - UNITS)
                    turn_exps(u, j)
                    if j:
                        weigh(u - 1, g, par, j - 1)
                    elif prev:
                        weigh(u - 1, g - 1, 1 - par, UNITS - 1)
                    if prev and j == 1:
                        turn_heads(g - 1)
                    if prev and j in (2, 3):
                        residual(g - 1, 1 - par, 2 * (j - 2))
                        residual(g - 1, 1 - par, 2 * (j - 2) + 1)
                    if nxt and j == 4:
                        if prev:
                            pe.wait_ge(S("ot_ready"), g)
                        cond(g + 1, 1 - par)
                    if nxt and j == 5:
                        cond_rest(g + 1)
                    if nxt and j == 6:
                        key(g + 1, 1 - par)
                    if prev and j == 7:
                        turn_norm(g - 1)
                    if prev and j == 9:
                        pe.wait_ge(S("key_ready"), g + 1 + nxt)
                        gate(g - 1)
                    if nxt and j == 10:
                        if prev:
                            pe.wait_ge(S("x1t_ready"), g)
                        query(g + 1, 1 - par)
                    if nxt and j == 11:
                        if prev:
                            pe.wait_ge(S("route_chain"), (g - 1) * ROUTE + TOP_LINK)
                        value(g + 1, 1 - par)
                    if prev and j == 13:
                        pe.wait_ge(S("query_ready"), g + 1 + nxt)
                        rank(g - 1)
            groups(pe, body)
            weigh(G * UNITS - 1, G - 1, 1, UNITS - 1)
            turn_heads(G - 1)
            for b in range(GB):
                residual(G - 1, 1, b)
            turn_norm(G - 1)
            gate(G - 1)
            rank(G - 1)
            pe.wait_ge(S("route_chain"), (G - 1) * ROUTE + SUM_LINK)
            pe.matmul(X0[:, 0:EXPERTS], ones_h[:, :], cs_h[:, :], start=True, stop=True).then_inc(S("cnt_mm"), 1)

            def slot_of(k, r):
                i = r % 2
                static = isinstance(k, int)
                if not (static and (k < 4 or k - 4 >= SLOTS)):
                    e = pe.value_load(exp_i[0:1, bass.ds(k - 4, 1)], min_val=0, max_val=EXPERTS - 1)
                    if not (static and k < 6):
                        pe.wait_ge(S("res_ready"), k - 5)
                    pe.matmul(YB[i], C("ones")[0:1, :], b2_s[:, bass.ds(e * D, D)], start=True, stop=False)
                    pe.wait_ge(S("ht_ready"), k - 3)
                    for f in range(2):
                        mm = pe.matmul(YB[i], ht_s[:, i, f * N:(f + 1) * N], w2_s[:, bass.ds(e * FF + f * D, D)],
                                       start=False, stop=(f == 1))
                    mm.then_inc(S("y_mm"), 1)
                if not (static and (k < 2 or k - 2 >= SLOTS)):
                    pe.wait_ge(S("xt_ready"), k - 1)
                    pe.wait_ge(S("w1_ready"), k - 1)
                    for f in range(2):
                        mm = pe.matmul(HT[i][:, f * N:(f + 1) * N], w1_r[:, (r - 2) % 4, f * 128:(f + 1) * 128],
                                       xt_s[:, i, :], start=True, stop=True)
                    mm.then_inc(S("ht_mm"), 1)
                if not (static and k >= SLOTS):
                    pe.wait_ge(S(f"in_tile{r}"), tile_turn(k, r))
                    pe.transpose(XT[i], tile_s[:, r, 0:D], C("ident")).then_inc(S("xt_mm"), 1)
            pe.wait_ge(S("in_experts"), 48)
            pe.wait_ge(S("table_ready"), 2)
            tiles(pe, slot_of)

        @block.vector
        def _(dve):
            dve.memset(parts[:, :, :], 0.0).then_inc(consts_ready, 1)
            dve.wait_ge(in_w, 16)
            dve.wait_ge(zq_mm, 1)
            dve.tensor_scalar(elu_z[:, :], U[:, 0:B], bias("qin"), None, ALU.add).then_inc(zq_done, 1)
            dve.wait_ge(zq_done, 1)
            dve.tensor_scalar(elu_n[:, :], elu_z[:, :], 0.0, None, ALU.min).then_inc(zneg_done, 1)
            dve.wait_ge(zexp_done, 1)
            dve.scalar_tensor_tensor(elu_s[:, :], elu_z[:, :], 0.0, elu_e[:, :], ALU.max, ALU.add).then_inc(zsum_done, 1)
            dve.wait_ge(zsum_done, 1)
            dve.tensor_scalar(q_base[:, :], elu_s[:, :], -1.0, None, ALU.add).then_inc(qbase_ready, 1)
            dve.tensor_scalar(bq_w1[:, :], w[:, WCOLS["w1t"][0]:WCOLS["w1t"][1]], bias("q"), None, ALU.mult)\
                .then_inc(bqw1_ready, 1)

            def v_columns(batches):
                dve.tensor_copy(w_x[:, batches, 0:D], W("v", 0).unsqueeze(1).broadcast_to([128, B // 2, D]))\
                    .then_inc(wv_const, 1)
            dve.wait_ge(in_w2, 16)
            v_columns(slice(0, B // 2))
            dve.wait_ge(in_c, 16)
            dve.tensor_copy(ident_h[:, :], C("ident")).then_inc(consts_ready, 1)
            dve.wait_ge(ck_ready, 1)
            dve.tensor_tensor(ck_w2[:, :, :], ck[:, :].unsqueeze(2).broadcast_to([128, T_ITER * B, TYPES]),
                              w[:, WCOLS["w2t"][0]:WCOLS["w2t"][1]].unsqueeze(1).broadcast_to([128, T_ITER * B, TYPES]),
                              ALU.mult).then_inc(ckw2_ready, 1)
            dve.wait_ge(ckw2_ready, 1)
            dve.tensor_scalar(bk_w2[:, :], ck_w2[:, :, :].rearrange("p a i -> p (a i)"), bias("k"), None, ALU.mult)\
                .then_inc(bkw2_ready, 1)
            v_columns(slice(B // 2, B))
            for par in range(2):
                dve.tensor_copy(w_v[:, par, :, :, 0:D],
                                W("v", 1, 2 * D).rearrange("p (c d) -> p c d", c=2).unsqueeze(1)
                                .broadcast_to([128, GB, 2, D])).then_inc(wv_const, 1)
            dve.wait_ge(in_adj, 16)
            adjs = adj_s[:, :].rearrange("p (b m) -> p b m", b=B)
            for i in range(TYPES):
                dve.tensor_scalar(penalty[:, :, i, :], adjs, float(i + 1), -BIG, ALU.not_equal, ALU.mult)\
                    .then_inc(pen_done, 1)
                if i == 1:
                    dve.wait_ge(kbias_mm, 1)
                    dve.tensor_copy(kbias[:, :, :, :].rearrange("p t b i -> p (t b i)"),
                                    PT[:, :, :].rearrange("p a n -> p (a n)")).then_inc(kbias_ready, 1)
                    dve.wait_ge(qbias_mm, 1)
                    dve.tensor_copy(qbias[:, :], PC[:, 0:TYPES]).then_inc(qbias_ready, 1)
            dve.wait_ge(in_mask, 16)
            dve.wait_ge(pen_done, TYPES)
            dve.tensor_scalar(ctx_t[:, :], mask_b[:, :], bias("init"), None, ALU.mult).then_inc(ctx_done, G)
            for pair in range(1, B // 2, 2):
                vx_out(dve.tensor_copy, dve, vx_dve, pair)
            def pl_times_pc(s, g):
                dve.wait_ge(pc_done, s + 1)
                dve.scalar_tensor_tensor(plpc[:, g % 2, :], PC[:, :], bias("pc"), pl_t[:, g * GT:(g + 1) * GT],
                                         ALU.add, ALU.mult).then_inc(plpc_done, 1)

            dve.wait_ge(pl_done, G)
            pl_times_pc(0, 0)
            dve.wait_ge(vx_act, B // GB)
            dve.wait_ge(vx_dve, B // GB)
            dve.wait_ge(qbias_ready, 1)
            dve.wait_ge(kbias_ready, 1)
            dve.tensor_tensor(qkx[:, :, :, 0:TYPES], qkx[:, :, :, 0:TYPES],
                              qbias[:, :].unsqueeze(1).unsqueeze(1).broadcast_to([128, B, T_ITER, TYPES]), ALU.add)\
                .then_inc(S("qkx_ready"), 1)
            dve.tensor_tensor(qkx[:, :, :, TYPES:QK], qkx[:, :, :, TYPES:QK],
                              kbias[:, :, :, :].rearrange("p t b i -> p b t i"), ALU.add).then_inc(S("qkx_ready"), 1)
            dve.wait_ge(S("qkx_ready"), 2)

            def score_columns(s, t, g):
                dve.wait_ge(v_done, s + 1)
                dve.tensor_tensor(qk[:, :, :], V[:, :, D:D + QK],
                                  qkx[:, g * GB:(g + 1) * GB, bass.ds(t, 1), :].rearrange("p b t j -> p (b t) j"),
                                  ALU.add).then_inc(qk_done, 1)
                dve.wait_ge(qk_done, s + 1)
                dve.tensor_copy(parts[:, :, 0:QK], qk[:, :, :]).then_inc(hi_done, 1)

            def score_parts(s):
                dve.wait_ge(hi_done, s + 1)
                dve.tensor_tensor(res1[:, :, :], qk[:, :, :], parts[:, :, 0:QK], ALU.subtract).then_inc(res1_done, 1)
                dve.wait_ge(res1_done, s + 1)
                dve.tensor_copy(parts[:, :, QK:2 * QK], res1[:, :, :]).then_inc(mid_done, 1)
                dve.wait_ge(mid_done, s + 1)
                dve.tensor_tensor(parts[:, :, 2 * QK:3 * QK], res1[:, :, :], parts[:, :, QK:2 * QK], ALU.subtract)\
                    .then_inc(parts_done, 1)

            def v_out(s, g):
                dve.tensor_tensor(v_s[:, g % 4, :, :], V[:, :, 0:D], vx[:, g * GB:(g + 1) * GB, :], ALU.add)\
                    .then_inc(v_evac, 1)

            def score_rows(s):
                dve.wait_ge(sel_done, s + 1)
                if not (isinstance(s, int) and s == 0):
                    dve.wait_ge(S("lhs_done"), s)
                dve.tensor_copy(sel_s[:, :], SEL).then_inc(sel_copied, 1)

            def score_operands(s):
                dve.wait_ge(sel_copied, s + 1)
                if not (isinstance(s, int) and s == 0):
                    dve.wait_ge(t_done, s * GB)
                for i in range(TYPES):
                    dve.tensor_scalar(t_rhs[:, i, :], sel_s[:, :], C("kmask")[:, i:i + 1], C("qind")[:, i:i + 1],
                                      ALU.mult, ALU.add)
                for b in range(GB // 2):
                    op = dve.tensor_scalar(t_lhs[:, b, :], sel_s[:, :], C("isq")[:, b:b + 1], C("isk")[:, b:b + 1],
                                           ALU.mult, ALU.add)
                op.then_inc(ops_done, 1)

            def leaky_out(s, h):
                bs = slice(2 * h, 2 * h + 2)
                dve.wait_ge(red_done, s * GB + 2 * h + 2)
                dve.scalar_tensor_tensor(leaky[:, bs, :], logit[:, bs, :], ALPHA, logit[:, bs, :], ALU.mult, ALU.max)\
                    .then_inc(leaky_done, 1)

            def scores_max(s, h):
                for b in (2 * h, 2 * h + 1):
                    dve.wait_ge(t_done, s * GB + b + 1)
                    dve.tensor_reduce(logit[:, b, :], TB[b % 2][:, :, :].rearrange("p i m -> p m i"), AX_X, ALU.max)\
                        .then_inc(red_done, 1)

            def top(s, h):
                bs = slice(2 * h, 2 * h + 2)
                dve.wait_ge(red_done, s * GB + 2 * h + 2)
                dve.tensor_reduce(neg_top[:, bs], logit[:, bs, :], AX_X, ALU.max, negate=True).then_inc(top_done, 1)

            def top_out(s, h):
                bs = slice(2 * h, 2 * h + 2)
                dve.wait_ge(top_done, 2 * s + h + 1)
                dve.scalar_tensor_tensor(shift[:, bs], neg_top[:, bs], ALPHA, neg_top[:, bs], ALU.mult, ALU.min)\
                    .then_inc(shift_done, 1)

            def scores_out(s):
                for h in range(2):
                    scores_max(s, h)
                    top(s, h)
                    leaky_out(s, h)
                    top_out(s, h)

            def inverse(s):
                dve.wait_ge(exp_done, (s + 1) * GB)
                dve.reciprocal(inv[:, :], total[:, :]).then_inc(inv_done, 1)

            score_columns(0, 0, 0)
            score_parts(0)
            dve.wait_ge(S("vx_ready"), G)
            v_out(0, 0)
            pl_times_pc(1, 1)
            score_rows(0)
            score_operands(0)
            score_columns(1, 0, 1)
            score_parts(1)
            scores_out(0)
            v_out(1, 1)
            inverse(0)
            score_rows(1)
            score_operands(1)
            pl_times_pc(2, 2)

            def step(t, g, front, ahead):
                s = t * G + g
                tn, n = after(t, g, 2)
                if front:
                    scores_out(s + 1)
                if ahead:
                    score_columns(s + 2, tn, n)
                    score_parts(s + 2)
                    v_out(s + 2, n)
                    score_rows(s + 2)
                if front:
                    inverse(s + 1)
                if ahead:
                    score_operands(s + 2)
                if not (isinstance(t, int) and s + 3 >= STEPS):
                    pl_times_pc(s + 3, (g + 3) % G)

            def mask_heads(g, par, heads):
                dve.wait_ge(S("key_ready"), g + 1)
                for h in heads:
                    dve.tensor_scalar(k_m[par][:, h, :], k_s[:, :], C("hmask")[:, h:h + 1], None, ALU.mult)\
                        .then_inc(S("km_dve"), 1)

            def value_out(g, par):
                dve.wait_ge(S("value_mm"), g + 1)
                dve.wait_ge(S("va_ones"), 2)
                dst = v_a[:, par, :, 0:HEADS * VW].rearrange("p b (h c) -> p b h c", c=VW)
                for b in range(GB):
                    op = dve.tensor_tensor(dst[:, b, :, 0:HD],
                                           X0[:, b * N:(b + 1) * N].rearrange("p (h c) -> p h c", c=HD),
                                           R("iv").rearrange("p (h c) -> p h c", c=HD), ALU.add)
                op.then_inc(S("value_ready"), 1)

            def row_tops(u, j):
                i = j % 2
                dve.wait_ge(S("scores_mm"), u + 1)
                if not (isinstance(u, int) and u < 2):
                    dve.wait_ge(S("ex_ready"), 4 * (u - 1))
                dve.tensor_reduce(neg_head[:, i, :], SB[i][:, :, :], AX_X, ALU.max, negate=True)\
                    .then_inc(S("top_ready"), 1)

            def sums_out(u, par, j):
                b, q = divmod(j, 4)
                dve.wait_ge(S("o_mm"), u + 1)
                dve.tensor_copy(o_a[:, par, b * HEADS + 4 * q:b * HEADS + 4 * q + 4, :], OB[j % 2][:, :, 0:VW])\
                    .then_inc(S("o_ready"), 1)

            def heads_out(p, par):
                dve.wait_ge(S("o_ready"), (p + 1) * UNITS)
                dve.reciprocal(rden[:, :], o_a[:, par, :, HD]).then_inc(S("rden_ready"), 1)
                dve.wait_ge(S("rden_ready"), p + 1)
                dve.tensor_tensor(o_n[:, :, :].rearrange("p b (h c) -> p (b h) c", c=HD), o_a[:, par, :, 0:HD],
                                  rden[:, :].unsqueeze(2).broadcast_to([128, GB * HEADS, HD]), ALU.mult)\
                    .then_inc(S("on_ready"), 1)

            def residual_out(p):
                dve.wait_ge(S("h_mm"), (p + 1) * GB)
                dve.tensor_tensor(h_s[:, :, :], X1.rearrange("p (b d) -> p b d", b=GB),
                                  R("bo").unsqueeze(1).broadcast_to([128, GB, D]), ALU.add).then_inc(S("h_ready"), 1)

            def norm1_stats(p):
                dve.wait_ge(S("h_ready"), p + 1)
                for b in range(GB):
                    op = dve.bn_stats(stats[:, b, :], h_s[:, b, :])
                op.then_inc(S("stats_ready"), 1)

            def norm1_variance(p):
                dve.wait_ge(S("stats_ready"), p + 1).then_inc(S("passed"), 1)
                for b in range(GB):
                    op = dve.bn_aggr(mv[:, b, :], stats[:, b, :])
                op.then_inc(S("mv_ready"), 1)
                dve.wait_ge(S("mv_ready"), p + 1)
                dve.tensor_scalar(ve[:, :], mv[:, :, 1], EPS, None, ALU.add).then_inc(S("var_ready"), 1)

            def norm1_out(p):
                dve.wait_ge(S("rstd_ready"), p + 1)
                for b in range(GB):
                    op = dve.tensor_scalar(xn[:, b, :], h_s[:, b, :], mv[:, b, 0:1], rstd[:, b:b + 1],
                                           ALU.subtract, ALU.mult)
                op.then_inc(S("xn_ready"), 1)

            def route(p, links):
                bc = lambda ap, n: ap.unsqueeze(2).broadcast_to([128, GB, n])
                per_batch = lambda ap, n: ap.unsqueeze(1).broadcast_to([128, GB, n])
                for n in links:
                    if n > 0:
                        dve.wait_ge(S("route_chain"), p * ROUTE + n)
                    if n == 0:
                        dve.wait_ge(S("gate_mm"), p + 1)
                        op = dve.tensor_tensor(lg[:, :, :], X0.rearrange("p (b d) -> p b d", b=GB)[:, :, 0:12],
                                               per_batch(R("gate"), 12), ALU.add)
                    elif n == 1:
                        op = dve.tensor_reduce(gm[:, :], lg[:, :, 0:4], AX_X, ALU.max)
                    elif n == 2:
                        op = dve.tensor_tensor(dg[:, :, :], lg[:, :, 0:4], bc(gm[:, :], 4), ALU.subtract)
                    elif n == 3:
                        op = dve.scalar_tensor_tensor(pick[:, :, :], dg[:, :, :], 0.0, per_batch(C("pref"), 4),
                                                      ALU.is_equal, ALU.mult)
                    elif n == 4:
                        op = dve.tensor_reduce(sm[:, :], pick[:, :, :], AX_X, ALU.max)
                    elif n == 5:
                        op = dve.tensor_tensor(oh[:, :, :], pick[:, :, :], bc(sm[:, :], 4), ALU.is_equal)
                    elif n == 6:
                        op = dve.tensor_tensor(pr[:, :, :, :], lg[:, :, 4:12].rearrange("p b (g k) -> p b g k", k=2),
                                               oh[:, :, :].unsqueeze(3).broadcast_to([128, GB, 4, 2]), ALU.mult)
                    elif n == 7:
                        op = dve.tensor_scalar(m2s[:, :], sm[:, :], -2.0, None, ALU.mult)
                    elif n == 8:
                        op = dve.tensor_reduce(el[:, :, :], pr[:, :, :, :].rearrange("p b g k -> p b k g"), AX_X, ALU.add)
                    elif n == 9:
                        op = dve.tensor_tensor(de[:, :], el[:, :, 1], el[:, :, 0], ALU.subtract)
                    elif n == 10:
                        op = dve.scalar_tensor_tensor(nd[:, :], de[:, :], -1.0, de[:, :], ALU.mult, ALU.min)
                    elif n == 11:
                        op = dve.scalar_tensor_tensor(ev[:, :], de[:, :], 0.0, m2s[:, :], ALU.is_gt, ALU.add)
                    elif n == 12:
                        op = dve.tensor_tensor(oh_h[:, :, :], per_batch(C("iota"), EXPERTS), bc(ev[:, :], EXPERTS),
                                               ALU.is_equal)
                    elif n == 13:
                        op = dve.tensor_reduce(csum[:, :], oh_h[:, :, :].rearrange("p b e -> p e b"), AX_X, ALU.add)
                    elif n == 14:
                        op = dve.tensor_tensor(cs[:, :], cs[:, :], csum[:, :], ALU.add)
                    elif n == 15:
                        dve.wait_ge(S("gate_exps"), 2 * (p + 1))
                        op = dve.tensor_reduce(gs[:, :], eg[:, :, :], AX_X, ALU.add)
                    elif n == 16:
                        op = dve.scalar_tensor_tensor(den[:, :], ee[:, :], 1.0, gs[:, :], ALU.add, ALU.mult)
                    elif n == 17:
                        dve.wait_ge(S("rank_mm"), p + 1)
                        op = dve.tensor_copy(cs_h[:, :], cs[:, :])
                    elif n == 18:
                        dve.wait_ge(S("in_rows"), 16 * (p + 1))
                        op = dve.reciprocal(rows[:, :, 2 * D], den[:, :])
                    elif n == 19:
                        op = dve.tensor_tensor(rk[:, :, :], X1[:, 0:GB * EXPERTS].rearrange("p (b e) -> p b e", b=GB),
                                               per_batch(C("base"), EXPERTS), ALU.add)
                    elif n == 20:
                        op = dve.tensor_tensor(rk2[:, :, :], rk[:, :, :], oh_h[:, :, :], ALU.mult)
                    elif n == 21:
                        op = dve.tensor_reduce(slot[:, :], rk2[:, :, :], AX_X, ALU.add)
                    else:
                        op = dve.tensor_copy(slot_i[:, :], slot[:, :])
                    op.then_inc(S("route_chain"), 1)

            rounds(dve, step)
            dve.wait_ge(in_bv, 16)
            dve.tensor_copy(before_h[:, :], C("before")).then_inc(S("halves_ready"), 1)
            dve.tensor_copy(ones_h[:, :], C("ones")).then_inc(S("halves_ready"), 1)
            dve.memset(cs[:, :], 0.0).then_inc(S("cs_zero"), 1)
            dve.memset(cs_h[:, :], 0.0).then_inc(S("cs_zero"), 1)
            dve.wait_ge(S("cs_zero"), 2)
            dve.wait_ge(S("halves_ready"), 2)
            mask_heads(0, 0, (0, 1, 2, 3, 8, 9, 10, 11))
            value_out(0, 0)
            dve.wait_ge(S("u_out"), STEPS + 1)
            row_tops(0, 0)
            row_tops(1, 1)

            def body(g, par, prev, nxt):
                for j in range(UNITS):
                    u = g * UNITS + j
                    if j + 2 < UNITS or nxt:
                        row_tops(u + 2, j)
                    if j >= 2:
                        sums_out(u - 2, par, j - 2)
                    if j == 0 and prev:
                        sums_out(u - 2, 1 - par, UNITS - 2)
                        sums_out(u - 1, 1 - par, UNITS - 1)
                        heads_out(g - 1, 1 - par)
                    if prev and j == 3:
                        residual_out(g - 1)
                    if prev and j == 4:
                        norm1_stats(g - 1)
                    if prev and j == 5:
                        norm1_variance(g - 1)
                    if prev and j == 6:
                        norm1_out(g - 1)
                    if nxt and 8 <= j < 14:
                        mask_heads(g + 1, 1 - par, ((0, 1), (2, 3), (8,), (9,), (10,), (11,))[j - 8])
                    if prev and j >= 10:
                        route(g - 1, ROUTE_SLOTS[j])
                    if nxt and j == 12:
                        value_out(g + 1, 1 - par)
            ROUTE_SLOTS = {10: range(0, 5), 11: range(5, 10), 12: range(10, 13), 13: (), 14: range(13, 19),
                           15: range(19, ROUTE)}
            groups(dve, body)
            sums_out(G * UNITS - 2, 1, UNITS - 2)
            sums_out(G * UNITS - 1, 1, UNITS - 1)
            heads_out(G - 1, 1)
            residual_out(G - 1)
            norm1_stats(G - 1)
            norm1_variance(G - 1)
            norm1_out(G - 1)
            route(G - 1, range(SUM_LINK + 1))

            done = [0]

            def then(ins):
                done[0] += 1
                ins.then_inc(S("table_chain"), 1)
                dve.wait_ge(S("table_chain"), done[0])
            row8 = lambda ap, n: ap.unsqueeze(1).broadcast_to([128, n, EXPERTS])
            dve.wait_ge(S("cnt_mm"), 1)
            then(dve.tensor_copy(cnt[:, :], X0[:, 0:EXPERTS]))
            then(dve.tensor_tensor(pad_at[:, :], cnt[:, :], C("base"), ALU.add))
            dve.tensor_copy(pad_i[:, :], pad_at[:, :]).then_inc(S("pads_known"), 1)
            route(G - 1, range(SUM_LINK + 1, ROUTE))
            then(dve.tensor_tensor(full[:, :, :], C("start").unsqueeze(1).broadcast_to([128, EXPERTS, 32]),
                                   cnt[:, :].unsqueeze(2).broadcast_to([128, EXPERTS, 32]), ALU.is_lt))
            then(dve.tensor_reduce(nt[:, :], full[:, :, :], AX_X, ALU.add))
            then(dve.tensor_tensor(ntu[:, :, :], C("upto").rearrange("p (a b) -> p a b", a=EXPERTS),
                                   row8(nt[:, :], EXPERTS), ALU.mult))
            then(dve.tensor_reduce(cum[:, :], ntu[:, :, :], AX_X, ALU.add))
            then(dve.tensor_scalar(hop[:, :], nt[:, :], float(-N), float(REGION), ALU.mult, ALU.add))
            then(dve.tensor_tensor(behind[:, :, :], C("tile").unsqueeze(2).broadcast_to([128, SLOTS, EXPERTS]),
                                   row8(cum[:, :], SLOTS), ALU.is_ge))
            then(dve.tensor_reduce(t_exp[:, :], behind[:, :, :], AX_X, ALU.add))
            then(dve.tensor_tensor(hops[:, :, :], behind[:, :, :], row8(hop[:, :], SLOTS), ALU.mult))
            then(dve.tensor_reduce(t_hop[:, :], hops[:, :, :], AX_X, ALU.add))
            then(dve.scalar_tensor_tensor(t_row[:, :], C("tile"), float(N), t_hop[:, :], ALU.mult, ALU.add))
            dve.tensor_scalar(row_i[:, 0:SLOTS], t_row[:, :], float(DUMMY), None, ALU.min).then_inc(S("table_ready"), 1)
            dve.tensor_scalar(exp_i[:, 0:SLOTS], t_exp[:, :], float(EXPERTS - 1), None, ALU.min).then_inc(S("table_ready"), 1)
            dve.memset(eps_s[:, :], EPS).then_inc(S("eps_ready"), 1)
            dve.wait_ge(S("table_ready"), 2)

            def slot_of(k, r):
                static = isinstance(k, int)
                last, i, ri = k - LAST, r % 2, (r - LAST) % 4
                fresh, qi, qq = k - 4, (r - 4) % 4, (r - 4) % RING
                ends = not (static and k < LAST)
                starts = not (static and (k < 4 or fresh >= SLOTS))
                if ends:
                    dve.wait_ge(S("sd_ready"), last + 1)
                    dve.reciprocal(rs2[:, ri:ri + 1], sd2[:, ri:ri + 1]).then_inc(S("rs2_ready"), 1)
                    dve.wait_ge(S("rs2_ready"), last + 1)
                    dve.tensor_scalar(xn2[:, i, :], res[:, ri, :], mv2[:, ri, 0:1], rs2[:, ri:ri + 1],
                                      ALU.subtract, ALU.mult).then_inc(S("xn2_ready"), 1)
                if starts:
                    dve.wait_ge(S("y_mm"), fresh + 1)
                    dve.scalar_tensor_tensor(res[:, qi, :], YB[i], tile_s[:, qq, 2 * D:2 * D + 1],
                                             tile_s[:, qq, 0:D], ALU.mult, ALU.add).then_inc(S("res_ready"), 1)
                if ends:
                    dve.wait_ge(S("xn2_ready"), last + 1)
                    dve.tensor_tensor(xg2[:, i, :], xn2[:, i, :], R("ln2g"), ALU.mult).then_inc(S("xg2_ready"), 1)
                if starts:
                    dve.wait_ge(S("res_ready"), fresh + 1)
                    dve.bn_stats(st2[:, i, :], res[:, qi, :]).then_inc(S("st2_ready"), 1)
                if ends:
                    dve.wait_ge(S("xg2_ready"), last + 1)
                    dve.wait_ge(S("xb_ready"), last + 1)
                    if not (static and last < 4):
                        dve.wait_ge(S(f"sent{ri}"), 4 * (last - 4 - ri) + 16)
                    dve.tensor_tensor(fin[:, ri, :], xg2[:, i, :], xb2[:, ri, :], ALU.add).then_inc(S("fin_ready"), 1)
                if starts:
                    dve.wait_ge(S("st2_ready"), fresh + 1).then_inc(S("passed"), 1)
                    dve.bn_aggr(mv2[:, qi, :], st2[:, i, :]).then_inc(S("mv2_ready"), 1)
            tiles(dve, slot_of)

        @block.scalar
        def _(act):
            act.wait_ge(zneg_done, 1)
            act.activation(elu_e[:, :], elu_n[:, :], ACT.Exp).then_inc(zexp_done, 1)
            act.wait_ge(in_w, 16)
            act.wait_ge(cmd_mm, 1)
            for t in range(T_ITER):
                act.activation(cmd[:, t, :], M[:, t, 0:B], ACT.Identity, bias=bias(f"qt{t}")).then_inc(cmd_ready, 1)
            act.wait_ge(ck_mm, 1)
            act.activation(ck[:, :], PT[:, 0, :], ACT.Identity, bias=bias("pk")).then_inc(ck_ready, 1)
            act.wait_ge(cv_mm, 1)
            act.activation(cv[:, :, :].rearrange("p t b -> p (t b)"), U[:, 0:N], ACT.Identity, bias=bias("pv"))\
                .then_inc(cv_ready, 1)
            for c, bk in enumerate((T0, T1, M)):
                act.wait_ge(fold_mm, c + 1)
                act.activation(key_fold[:, c, :, :, :].rearrange("p t b i -> p (t b i)"),
                               bk[:, :, :].rearrange("p a n -> p (a n)"), ACT.Copy)\
                    .then_inc(fold_ready if c < 2 else msg_evac, 1)
            act.wait_ge(qfold_mm, 1)
            act.activation(query_fold[:, :, :].rearrange("p c i -> p (c i)"), U[:, 0:3 * TYPES], ACT.Copy)\
                .then_inc(S("u_out"), 1)
            for g in range(G):
                act.wait_ge(pl_mm, g + 1)
                act.activation(pl_t[:, g * GT:(g + 1) * GT], TB[g % 2][:, :, :].rearrange("p a n -> p (a n)"),
                               ACT.Identity, bias=bias("pl")).then_inc(pl_done, 1)

            for pair in range(0, B // 2, 2):
                vx_out(act.copy, act, vx_act, pair)

            def probabilities_out(s):
                act.wait_ge(pt_done, s + 1)
                act.activation(prob_t[:, :, :], PT[:, :, :], ACT.Copy).then_inc(pt_evac, 1)

            def message_out(s, t, g):
                act.wait_ge(msg_done, s + 1)
                for b in range(GB):
                    scale = cv[:, bass.ds(t, 1), g * GB + b:g * GB + b + 1].rearrange("p t b -> p (t b)")
                    op = act.activation(msg_s[:, b * N:(b + 1) * N], M[:, b, :], ACT.Copy, scale=scale)
                op.then_inc(msg_evac, 1)

            def exps(s):
                if not (isinstance(s, int) and s == 0):
                    act.wait_ge(prob_done, s)
                for b in range(GB):
                    act.wait_ge(shift_done, 2 * s + b // 2 + 1)
                    act.wait_ge(leaky_done, 2 * s + b // 2 + 1)
                    act.activation(expo[:, b, :], leaky[:, b, :], ACT.Exp, bias=shift[:, b:b + 1],
                                   accum_out=total[:, b:b + 1]).then_inc(exp_done, 1)

            def probabilities(s):
                act.wait_ge(inv_done, s + 1)
                if not (isinstance(s, int) and s == 0):
                    act.wait_ge(pt_done, s)
                for b in range(GB):
                    op = act.activation(prob[:, b, :], expo[:, b, :], ACT.Copy, scale=inv[:, b:b + 1])
                op.then_inc(prob_done, 1)

            def left_operands(s):
                act.wait_ge(sel_copied, s + 1)
                if not (isinstance(s, int) and s == 0):
                    act.wait_ge(t_done, s * GB)
                for b in range(GB // 2, GB):
                    op = act.activation(t_lhs[:, b, :], sel_s[:, :], ACT.Identity, scale=C("isq")[:, b:b + 1],
                                        bias=C("isk")[:, b:b + 1])
                op.then_inc(S("lhs_done"), 1)

            def context(s, t, g):
                if isinstance(t, int) and t == T_ITER - 1:
                    act.wait_ge(mu_done, s + 1)
                    act.activation(ctx_t[:, g * GT:(g + 1) * GT], U[:, :], ACT.Identity, bias=bias("mu"))\
                        .then_inc(S("u_out"), 1)
                else:
                    act.wait_ge(ctx_done, G + s)
                    act.wait_ge(mu_done, s + 1)
                    act.activation(ctx_raw[:, :], U[:, :], ACT.Identity, bias=bias("mu")).then_inc(S("u_out"), 1)

            act.wait_ge(cv_ready, 1)
            left_operands(0)
            exps(0)
            left_operands(1)
            probabilities(0)

            def step(t, g, front, ahead):
                s = t * G + g
                probabilities_out(s)
                if front:
                    exps(s + 1)
                message_out(s, t, g)
                if isinstance(t, int) and g == G - 2:
                    cond_out(0, 0)
                if front:
                    probabilities(s + 1)
                if ahead:
                    left_operands(s + 2)
                context(s, t, g)
                if isinstance(t, int) and g == G - 2:
                    query_out(0, 0)
                    key_out(0, 0)

            def cond_out(g, par):
                act.wait_ge(S("cond_mm"), g + 1)
                act.activation(xc_s[:, par, :], X0, ACT.Identity, bias=bias("cb")).then_inc(S("cond_ready"), 1)

            def query_out(g, par):
                act.wait_ge(S("query_mm"), g + 1)
                act.activation(q_s[:, par, :], X1, ACT.Identity, scale=float(HD) ** -0.5, bias=iq_s[:, :]).then_inc(S("query_ready"), 1)

            def key_out(g, par):
                act.wait_ge(S("key_mm"), g + 1)
                act.activation(k_s[:, :], X0, ACT.Identity, bias=bias("ik")).then_inc(S("key_ready"), 1)

            def exponentials(u, j):
                i = j % 2
                act.wait_ge(S("top_ready"), u + 1)
                if not (isinstance(u, int) and u < 2):
                    act.wait_ge(S("ext_mm"), u - 1)
                for h in range(4):
                    act.activation(ex[:, i, h, :], SB[i][:, h, :], ACT.Exp, bias=neg_head[:, i, h:h + 1])\
                        .then_inc(S("ex_ready"), 1)

            def turned_out(u, j):
                i = j % 2
                act.wait_ge(S("ext_mm"), u + 1)
                if not (isinstance(u, int) and u < 2):
                    act.wait_ge(S("o_mm"), u - 1)
                act.activation(ex_t[:, i, :, :], PB[i][:, :, :], ACT.Copy).then_inc(S("ext_ready"), 1)

            def heads_turned(p):
                act.wait_ge(S("ot_mm"), p + 1)
                act.activation(o_t[:, :], X0, ACT.Copy).then_inc(S("ot_ready"), 1)

            def norm1_turned(p):
                act.wait_ge(S("x1t_mm"), p + 1)
                act.activation(x1_t[:, :], X1, ACT.Identity, scale=bias("ln1g"), bias=bias("ln1b"))\
                    .then_inc(S("x1t_ready"), 1)

            def gate_exps(p):
                act.wait_ge(S("route_chain"), p * ROUTE + DIFF_LINK)
                act.activation(eg[:, :, :], dg[:, :, :], ACT.Exp).then_inc(S("gate_exps"), 1)
                act.activation(ee[:, :], nd[:, :], ACT.Exp).then_inc(S("gate_exps"), 1)

            act.activation(iq_s[:, :], bias("iq"), ACT.Copy, scale=float(HD) ** -0.5).then_inc(S("iq_ready"), 1)
            act.wait_ge(S("iq_ready"), 1)
            rounds(act, step)
            act.wait_ge(S("u_out"), STEPS + 1)
            exponentials(0, 0)
            exponentials(1, 1)

            def body(g, par, prev, nxt):
                for j in range(UNITS):
                    u = g * UNITS + j
                    turned_out(u, j)
                    if j + 2 < UNITS or nxt:
                        exponentials(u + 2, j)
                    if prev and j == 1:
                        heads_turned(g - 1)
                    if nxt and j == 5:
                        cond_out(g + 1, 1 - par)
                    if nxt and j == 6:
                        key_out(g + 1, 1 - par)
                    if prev and j == 8:
                        norm1_turned(g - 1)
                    if nxt and j == 10:
                        query_out(g + 1, 1 - par)
                    if prev and j == 13:
                        gate_exps(g - 1)
            groups(act, body)
            heads_turned(G - 1)
            norm1_turned(G - 1)
            gate_exps(G - 1)

            act.wait_ge(S("pad_ready"), 2)
            act.wait_ge(S("pads_known"), 1)
            for e in range(EXPERTS // 2, EXPERTS):
                at = act.value_load(pad_i[0:1, e:e + 1], min_val=e * REGION, max_val=e * REGION + TOK)
                act.dma_start(sorted_rows[bass.ds(at, N), :], pad_row[:, :]).then_inc(S("padded"), 16)

            act.wait_ge(S("eps_ready"), 1)
            act.wait_ge(S("in_experts"), 48)
            act.wait_ge(S("table_ready"), 2)

            def slot_of(k, r):
                static = isinstance(k, int)
                if not (static and (k < 1 or k - 1 >= SLOTS)):
                    q = (r - 1) % 2
                    act.wait_ge(S("xt_mm"), k)
                    if not (static and k < 3):
                        act.wait_ge(S("ht_mm"), k - 2)
                    act.activation(xt_s[:, q, :], XT[q], ACT.Copy).then_inc(S("xt_ready"), 1)
                if not (static and (k < 3 or k - 3 >= SLOTS)):
                    q = (r - 3) % 2
                    act.wait_ge(S("ht_mm"), k - 2)
                    if not (static and k < 5):
                        act.wait_ge(S("y_mm"), k - 4)
                    for f in range(2):
                        op = act.activation(ht_s[:, q, f * N:(f + 1) * N], HT[q][:, f * N:(f + 1) * N], ACT.Relu,
                                            bias=w1_r[:, (r - 3) % 4, FF + f:FF + f + 1])
                    op.then_inc(S("ht_ready"), 1)
                if not (static and k >= SLOTS):
                    e = act.value_load(exp_i[0:1, bass.ds(k, 1)], min_val=0, max_val=EXPERTS - 1)
                if not (static and (k < 5 or k - 5 >= SLOTS)):
                    ri = (r - 5) % 4
                    act.wait_ge(S("mv2_ready"), k - 4)
                    act.activation(sd2[:, ri:ri + 1], mv2[:, ri, 1:2], ACT.Sqrt, bias=eps_s[:, :]).then_inc(S("sd_ready"), 1)
                if not (static and k >= SLOTS):
                    if not (static and k < 4):
                        act.wait_ge(S("ht_ready"), k - 3).then_inc(S("passed"), 1)
                    act.activation(w1_r[:, r % 4, :], w1_s[:, bass.ds(e * W1ROW, W1ROW)], ACT.Copy)\
                        .then_inc(S("w1_ready"), 1)
            tiles(act, slot_of)


def kernel(**inputs):
    import concourse.bacc as bacc
    from concourse.bass_utils import run_bass_kernel_spmd
    a = {k: np.asarray(v) for k, v in inputs.items()}
    nc = bacc.Bacc("TRN2", target_bir_lowering=False, num_devices=1)
    arrays = layouts(a)
    aps = {n: nc.dram_tensor(n, v.shape, mybir.dt.from_np(v.dtype), kind="ExternalInput").ap()
           for n, v in arrays.items()}
    aps["out"] = nc.dram_tensor("out", (TOK, D), F32, kind="ExternalOutput").ap()
    build(nc, **aps)
    r = run_bass_kernel_spmd(nc, [arrays], core_ids=[0])
    return r.results[0]["out"].reshape(B, N, D)


def layouts(a):
    c = {k[8:]: v for k, v in a.items() if k.startswith("L0_cond_")}
    f = {k[7:]: v for k, v in a.items() if k.startswith("L0_ffn_")}
    qt, bqt, wes = a["fside_BxSxS_0"], a["mask_BxS_ff0"], a["cond_2048"]

    def chunks(m):
        return m.reshape(m.shape[0], -1, 128).transpose(2, 1, 0).reshape(128, -1)
    cols = np.zeros((128, 24), np.float32)
    for n, v in (("qin", c["b_qin"]), ("pl", c["b_pl"]), ("pc", c["b_pc"]), ("q", c["b_q"]), ("k", c["b_k"]),
                 ("mu", c["b_mu"]), ("cb", c["b_cb"]), ("pk", c["b_pk"]), ("pv", c["b_pv"]), ("qt0", bqt[0]),
                 ("qt1", bqt[1]), ("qt2", bqt[2]), ("qt3", bqt[3]), ("init", c["init_mem"][0]),
                 ("iq", f["in_proj_b"][:D]), ("ik", f["in_proj_b"][D:2 * D]), ("ln1g", f["ln1_g"]),
                 ("ln1b", f["ln1_b"])):
        cols[:, BIAS[n]] = v
    gates = np.zeros((128, D), np.float32)
    gates[:, 0:GROUPS_E] = f["w_group"]
    gates[:, GROUPS_E:GROUPS_E + EXPERTS] = f["w_expert"].transpose(1, 0, 2).reshape(D, EXPERTS)
    pieces = {"qin": c["w_qin"].T, "pk": c["w_pk"].T, "pv": c["w_pv"].T,
              "qt": qt[:T_ITER].transpose(2, 0, 1).reshape(128, -1), "wq": c["w_q"], "wk": c["w_k"],
              "fside": a["fside_BxS_0"].T, "w1t": wes[:TYPES, :D].T, "w2t": wes[:TYPES, D:].T,
              "pl": c["w_pl"].T, "pc": c["w_pc"].T, "v": chunks(c["w_v"]), "mu": chunks(c["w_mu"]),
              "cb": chunks(c["w_cb"]), "wi": f["in_proj_w"].T, "wo": f["out_proj_w"].T, "gate": gates, "bias": cols}
    rowvecs = np.concatenate([f["in_proj_b"][2 * D:], f["out_proj_b"], f["ln1_g"], f["ln1_b"], f["ln2_g"],
                              f["ln2_b"], f["b_group"], f["b_expert"].reshape(-1), c["b_v"]]).reshape(1, NR)
    return {"xT": np.ascontiguousarray(a["x"].transpose(2, 0, 1).reshape(128, TOK)),
            "adj": np.ascontiguousarray(a["itok_BxSxS_0_4"].transpose(1, 0, 2).reshape(128, TOK)),
            "mask": np.ascontiguousarray(a["mask_BxS_ff1"].reshape(1, TOK)),
            "weights": np.ascontiguousarray(np.concatenate([pieces[n] for n in WCOLS], axis=1)),
            "rowvecs": rowvecs, "consts": shape_constants(),
            "ids": (np.arange(B)[None, :] * N + np.arange(N)[:, None]).astype(np.int32),
            "x": np.ascontiguousarray(a["x"]),
            "w1": np.ascontiguousarray(np.concatenate(
                [f["w1"].transpose(1, 0, 2), f["b1"].reshape(EXPERTS, 2, 128).transpose(2, 0, 1)], axis=2)
                .reshape(128, EXPERTS * W1ROW)),
            "w2": np.ascontiguousarray(f["w2"].reshape(EXPERTS, 2, 128, D).transpose(2, 0, 1, 3).reshape(128, -1)),
            "b2": np.ascontiguousarray(f["b2"].reshape(1, EXPERTS * D))}
```
